# Optimizing a Trainium2 kernel written in Bass

```python
import numpy as np
import jax
import jax.numpy as jnp

def _softmax(x, axis=-1):
    return jax.nn.softmax(x, axis=axis)

def _gelu(x):
    return jax.nn.gelu(x, approximate=True)

def _silu(x):
    return jax.nn.silu(x)

def _sigmoid(x):
    return jax.nn.sigmoid(x)

def _layernorm(x, axis=-1, eps=1e-05):
    m = jnp.mean(x, axis=axis, keepdims=True)
    v = jnp.var(x, axis=axis, keepdims=True)
    return (x - m) / jnp.sqrt(v + eps)

def _scatter_add(tgt, idx, src, axis=0):
    return tgt.at[idx].add(src)

def _segment_sum(src, seg, n):
    return jax.ops.segment_sum(src, seg, n)
kernel_name = 'mk_perceiver_d2_seqx_r4_459745'

def setup_inputs(seed: int=0):
    np.random.seed(seed)
    _w = jnp.asarray

    def _rec_inputs():
        import jax
        import jax.numpy as jnp
        _rk = jax.random.key(seed)
        x = -0.0005207 + 1.001 * jax.random.normal(jax.random.fold_in(_rk, 1), (8, 64, 256), jnp.float32)
        _lenS = 64 - jax.random.randint(jax.random.fold_in(_rk, 7), (8,), 0, max(1, 64 // 4) + 1, jnp.int32)
        _lenS2 = 256 - jax.random.randint(jax.random.fold_in(_rk, 8), (8,), 0, max(1, 256 // 4) + 1, jnp.int32)
        _ctx_1024P = jax.random.normal(jax.random.fold_in(_rk, 12), (8, 16, 256), jnp.float32)
        _ctx_1024c = jax.random.dirichlet(jax.random.fold_in(_rk, 512), 0.3 * jnp.ones((16,), jnp.float32), (8, 256))
        _ctx_1024t = jnp.einsum('bsk,bkd->bsd', _ctx_1024c, _ctx_1024P)
        _ctx_1024t = _ctx_1024t * jax.lax.rsqrt(jnp.mean(jnp.square(_ctx_1024t)) + 1e-12) * 0.953939
        ctx_1024 = 0.00191187 + 0.999416 * (_ctx_1024t + 0.3 * jax.random.normal(jax.random.fold_in(_rk, 612), (8, 256, 256), jnp.float32))
        _validS = jnp.arange(64)[None, :] < _lenS[:, None]
        _validS2 = jnp.arange(256)[None, :] < _lenS2[:, None]
        _causal = jnp.tril(jnp.ones((64, 64), dtype=bool))
        mask_BxS_ff1 = jnp.where(jnp.ones((8, 64), dtype=bool), 1.0, 0.0).astype(jnp.float32)
        mask_BxS2_ik0 = jnp.where(jnp.broadcast_to(_validS2[:, :], (8, 256)), 0, 1).astype(jnp.int32)
        return (x, ctx_1024, mask_BxS_ff1, mask_BxS2_ik0)
    x, ctx_1024, mask_BxS_ff1, mask_BxS2_ik0 = _rec_inputs()

    def _L0_xattn_setup():
        import jax, jax.numpy as jnp
        import numpy as np
        B, F, T, D = (8, 64, 32, 256)
        NEG = -1e+30
        key = jax.random.key(seed)
        ks = jax.random.split(key, 10)
        s = 1.0 / np.sqrt(D)
        return {'features': jax.random.normal(ks[0], (B, F, D), jnp.float32), 'masks': jnp.ones((B, F), jnp.float32), 'textual_features': jax.random.normal(ks[1], (B, T, D), jnp.float32), 'q_masks': jax.random.randint(ks[2], (B, T), 0, 2, jnp.int32), 'Ws': jax.random.normal(ks[3], (D, D), jnp.float32) * s, 'W': jax.random.normal(ks[4], (D, D), jnp.float32) * s, 'w': jax.random.normal(ks[5], (D, 1), jnp.float32) * s, 'b': jax.random.normal(ks[6], (1, D), jnp.float32) * s, 'Wcw': jax.random.normal(ks[7], (1, D), jnp.float32) * s, 'bcw': jnp.zeros((1,), jnp.float32), 'Wcb': jax.random.normal(ks[8], (1, D), jnp.float32) * s, 'bcb': jnp.zeros((1,), jnp.float32)}
    _L0_xattn_all = _L0_xattn_setup()
    _L0_xattn_in = {k: v for k, v in _L0_xattn_all.items() if k in ('Ws', 'W', 'w', 'b', 'Wcw', 'bcw', 'Wcb', 'bcb')}
    del _L0_xattn_all

    def _L0_attn_setup():
        import jax, jax.numpy as jnp
        import numpy as np
        B, T, E, H, L = (8, 1024, 256, 16, 64)
        HD = E // H
        key = jax.random.key(seed)
        ks = jax.random.split(key, 5)
        s = 1.0 / np.sqrt(E).astype(np.float32)
        x = jax.random.normal(ks[0], (B, T, E), dtype=jnp.float32)
        W_qkv = jax.random.normal(ks[1], (3 * E, E), dtype=jnp.float32) * s
        b_qkv = jnp.zeros((3 * E,), dtype=jnp.float32)
        W_out = jax.random.normal(ks[2], (E, E), dtype=jnp.float32) * s
        b_out = jnp.zeros((E,), dtype=jnp.float32)
        return {'x': x, 'W_qkv': W_qkv, 'b_qkv': b_qkv, 'W_out': W_out, 'b_out': b_out}
    _L0_attn_all = _L0_attn_setup()
    _L0_attn_in = {k: v for k, v in _L0_attn_all.items() if k in ('W_qkv', 'b_qkv', 'W_out', 'b_out')}
    del _L0_attn_all

    def _L0_ffn_setup():
        import jax, jax.numpy as jnp
        import numpy as np
        B, S, H = (2, 256, 256)
        DFF = 512
        E = 8
        TOPK = 2

        def _expert_ffn(x, w1, b1, w2, b2, wg, bg, w3, b3):
            x1 = jnp.einsum('bsh,hf->bsf', x, w1) + b1
            x2 = jnp.einsum('bsh,hf->bsf', x, w2) + b2
            z = x1 * x2
            s = jax.nn.silu(jnp.einsum('bsf,fg->bsg', z, wg) + bg)
            return jnp.einsum('bsg,gh->bsh', s, w3) + b3
        key = jax.random.key(seed)
        ks = jax.random.split(key, 12)
        sc = 0.02
        return {'x': jax.random.normal(ks[0], (B, S, H), jnp.float32), 'gate_w': jax.random.normal(ks[1], (H, E), jnp.float32) * sc, 'gate_b': jnp.zeros((E,), jnp.float32), 'w1': jax.random.normal(ks[2], (E, H, DFF), jnp.float32) * sc, 'b1': jnp.zeros((E, DFF), jnp.float32), 'w2': jax.random.normal(ks[3], (E, H, DFF), jnp.float32) * sc, 'b2': jnp.zeros((E, DFF), jnp.float32), 'wg': jax.random.normal(ks[4], (E, DFF, DFF), jnp.float32) * sc, 'bg': jnp.zeros((E, DFF), jnp.float32), 'w3': jax.random.normal(ks[5], (E, DFF, H), jnp.float32) * sc, 'b3': jnp.zeros((E, H), jnp.float32)}
    _L0_ffn_all = _L0_ffn_setup()
    _L0_ffn_in = {k: v for k, v in _L0_ffn_all.items() if k in ('gate_w', 'gate_b', 'w1', 'b1', 'w2', 'b2', 'wg', 'bg', 'w3', 'b3')}
    del _L0_ffn_all

    def _L1_xattn_setup():
        import jax, jax.numpy as jnp
        import numpy as np
        DIM = 256
        MEMORY_SIZE = 64
        MEMORY_DIM = 256
        SUMMARY_LEN = 16
        STRIDE = 8
        EPS = 1.1920929e-07

        def _rmsnorm2d(x, w):
            ms = jnp.mean(jnp.square(x), axis=(-2, -1), keepdims=True)
            return x * jax.lax.rsqrt(ms + EPS) * w
        key = jax.random.key(seed)
        ks = jax.random.split(key, 11)
        s = lambda k, shape, scale: jax.random.normal(k, shape, dtype=jnp.float32) * scale
        return {'x': s(ks[0], (4, 1024, DIM), 1.0), 'h': s(ks[1], (4, MEMORY_SIZE, MEMORY_DIM), 1.0), 'ws_w': s(ks[2], (MEMORY_DIM, DIM * SUMMARY_LEN), 0.008), 'sa_wq': s(ks[3], (MEMORY_DIM, MEMORY_DIM), 0.03), 'sa_wk': s(ks[4], (MEMORY_DIM, MEMORY_DIM), 0.03), 'sa_wv': s(ks[5], (MEMORY_DIM, MEMORY_DIM), 0.03), 'qa_q': s(ks[6], (MEMORY_SIZE, MEMORY_DIM), 1.0), 'qa_wk': s(ks[7], (MEMORY_DIM, MEMORY_DIM), 0.03), 'qa_wv': s(ks[8], (MEMORY_DIM, MEMORY_DIM), 0.03), 'mn_w': s(ks[9], (MEMORY_SIZE, MEMORY_DIM), 1.0), 'hn_w': s(ks[10], (MEMORY_SIZE, MEMORY_DIM), 1.0)}
    _L1_xattn_all = _L1_xattn_setup()
    _L1_xattn_in = {k: v for k, v in _L1_xattn_all.items() if k in ('ws_w', 'sa_wq', 'sa_wk', 'sa_wv', 'qa_q', 'qa_wk', 'qa_wv', 'mn_w', 'hn_w')}
    del _L1_xattn_all

    def _L1_attn_setup():
        import math
        import jax, jax.numpy as jnp
        import numpy as np
        D_MODEL = 256
        N_HEADS = 16
        HEAD_DIM = D_MODEL // N_HEADS
        B, L = (2, 512)
        EPS = 1e-05

        def _gammas():
            return jnp.array([1.0 - 2.0 ** (-5 - math.floor(8 * i / N_HEADS)) for i in range(N_HEADS)], dtype=jnp.float32)

        def _decay_mask(seq_len):
            idx = jnp.arange(seq_len)
            diff = idx[:, None] - idx[None, :]
            g = _gammas()[:, None, None]
            pow_ = g ** jnp.maximum(diff, 0).astype(jnp.float32)
            return jnp.where(diff >= 0, pow_, 0.0)
        key = jax.random.key(seed)
        ks = jax.random.split(key, 7)
        s = 1.0 / math.sqrt(D_MODEL)
        x = jax.random.normal(ks[0], (B, L, D_MODEL), dtype=jnp.float32)
        Wq = jax.random.normal(ks[1], (N_HEADS, D_MODEL, HEAD_DIM), dtype=jnp.float32) * s
        Wk = jax.random.normal(ks[2], (N_HEADS, D_MODEL, HEAD_DIM), dtype=jnp.float32) * s
        Wv = jax.random.normal(ks[3], (N_HEADS, D_MODEL, HEAD_DIM), dtype=jnp.float32) * s
        gn_weight = jnp.ones((D_MODEL,), dtype=jnp.float32)
        gn_bias = jnp.zeros((D_MODEL,), dtype=jnp.float32)
        Wout = jax.random.normal(ks[4], (D_MODEL, D_MODEL), dtype=jnp.float32) * s
        return {'x': x, 'Wq': Wq, 'Wk': Wk, 'Wv': Wv, 'gn_weight': gn_weight, 'gn_bias': gn_bias, 'Wout': Wout}
    _L1_attn_all = _L1_attn_setup()
    _L1_attn_in = {k: v for k, v in _L1_attn_all.items() if k in ('Wq', 'Wk', 'Wv', 'gn_weight', 'gn_bias', 'Wout')}
    del _L1_attn_all

    def _L1_ffn_setup():
        import jax, jax.numpy as jnp
        import numpy as np
        TOP_K = 2
        key = jax.random.key(seed)
        ks = jax.random.split(key, 7)
        B, T, C, E = (4, 512, 256, 8)
        H = 4 * C
        s = 0.02
        return {'x': jax.random.normal(ks[0], (B, T, C), dtype=jnp.float32), 'w_gate': jax.random.normal(ks[1], (C, E), dtype=jnp.float32) * s, 'w1': jax.random.normal(ks[2], (E, C, H), dtype=jnp.float32) * s, 'b1': jnp.zeros((E, H), dtype=jnp.float32), 'w2': jax.random.normal(ks[3], (E, H, C), dtype=jnp.float32) * s, 'b2': jnp.zeros((E, C), dtype=jnp.float32)}
    _L1_ffn_all = _L1_ffn_setup()
    _L1_ffn_in = {k: v for k, v in _L1_ffn_all.items() if k in ('w_gate', 'w1', 'b1', 'w2', 'b2')}
    del _L1_ffn_all
    return {'x': x, 'ctx_1024': ctx_1024, 'mask_BxS_ff1': mask_BxS_ff1, 'mask_BxS2_ik0': mask_BxS2_ik0, 'L0_xattn_Ws': _L0_xattn_in['Ws'], 'L0_xattn_W': _L0_xattn_in['W'], 'L0_xattn_w': _L0_xattn_in['w'], 'L0_xattn_b': _L0_xattn_in['b'], 'L0_xattn_Wcw': _L0_xattn_in['Wcw'], 'L0_xattn_bcw': _L0_xattn_in['bcw'], 'L0_xattn_Wcb': _L0_xattn_in['Wcb'], 'L0_xattn_bcb': _L0_xattn_in['bcb'], 'L0_attn_W_qkv': _L0_attn_in['W_qkv'], 'L0_attn_b_qkv': _L0_attn_in['b_qkv'], 'L0_attn_W_out': _L0_attn_in['W_out'], 'L0_attn_b_out': _L0_attn_in['b_out'], 'L0_ffn_gate_w': _L0_ffn_in['gate_w'], 'L0_ffn_gate_b': _L0_ffn_in['gate_b'], 'L0_ffn_w1': _L0_ffn_in['w1'], 'L0_ffn_b1': _L0_ffn_in['b1'], 'L0_ffn_w2': _L0_ffn_in['w2'], 'L0_ffn_b2': _L0_ffn_in['b2'], 'L0_ffn_wg': _L0_ffn_in['wg'], 'L0_ffn_bg': _L0_ffn_in['bg'], 'L0_ffn_w3': _L0_ffn_in['w3'], 'L0_ffn_b3': _L0_ffn_in['b3'], 'L1_xattn_ws_w': _L1_xattn_in['ws_w'], 'L1_xattn_sa_wq': _L1_xattn_in['sa_wq'], 'L1_xattn_sa_wk': _L1_xattn_in['sa_wk'], 'L1_xattn_sa_wv': _L1_xattn_in['sa_wv'], 'L1_xattn_qa_q': _L1_xattn_in['qa_q'], 'L1_xattn_qa_wk': _L1_xattn_in['qa_wk'], 'L1_xattn_qa_wv': _L1_xattn_in['qa_wv'], 'L1_xattn_mn_w': _L1_xattn_in['mn_w'], 'L1_xattn_hn_w': _L1_xattn_in['hn_w'], 'L1_attn_Wq': _L1_attn_in['Wq'], 'L1_attn_Wk': _L1_attn_in['Wk'], 'L1_attn_Wv': _L1_attn_in['Wv'], 'L1_attn_gn_weight': _L1_attn_in['gn_weight'], 'L1_attn_gn_bias': _L1_attn_in['gn_bias'], 'L1_attn_Wout': _L1_attn_in['Wout'], 'L1_ffn_w_gate': _L1_ffn_in['w_gate'], 'L1_ffn_w1': _L1_ffn_in['w1'], 'L1_ffn_b1': _L1_ffn_in['b1'], 'L1_ffn_w2': _L1_ffn_in['w2'], 'L1_ffn_b2': _L1_ffn_in['b2']}

def reference(x, ctx_1024, mask_BxS_ff1, mask_BxS2_ik0, L0_xattn_Ws, L0_xattn_W, L0_xattn_w, L0_xattn_b, L0_xattn_Wcw, L0_xattn_bcw, L0_xattn_Wcb, L0_xattn_bcb, L0_attn_W_qkv, L0_attn_b_qkv, L0_attn_W_out, L0_attn_b_out, L0_ffn_gate_w, L0_ffn_gate_b, L0_ffn_w1, L0_ffn_b1, L0_ffn_w2, L0_ffn_b2, L0_ffn_wg, L0_ffn_bg, L0_ffn_w3, L0_ffn_b3, L1_xattn_ws_w, L1_xattn_sa_wq, L1_xattn_sa_wk, L1_xattn_sa_wv, L1_xattn_qa_q, L1_xattn_qa_wk, L1_xattn_qa_wv, L1_xattn_mn_w, L1_xattn_hn_w, L1_attn_Wq, L1_attn_Wk, L1_attn_Wv, L1_attn_gn_weight, L1_attn_gn_bias, L1_attn_Wout, L1_ffn_w_gate, L1_ffn_w1, L1_ffn_b1, L1_ffn_w2, L1_ffn_b2):
    import jax
    import jax.numpy as jnp

    def _L0_xattn_ref(features, masks, textual_features, q_masks, Ws, W, w, b, Wcw, bcw, Wcb, bcb):
        import jax, jax.numpy as jnp
        import numpy as np
        B, F, T, D = (8, 64, 32, 256)
        NEG = -1e+30
        txt_proj = jnp.einsum('btd,de->bte', textual_features, Ws)
        feat_proj = jnp.einsum('bfd,de->bfe', features, W)
        h = jnp.tanh(txt_proj[:, None, :, :] + feat_proj[:, :, None, :] + b[None, None, :, :][..., 0, :])
        rho = jnp.einsum('bftd,d->bft', h, w[:, 0])
        qm = q_masks.astype(jnp.float32)
        rho = rho + (1.0 - qm)[:, None, :] * NEG
        att = jax.nn.softmax(rho, axis=-1)
        txt_h = jnp.einsum('bft,btd->bfd', att, textual_features)
        w_s = jnp.tanh(jnp.einsum('bfd,od->bfo', txt_h, Wcw) + bcw)
        b_s = jnp.tanh(jnp.einsum('bfd,od->bfo', txt_h, Wcb) + bcb)
        return w_s * features + b_s

    def _L0_attn_ref(x, W_qkv, b_qkv, W_out, b_out):
        import jax, jax.numpy as jnp
        import numpy as np
        B, T, E, H, L = (8, 1024, 256, 16, 64)
        HD = E // H
        b, t, e = x.shape
        scaling = HD ** (-0.5)
        qkv = x @ W_qkv.T + b_qkv
        q, k, v = jnp.split(qkv, 3, axis=-1)
        q = q * scaling

        def to_blocks(a):
            return a.reshape(b, t, H, HD).transpose(0, 2, 1, 3).reshape(b, H, t // L, L, HD)
        qb, kb, vb = (to_blocks(q), to_blocks(k), to_blocks(v))
        attn = jax.nn.softmax(jnp.einsum('bhnld,bhnmd->bhnlm', qb, kb), axis=-1)
        out = jnp.einsum('bhnlm,bhnmd->bhnld', attn, vb)
        out = out.reshape(b, H, t, HD).transpose(0, 2, 1, 3).reshape(b, t, e)
        return out @ W_out.T + b_out

    def _L0_ffn_ref(x, gate_w, gate_b, w1, b1, w2, b2, wg, bg, w3, b3):
        import jax, jax.numpy as jnp
        import numpy as np
        B, S, H = (2, 256, 256)
        DFF = 512
        E = 8
        TOPK = 2

        def _expert_ffn(x, w1, b1, w2, b2, wg, bg, w3, b3):
            x1 = jnp.einsum('bsh,hf->bsf', x, w1) + b1
            x2 = jnp.einsum('bsh,hf->bsf', x, w2) + b2
            z = x1 * x2
            s = jax.nn.silu(jnp.einsum('bsf,fg->bsg', z, wg) + bg)
            return jnp.einsum('bsg,gh->bsh', s, w3) + b3
        logits = jnp.einsum('bsh,he->bse', x, gate_w) + gate_b
        topv, topi = jax.lax.top_k(logits, TOPK)
        probs = jax.nn.softmax(topv, axis=-1)
        out = jnp.zeros_like(x)
        for e in range(E):
            we = jnp.sum(probs * (topi == e), axis=-1)
            y = _expert_ffn(x, w1[e], b1[e], w2[e], b2[e], wg[e], bg[e], w3[e], b3[e])
            out = out + we[..., None] * y
        return out

    def _L1_xattn_ref(x, h, ws_w, sa_wq, sa_wk, sa_wv, qa_q, qa_wk, qa_wv, mn_w, hn_w):
        import jax, jax.numpy as jnp
        import numpy as np
        DIM = 256
        MEMORY_SIZE = 64
        MEMORY_DIM = 256
        SUMMARY_LEN = 16
        STRIDE = 8
        EPS = 1.1920929e-07

        def _rmsnorm2d(x, w):
            ms = jnp.mean(jnp.square(x), axis=(-2, -1), keepdims=True)
            return x * jax.lax.rsqrt(ms + EPS) * w
        bsz, seqlen, dim = x.shape
        conv_seqlen = seqlen + STRIDE - (seqlen - SUMMARY_LEN) % STRIDE
        nwin = (conv_seqlen - SUMMARY_LEN) // STRIDE + 1
        seq = jnp.pad(x, ((0, 0), (0, conv_seqlen - seqlen), (0, 0)))
        idx = jnp.arange(nwin)[:, None] * STRIDE + jnp.arange(SUMMARY_LEN)[None, :]
        windows = seq[:, idx, :]
        summary = windows.reshape(bsz, nwin, dim * SUMMARY_LEN)
        summary = jnp.einsum('bnf,mf->bnm', summary, ws_w)
        scale = 1.0 / jnp.sqrt(jnp.float32(MEMORY_DIM))
        xq = jnp.einsum('bnm,hm->bnh', summary, sa_wq)
        xk = jnp.einsum('bnm,hm->bnh', summary, sa_wk)
        xv = jnp.einsum('bnm,hm->bnh', summary, sa_wv)
        sa_scores = jax.nn.softmax(jnp.einsum('bnh,bkh->bnk', xq, xk) * scale, axis=-1)
        att_summary = jnp.einsum('bnk,bkh->bnh', sa_scores, xv)
        qk = jnp.einsum('bnm,hm->bnh', summary, qa_wk)
        qv = jnp.einsum('bnm,hm->bnh', summary, qa_wv)
        q_scores = jax.nn.softmax(jnp.einsum('qh,bnh->bqn', qa_q, qk) * scale, axis=-1)
        memory = jnp.einsum('bqn,bnh->bqh', q_scores, qv)
        h = h + _rmsnorm2d(memory, mn_w)
        return _rmsnorm2d(h, hn_w)

    def _L1_attn_ref(x, Wq, Wk, Wv, gn_weight, gn_bias, Wout):
        import math
        import jax, jax.numpy as jnp
        import numpy as np
        D_MODEL = 256
        N_HEADS = 16
        HEAD_DIM = D_MODEL // N_HEADS
        B, L = (2, 512)
        EPS = 1e-05

        def _gammas():
            return jnp.array([1.0 - 2.0 ** (-5 - math.floor(8 * i / N_HEADS)) for i in range(N_HEADS)], dtype=jnp.float32)

        def _decay_mask(seq_len):
            idx = jnp.arange(seq_len)
            diff = idx[:, None] - idx[None, :]
            g = _gammas()[:, None, None]
            pow_ = g ** jnp.maximum(diff, 0).astype(jnp.float32)
            return jnp.where(diff >= 0, pow_, 0.0)
        Bq, Lq, _ = x.shape
        Q = jnp.einsum('bld,hde->bhle', x, Wq)
        K = jnp.einsum('bld,hde->bhle', x, Wk)
        V = jnp.einsum('bld,hde->bhle', x, Wv)
        Dm = _decay_mask(Lq)
        scores = jnp.einsum('bhle,bhme->bhlm', Q, K) * Dm[None] / math.sqrt(HEAD_DIM)
        out = jnp.einsum('bhlm,bhme->bhle', scores, V)
        combined = out.transpose(0, 2, 1, 3).reshape(Bq, Lq, D_MODEL)
        c = combined.transpose(0, 2, 1).reshape(Bq, N_HEADS, HEAD_DIM, Lq)
        mean = jnp.mean(c, axis=(2, 3), keepdims=True)
        var = jnp.var(c, axis=(2, 3), keepdims=True)
        c = (c - mean) / jnp.sqrt(var + EPS)
        c = c.reshape(Bq, D_MODEL, Lq)
        c = c * gn_weight[None, :, None] + gn_bias[None, :, None]
        combined = c.transpose(0, 2, 1)
        return combined @ Wout

    def _L1_ffn_ref(x, w_gate, w1, b1, w2, b2):
        import jax, jax.numpy as jnp
        import numpy as np
        TOP_K = 2
        B, T, C = x.shape
        E = w1.shape[0]
        xf = x.reshape(-1, C)
        logits = xf @ w_gate
        top_vals, top_idx = jax.lax.top_k(logits, TOP_K)
        scores = jax.nn.softmax(top_vals, axis=-1)
        out = jnp.zeros_like(xf)
        for e in range(E):
            w = jnp.sum(scores * (top_idx == e), axis=-1)
            h = jax.nn.gelu(xf @ w1[e] + b1[e], approximate=False)
            y = h @ w2[e] + b2[e]
            out = out + w[:, None] * y
        return out.reshape(B, T, C)
    x = x + _L0_xattn_ref(_layernorm(x, axis=-1), mask_BxS_ff1, ctx_1024, mask_BxS2_ik0, L0_xattn_Ws, L0_xattn_W, L0_xattn_w, L0_xattn_b, L0_xattn_Wcw, L0_xattn_bcw, L0_xattn_Wcb, L0_xattn_bcb)
    x = x + _L0_attn_ref(_layernorm(x, axis=-1), L0_attn_W_qkv, L0_attn_b_qkv, L0_attn_W_out, L0_attn_b_out)
    x = x + _L0_ffn_ref(_layernorm(x, axis=-1), L0_ffn_gate_w, L0_ffn_gate_b, L0_ffn_w1, L0_ffn_b1, L0_ffn_w2, L0_ffn_b2, L0_ffn_wg, L0_ffn_bg, L0_ffn_w3, L0_ffn_b3)
    x = x + _L1_xattn_ref(ctx_1024, _layernorm(x, axis=-1), L1_xattn_ws_w, L1_xattn_sa_wq, L1_xattn_sa_wk, L1_xattn_sa_wv, L1_xattn_qa_q, L1_xattn_qa_wk, L1_xattn_qa_wv, L1_xattn_mn_w, L1_xattn_hn_w)
    x = x + _L1_attn_ref(_layernorm(x, axis=-1), L1_attn_Wq, L1_attn_Wk, L1_attn_Wv, L1_attn_gn_weight, L1_attn_gn_bias, L1_attn_Wout)
    x = x + _L1_ffn_ref(_layernorm(x, axis=-1), L1_ffn_w_gate, L1_ffn_w1, L1_ffn_b1, L1_ffn_w2, L1_ffn_b2)
    return x

_drawn_inputs = setup_inputs


def setup_inputs(seed=0):
    import zlib

    import numpy as np

    out = dict(_drawn_inputs(seed))
    spreads = {'L0_attn_b_qkv': (0.0, 0.1),
     'L0_attn_b_out': (0.0, 0.1),
     'L0_ffn_gate_b': (0.0, 0.1),
     'L0_ffn_b1': (0.0, 0.8),
     'L0_ffn_b2': (0.0, 0.8),
     'L0_ffn_bg': (0.0, 0.424),
     'L0_ffn_b3': (0.0, 0.8),
     'L1_attn_gn_weight': (1.0, 0.6),
     'L1_attn_gn_bias': (0.0, 0.586),
     'L1_ffn_b1': (0.0, 2.0),
     'L1_ffn_b2': (0.0, 0.8)}
    factors = {'L0_xattn_b': 8.0,
     'L0_ffn_w1': 5.909,
     'L0_ffn_w2': 6.433,
     'L0_ffn_wg': 5.759,
     'L0_ffn_w3': 2.87,
     'L1_xattn_qa_q': 8.0,
     'L1_xattn_qa_wk': 8.0,
     'L1_ffn_w1': 5.075}
    for name, (base, spread) in spreads.items():
        noise = np.random.default_rng([zlib.crc32(name.encode()), seed]).standard_normal(out[name].shape)
        drawn = base * np.exp(spread * noise) if base else spread * noise
        out[name] = jnp.asarray(drawn.astype(out[name].dtype))
    for name, factor in factors.items():
        out[name] = (out[name] * factor).astype(out[name].dtype)
    return out
```

```python
from contextlib import ExitStack

import numpy as np
import concourse.bass as bass
from concourse import mybir

F32 = mybir.dt.float32
I32 = mybir.dt.int32
U32 = mybir.dt.uint32
ALU = mybir.AluOpType
ACT = mybir.ActivationFunctionType
AX_X = mybir.AxisListType.X
P = 128

B, S, D, T = 8, 64, 256, 256
TOK = B * S
NQ = TOK // P
KT = D // P
H, HD = 16, D // 16
HH = H // KT
STRIDE, WIN = 8, 16
NWIN = T // STRIDE
TPAD = T + STRIDE
E = 8
F0 = 512
F1 = 1024
NT_MAX = 16
NEG = -1e30
NT_ROWS = NT_MAX + 4
LN_EPS, GN_EPS, RMS_EPS = 1e-5, 1e-5, 1.1920929e-07
HEAD = 1
SLOTS = 4

W_COLS = dict(Ws=KT * D, W=KT * D, wvec=KT, bvec=KT)
C_COLS = dict(ident=P, tri=P, ones=P, gmean=P, bmean=P, pmask=2 * P, hmask=HH, decay=KT * HH * S,
              iota=E)
V_COLS = dict(qkv=KT * 3 * D, wo=KT * D, bqk=4, wcw=D, wcb=D, bcw=1, bcb=1, bv=D, bo=D,
              gw0=KT * E, gb0=E, gw1=KT * E, qawk=KT * D, qawv=KT * D, qaq=KT * P, mnw=D, hnw=D,
              gnw=KT, gnb=KT)
R_COLS = dict(rq=KT * D, rk=KT * D, rv=KT * D, ro=KT * D)
E0_COLS = dict(w1=KT * F0, w2=KT * F0, wg=4 * F0, w3=4 * D, b1=4, b2=4, bg=4, b3=D)
E1_COLS = dict(w1=KT * F1, w2=8 * D, b1=8, b2=D)


def offsets(cols):
    at, out = 0, {}
    for name, n in cols.items():
        out[name] = (at, n)
        at += n
    return out, at


W_AT, W_N = offsets(W_COLS)
C_AT, C_N = offsets(C_COLS)
V_AT, V_N = offsets(V_COLS)
R_AT, R_N = offsets(R_COLS)
E0_AT, E0_N = offsets(E0_COLS)
E1_AT, E1_N = offsets(E1_COLS)


def perceiver(nc, x_in, ctx_rows, ctx_cols, mask_in, w_in, c_in, v_in, r_in, ws_in, e0_in, e1_in, out):
    with ExitStack() as ctx:
        def sb(name, shape, dt=F32):
            return ctx.enter_context(nc.sbuf_tensor(name, shape, dt))

        sems = {}

        def sem(name):
            if name not in sems:
                sems[name] = ctx.enter_context(nc.semaphore(name))
            return sems[name]

        bank = [ctx.enter_context(nc.psum_tensor(f"bank{i}", [P, 512], F32)) for i in range(8)]

        xg = [nc.dram_tensor(f"expert_rows{l}", [NT_ROWS * P, D], F32).ap() for l in range(2)]
        yg = [nc.dram_tensor(f"expert_out{l}", [NT_ROWS * P, D], F32).ap() for l in range(2)]

        w_sb = sb("w_sb", [P, W_N])
        c_sb = sb("c_sb", [P, C_N])
        v_sb = sb("v_sb", [P, V_N])

        def W(name, *dims):
            return _view(w_sb, W_AT[name], dims)

        def C(name, *dims):
            return _view(c_sb, C_AT[name], dims)

        def V(name, *dims):
            return _view(v_sb, V_AT[name], dims)

        def R(name, *dims):
            return _view(v_sb, R_AT[name], dims)

        x = sb("x", [P, NQ, D])
        ln = sb("ln", [P, NQ, D])
        lnT = sb("lnT", [P, KT, TOK])
        bn = sb("bn", [P, NQ, 6])
        mv = sb("mv", [P, NQ, 2])
        veps = sb("veps", [P, NQ])
        mhalf = sb("mhalf", [P, 16])
        token = sb("token", [P, 1])
        rstd = sb("rstd", [P, NQ])
        zeros = sb("zeros", [P, D])
        memn = sb("memn", [P, NQ, D])

        arena_a = sb("arena_a", [P, 4 * 2048 + B * 512])
        hbuf = arena_a[:, 0:4 * 2048].rearrange("p (s g k t) -> p s g k t", s=SLOTS, g=4, k=KT)
        txt = arena_a[:, 4 * 2048:].rearrange("p (q k b t) -> p q k b t", q=NQ, k=KT, b=2)
        tmp = arena_a[:, 2 * E0_N:2 * E0_N + NQ * D].rearrange("p (q d) -> p q d", q=NQ)
        arena_s = sb("arena_s", [P, 2 * E0_N])
        slot = [arena_s[:, 0:E0_N], arena_s[:, E0_N:2 * E0_N],
                arena_a[:, 0:E0_N], arena_a[:, E0_N:2 * E0_N]]

        arena_b = sb("arena_b", [P, 11264])
        at = [0]

        def carve(n):
            a = at[0]
            at[0] += n
            assert at[0] <= 11264, at[0]
            return arena_b[:, a:a + n]

        ctxT = carve(KT * B * TPAD).rearrange("p (k b t) -> p k b t", k=KT, b=B)
        ctxN = carve(B * 2 * D).rearrange("p (b h d) -> p b h d", b=B, h=2)
        txs = carve(KT * 2 * T).rearrange("p (k b t) -> p k b t", k=KT, b=2)
        rho = carve(NQ * T).rearrange("p (q t) -> p q t", q=NQ)
        fts = carve(KT * P).rearrange("p (k f) -> p k f", k=KT)
        attT = carve(2 * P).rearrange("p (h f) -> p h f", h=2)
        at[0] = 0
        blk = carve(HH * TOK).rearrange("p (h t) -> p h t", h=HH)
        vblk = carve(B * D).rearrange("p (b g c e) -> p b g c e", b=B, g=H // 2, c=2)
        qT = carve(KT * TOK).rearrange("p (k t) -> p k t", k=KT)
        kT = carve(KT * TOK).rearrange("p (k t) -> p k t", k=KT)
        oT = carve(KT * TOK).rearrange("p (k t) -> p k t", k=KT)
        pr = carve(2 * 512).rearrange("p (s n) -> p s n", s=2)
        prT = carve(2 * 512).rearrange("p (s n) -> p s n", s=2)
        at[0] = HH * TOK
        vz = carve(NQ * H * 32).rearrange("p (q h e) -> p q h e", q=NQ, h=H)
        assert NQ * H * 32 <= B * D

        arena_c = sb("arena_c", [P, 5120])
        ws_sb = arena_c[:, 0:8 * D].rearrange("p (k d) -> p k d", k=8)
        negm = arena_c[:, 2048:3072].rearrange("p (q t) -> p q t", q=NQ)
        mask_sb = arena_c[:, 3072:4096].bitcast(I32).rearrange("p (q t) -> p q t", q=NQ)
        featT = arena_c[:, 4096:5120].rearrange("p (k t) -> p k t", k=KT)
        wz = sb("wz", [P, KT, 63])
        nmax = sb("nmax", [P, NQ])
        rsum = sb("rsum", [P, NQ])
        rinv = sb("rinv", [P, NQ])
        dots = sb("dots", [P, NQ, 2])
        wbs = sb("wbs", [P, NQ, 2])
        junk = sb("junk", [P, D])
        hmx = sb("hmx", [P, 2, HH])
        hsum = sb("hsum", [P, 2, HH])
        hinv = sb("hinv", [P, 2, HH])
        gstat = sb("gstat", [P, KT, B])
        gvar = sb("gvar", [P, KT, B])
        grs = sb("grs", [P, KT, B])
        gsc = sb("gsc", [P, KT, B])
        ssq = sb("ssq", [P, NQ])
        mmx = sb("mmx", [P, B])
        msum = sb("msum", [P, B])
        ca = [0]

        def carve_c(*dims):
            n = int(np.prod(dims))
            a = ca[0]
            ca[0] += n
            return _view(arena_c, (a, n), dims if len(dims) > 1 else ())
        smT = carve_c(KT, B * NWIN)
        qkT = carve_c(KT, B * NWIN)
        mpr = carve_c(B, NWIN)
        ptm = carve_c(NQ, P)
        qv = carve_c(2, D)
        lg = sb("lg", [P, NQ, E])
        top = sb("top", [P, NQ, 8])
        topi = sb("topi", [P, NQ, 8], U32)
        topf = sb("topf", [P, NQ, 2])
        oh = sb("oh", [P, NQ, 2, E])
        sel = sb("sel", [P, NQ, E])
        ntf = sb("ntf", [P, 3, E])
        rowf = sb("rowf", [P, NQ, E])
        ohr = sb("ohr", [P, NQ, 2, E])
        ridf = sb("ridf", [P, NQ, 2])
        rid = sb("rid", [P, NQ * 2], U32)
        meta = sb("meta", [P, 3, E], I32)
        gd = sb("gd", [P, NQ])
        ge = sb("ge", [P, NQ])
        gden = sb("gden", [P, NQ])
        gw = sb("gw", [P, NQ, 2])
        xrow = carve_c(D)
        xT = carve_c(KT, P)
        hT = carve_c(8, P)
        zT = carve_c(4, P)
        sT = carve_c(4, P)
        yrow = carve_c(D)
        assert ca[0] <= 5120
        yk = arena_b[:, 0:NQ * 2 * D].rearrange("p (q k d) -> p q k d", q=NQ, k=2)

        blk_ctx = ctx.enter_context(nc.Block())
        block = blk_ctx

        def bc(ap, axis, n):
            a = ap.unsqueeze(axis)
            shape = list(a.shape)
            shape[axis] = n
            return a.broadcast_to(shape)

        def experts(l, slot_of, at_of):
            def view(s, name, *dims):
                a, n = at_of[name]
                return _view(slot_of[s], (a, n), dims)
            return view

        E0 = experts(0, slot, E0_AT)
        E1 = experts(1, slot, E1_AT)

        @block.sync
        def _(sp):
            sp.dma_start(x[:], x_in.rearrange("(q p) d -> p q d", p=P)).then_inc(sem("x_in"), 16)
            sp.dma_start(c_sb[:], c_in).then_inc(sem("c_in"), 16)
            sp.dma_start(w_sb[:], w_in).then_inc(sem("w_in"), 16)
            for k in range(KT):
                sp.dma_start(ctxT[:, k, :, 0:T], ctx_cols[:, k]).then_inc(sem("ctxT_in"), 16)
            sp.dma_start(ctxN, ctx_rows).then_inc(sem("ctxN_in"), 16)
            sp.dma_start(v_sb[:], v_in).then_inc(sem("v_in"), 16)
            with sp.Fori(0, NQ) as p:
                sp.wait_ge(sem("ws_used"), HEAD + p)
                sp.dma_start(ws_sb[:], ws_in[bass.ds(p, 1)].rearrange("o p k d -> (o p) k d")).then_inc(sem("ws_in"), 16)
            sp.wait_ge(sem("o_mm0"), NQ)
            sp.dma_start(v_sb[:, 0:R_N], r_in).then_inc(sem("r_in"), 16)
            for l in range(2):
                sp.wait_ge(sem(f"meta{l}"), 1)
                sp.wait_ge(sem(f"scattered{l}"), 16 * 2 * NQ)
                with sp.Fori(0, 2) as half:
                    for s in range(SLOTS):
                        e = half * SLOTS + s
                        nt = sp.value_load(meta[0:1, 0, bass.ds(e, 1)], min_val=1, max_val=4)
                        first = sp.value_load(meta[0:1, 1, bass.ds(e, 1)], min_val=0, max_val=NT_MAX)
                        with sp.Fori(0, nt) as t:
                            n = first + t
                            sp.wait_ge(sem(f"row_used{l}"), HEAD + n)
                            sp.dma_start(xrow[:], xg[l][bass.ds(n * P, P), :]).then_inc(sem(f"row_in{l}"), 16)
            sp.wait_ge(sem("x_done"), 1)
            sp.dma_start(out.rearrange("(q p) d -> p q d", p=P), x[:]).then_inc(sem("out_done"), 16)
            sp.wait_ge(sem("out_done"), 16)

        @block.gpsimd
        def _(pool):
            def rsqrt(k, dst, src, n):
                pool.wait_ge(sem("var_ready"), k + 1)
                pool.tensor_tensor(dst, src, mhalf[:, 0:n], ALU.pow).then_inc(sem("rstd_ready"), 1)

            passes = [0]

            def passed():
                passes[0] += 1
                pool.tensor_tensor(token[:], mhalf[:, 0:1], mhalf[:, 0:1], ALU.add).then_inc(sem("passed"), 1)
                pool.wait_ge(sem("passed"), passes[0])

            pool.memset(mhalf[:], -0.5).then_inc(sem("pool_const"), 1)
            pool.memset(zeros[:], 0.0).then_inc(sem("pool_const"), 1)
            pool.memset(ctxT[:, :, :, T:TPAD], 0.0).then_inc(sem("pool_const"), 1)
            pool.dma_start(mask_sb[:], mask_in).then_inc(sem("mask_in"), 16)
            pool.wait_ge(sem("pool_const"), 3)
            rsqrt(0, rstd[:], veps[:], NQ)
            for l in range(2):
                for rows in (xg[l], yg[l]):
                    pool.dma_start(rows.rearrange("(n p) d -> p n d", p=P),
                                   bc(zeros[:], 1, NT_ROWS)).then_inc(sem("rows_zero"), 16)
            for s in range(2):
                pool.dma_start(slot[s][:, 0:E0_N], e0_in[s]).then_inc(sem(f"slot{s}_in"), 16)
            pool.wait_ge(sem("slot_free"), SLOTS + NQ * 32)
            pool.wait_ge(sem("staged"), 2 * NQ)
            for s in range(2, SLOTS):
                pool.dma_start(slot[s][:, 0:E0_N], e0_in[s]).then_inc(sem(f"slot{s}_in"), 16)
            rsqrt(1, rstd[:], veps[:], NQ)
            pool.wait_ge(sem("x1_ready"), NQ)
            pool.memset(vblk[:], 0.0).then_inc(sem("vblk_zero"), 1)

            def route(l, k, n_in):
                rsqrt(k, rstd[:], veps[:], NQ)
                pool.wait_ge(sem("rows_zero"), 64)
                pool.wait_ge(sem("ln_ready"), 4 * (n_in + 1))
                pool.wait_ge(sem(f"rid{l}"), 1)
                for q in range(NQ):
                    for c in range(2):
                        pool.indirect_dma_start(
                            out=xg[l], out_offset=bass.IndirectOffsetOnAxis(ap=rid[:, 2 * q + c:2 * q + c + 1], axis=0),
                            in_=ln[:, q, :], in_offset=None).then_inc(sem(f"scattered{l}"), 16)

            def more_weights(l, e_in, n_cols, next_in, next_cols):
                for e in range(E):
                    s = e % SLOTS
                    end = pool.value_load(meta[0:1, 2, e:e + 1], min_val=1, max_val=NT_MAX)
                    if e + SLOTS < E:
                        pool.wait_ge(sem(f"y_evac{l}"), HEAD + end)
                        passed()
                        pool.dma_start(slot[s][:, 0:n_cols], e_in[e + SLOTS]).then_inc(sem(f"slot{s}_in"), 16)
                    elif next_in is not None:
                        pool.wait_ge(sem(f"y_evac{l}"), HEAD + end)
                        passed()
                        pool.dma_start(slot[s][:, 0:next_cols], next_in[s]).then_inc(sem(f"slot{s}_in"), 16)

            def gather(l):
                end = pool.value_load(meta[0:1, 2, E - 1:E], min_val=E, max_val=NT_MAX)
                pool.wait_ge(sem(f"y_stored{l}"), HEAD + end * 16)
                passed()
                for q in range(NQ):
                    for c in range(2):
                        pool.indirect_dma_start(
                            out=yk[:, q, c, :], out_offset=None, in_=yg[l],
                            in_offset=bass.IndirectOffsetOnAxis(ap=rid[:, 2 * q + c:2 * q + c + 1], axis=0)
                        ).then_inc(sem(f"gathered{l}"), 16)

            route(0, 2, 2)
            pool.wait_ge(sem(f"meta0"), 1)
            rsqrt(3, rinv[:], veps[:], NQ)
            more_weights(0, e0_in, E0_N, e1_in, E1_N)
            gather(0)
            rsqrt(4, rstd[:], veps[:], NQ)
            rsqrt(5, rinv[:], veps[:], NQ)
            rsqrt(6, rstd[:], veps[:], NQ)
            pool.wait_ge(sem("x_ready"), 4)
            pool.memset(vz[:], 0.0).then_inc(sem("vz_zero"), 1)
            rsqrt(7, grs[:].rearrange("p k b -> p (k b)"), gvar[:].rearrange("p k b -> p (k b)"), KT * B)
            route(1, 8, 5)
            pool.wait_ge(sem(f"meta1"), 1)
            more_weights(1, e1_in, E1_N, None, 0)
            gather(1)

        @block.scalar
        def _(act):
            for name in ("s_done", "h_done", "y_stored0", "y_stored1"):
                act.sem_inc(sem(name), HEAD)
            def lnT_half(k):
                act.wait_ge(sem("tr_ready"), k + 1)
                act.activation(lnT[:, 0, :], bank[0][:], ACT.Copy).then_inc(sem("lnT0_ready"), 1)

            def ffn_loop(l, tile_body):
                act.wait_ge(sem(f"meta{l}"), 1)
                with act.Fori(0, 2) as half:
                    for s in range(SLOTS):
                        e = half * SLOTS + s
                        nt = act.value_load(meta[0:1, 0, bass.ds(e, 1)], min_val=1, max_val=4)
                        first = act.value_load(meta[0:1, 1, bass.ds(e, 1)], min_val=0, max_val=NT_MAX)
                        with act.Fori(0, nt) as t:
                            tile_body(s, first + t)

            lnT_half(0)
            act.wait_ge(sem("w_in"), 16)
            for m in range(KT):
                act.wait_ge(sem("feat_mm"), m + 1)
                act.activation(featT[:, m, :], bank[2 + m][:], ACT.Identity,
                               bias=W("bvec")[:, m:m + 1]).then_inc(sem("feat_ready"), 1)
            for q in range(NQ):
                act.wait_ge(sem("txt_mm"), 2 * q + 1)
                act.activation(txt[:, q, 0].rearrange("p b t -> p (b t)"), bank[4 + 2 * (q % 2)][:], ACT.Copy)\
                   .then_inc(sem("txt0_ready"), 1)
            with act.Fori(0, NQ) as p:
                for j in range(32):
                    act.wait_ge(sem("h_filled"), HEAD + p * 32 + (j + 1))
                    hj = hbuf[:, j % SLOTS].rearrange("p g k t -> p (g k t)")
                    act.activation(hj, hj, ACT.Tanh).then_inc(sem("h_tanh"), 1)
            act.wait_ge(sem("nmax_ready"), 1)
            for q in range(NQ):
                act.activation(rho[:, q, :], rho[:, q, :], ACT.Exp, bias=nmax[:, q:q + 1],
                               accum_out=rsum[:, q:q + 1]).then_inc(sem("att_exp"), 1)
            act.wait_ge(sem("v_in"), 16)
            act.wait_ge(sem("rinv_ready"), 1)
            for q in range(NQ):
                act.wait_ge(sem("att_tr"), q + 1)
                if q:
                    act.wait_ge(sem("txth_mm"), q)
                act.activation(attT[:].rearrange("p h f -> p (h f)"), bank[4][:, 0:2 * P], ACT.Copy)\
                   .then_inc(sem("attT_ready"), 1)
            for q in range(NQ):
                act.wait_ge(sem("dots_ready"), 2 * (q + 1))
                for c, b_ in enumerate(("bcw", "bcb")):
                    act.activation(wbs[:, q, c:c + 1], dots[:, q, c:c + 1], ACT.Tanh,
                                   bias=V(b_), scale=rinv[:, q:q + 1]).then_inc(sem("wbs_ready"), 1)
            lnT_half(1)
            for k in range(KT):
                act.wait_ge(sem("k_mm0"), k + 1)
                act.activation(kT[:, k, :], bank[4 + k][:], ACT.Identity,
                               bias=V("bqk")[:, 2 + k:3 + k]).then_inc(sem("kT_ready0"), 1)
            for i in range(2 * NQ):
                act.wait_ge(sem("sc_shift"), i + 1)
                act.activation(pr[:, i % 2, :], pr[:, i % 2, :], ACT.Exp).then_inc(sem("sc_exp"), 1)
                if i >= 1:
                    _evac_prT(act, sem, prT, bank, i - 1)
            _evac_prT(act, sem, prT, bank, 2 * NQ - 1)
            for k in range(KT):
                act.wait_ge(sem("pv_tile0"), NQ * (k + 1))
                act.activation(oT[:, k, :], bank[6 + k][:], ACT.Copy).then_inc(sem("oT_ready0"), 1)
            lnT_half(2)
            act.wait_ge(sem("gd_ready0"), 1)
            act.activation(ge[:], gd[:], ACT.Exp).then_inc(sem("ge_ready0"), 1)
            for m in range(KT):
                act.wait_ge(sem("sm_mm"), 1)
                act.activation(smT[:, m, :], bank[2 + m][:, 0:D], ACT.Copy).then_inc(sem("smT_ready"), 1)
            for m in range(KT):
                act.wait_ge(sem("qk_mm"), m + 1)
                act.activation(qkT[:, m, :], bank[4 + m][:, 0:D], ACT.Copy).then_inc(sem("qkT_ready"), 1)
            for h in range(2):
                act.wait_ge(sem("qv_mm"), 2)
                act.activation(qv[:, h, :], bank[6][:, h * D:(h + 1) * D], ACT.Copy).then_inc(sem("qv_ready"), 1)
            act.wait_ge(sem("mem_shift"), 1)
            m2 = mpr[:].rearrange("p b n -> p (b n)")
            act.activation(m2, m2, ACT.Exp, scale=1.0 / 16.0).then_inc(sem("mem_exp"), 1)
            for q in range(NQ):
                act.wait_ge(sem("mem_mm"), 2 * (q // 2) + 2)
                act.activation(tmp[:, q, :], bank[2 + q // 2][:, (q % 2) * D:(q % 2 + 1) * D], ACT.Square,
                               accum_out=ssq[:, q:q + 1]).then_inc(sem("mem_sq"), 1)

            def tile0(s, n):
                act.wait_ge(sem("z_done"), HEAD + n * 4)
                for m in range(4):
                    act.wait_ge(sem("x12_mm"), n * 4 + (m + 1))
                    act.activation(hT[:, m, :], bank[1 + m % 2][:, 0:P], ACT.Identity,
                                   bias=E0(s, "b1")[:, m:m + 1]).then_inc(sem("x1_done"), 1)
                act.wait_ge(sem("y_mm0"), HEAD + n)
                for m in range(4):
                    act.wait_ge(sem("g_mm"), HEAD + n * 2 + (m // 2 + 1))
                    act.activation(sT[:, m, :], bank[5 + m // 2][:, (m % 2) * P:(m % 2 + 1) * P], ACT.Silu,
                                   bias=E0(s, "bg")[:, m:m + 1]).then_inc(sem("s_done"), 1)
                store(0, n)

            def store(l, n):
                act.wait_ge(sem(f"y_evac{l}"), HEAD + n + 1)
                act.dma_start(yg[l][bass.ds(n * P, P), :], yrow[:]).then_inc(sem(f"y_stored{l}"), 16)

            def tile1(s, n):
                act.wait_ge(sem("y_mm1"), HEAD + n)
                for m in range(8):
                    act.wait_ge(sem("h_mm"), n * 4 + (m // 2 + 1))
                    act.activation(hT[:, m, :], bank[1 + m // 2][:, (m % 2) * P:(m % 2 + 1) * P], ACT.Gelu,
                                   bias=E1(s, "b1")[:, m:m + 1]).then_inc(sem("h_done"), 1)
                store(1, n)

            for s in range(SLOTS):
                act.wait_ge(sem(f"slot{s}_in"), 16)
            ffn_loop(0, tile0)
            for q in range(NQ):
                act.wait_ge(sem("h2_ready"), q + 1)
                act.activation(tmp[:, q, :], ln[:, q, :], ACT.Square,
                               accum_out=ssq[:, q:q + 1]).then_inc(sem("h2_sq"), 1)
            lnT_half(3)
            for k in range(KT):
                act.wait_ge(sem("k_mm1"), k + 1)
                act.activation(kT[:, k, :], bank[4 + k][:], ACT.Copy).then_inc(sem("kT_ready1"), 1)
            for q in range(NQ):
                for c in range(2):
                    act.wait_ge(sem("v_mm1"), 2 * (q // 2) + 2)
                    if q == 0:
                        act.wait_ge(sem("vz_zero"), 1)
                    v_ps = bank[6 + q // 2][:, (q % 2) * D:(q % 2 + 1) * D].rearrange("p (g c e) -> p g c e", c=2, e=HD)
                    vz_v = vz[:, q].rearrange("p (g c) (d e) -> p g c d e", c=2, e=HD)
                    act.activation(vz_v[:, :, c, c, :], v_ps[:, :, c, :], ACT.Copy).then_inc(sem("vz_ready"), 1)
            lnT_half(4)
            act.wait_ge(sem("gd_ready1"), 1)
            act.activation(ge[:], gd[:], ACT.Exp).then_inc(sem("ge_ready1"), 1)
            for s in range(SLOTS):
                act.wait_ge(sem(f"slot{s}_in"), 16 * 3)
            ffn_loop(1, tile1)

        @block.tensor
        def _(pe):
            ident = C("ident")
            for name in ("ws_used", "row_used0", "row_used1", "y_mm0", "y_mm1", "g_mm"):
                pe.sem_inc(sem(name), HEAD)

            def ln_transpose(k, n):
                for q in range(NQ):
                    pe.wait_ge(sem("ln_ready"), 4 * n + q + 1)
                    for kt in range(KT):
                        ins = pe.transpose(bank[kt][:, q * P:(q + 1) * P], ln[:, q, kt * P:(kt + 1) * P], ident)
                ins.then_inc(sem("tr_ready"), 1)

            def project(dst, w, o, m=P):
                for kt in range(KT):
                    ins = pe.matmul(dst, w[:, kt, o:o + m], lnT[:, kt, :], start=(kt == 0), stop=(kt == KT - 1))
                return ins

            pe.wait_ge(sem("c_in"), 16)
            ln_transpose(0, 0)
            for half in ("lnT0_ready", "lnT1_ready"):
                pe.wait_ge(sem(half), 1)
            pe.wait_ge(sem("w_in"), 16)
            Wf, Ws = W("W", KT, D), W("Ws", KT, D)
            for m in range(KT):
                project(bank[2 + m][:], Wf, m * P).then_inc(sem("feat_mm"), 1)
            pe.wait_ge(sem("ctxT_in"), 32)
            for q in range(NQ):
                if q >= 2:
                    pe.wait_ge(sem("txt0_ready"), q - 1)
                    pe.wait_ge(sem("txt1_ready"), q - 1)
                for m in range(KT):
                    for kt in range(KT):
                        ins = pe.matmul(bank[4 + 2 * (q % 2) + m][:], Ws[:, kt, m * P:(m + 1) * P],
                                        ctxT[:, kt, 2 * q:2 * q + 2, 0:T], start=(kt == 0), stop=(kt == KT - 1))
                    ins.then_inc(sem("txt_mm"), 1)
            pe.wait_ge(sem("feat_ready"), 2)
            pe.wait_ge(sem("pool_const"), 3)
            for m in range(KT):
                pe.matmul(bank[2 + m][:, 0:D], zeros[:, 0:P], zeros[:], start=True, stop=False)
            pe.wait_ge(sem("wz_ready"), 1)
            with pe.Fori(0, NQ) as p:
                pe.wait_ge(sem("rho_evac"), HEAD + p)
                pe.wait_ge(sem("ws_in"), (p + 1) * 16)
                for j in range(32):
                    pe.wait_ge(sem("h_tanh"), p * 32 + (j + 1))
                    for k in range(KT):
                        for g in range(4):
                            ins = pe.matmul(bank[0][32 * g:32 * g + 32, 0:T], wz[:, k, 31 - j:63 - j],
                                            hbuf[:, j % SLOTS, g, k, :], start=(j == 0 and k == 0),
                                            stop=(j == 31 and k == KT - 1))
                    ins.then_inc(sem("slot_free"), 1)
                    if j < 16:
                        i, m = j // 2, j % 2
                        ins = pe.matmul(bank[2 + m][:, 0:D], ws_sb[:, i, m * P:(m + 1) * P],
                                        ctxT[:, i % 2, :, bass.ds(p * 4 + i // 2, NWIN, step=STRIDE)],
                                        start=False, stop=False)
                    if j == 15:
                        ins.then_inc(sem("ws_used"), 1)
            for m in range(KT):
                ins = pe.matmul(bank[2 + m][:, 0:D], zeros[:, 0:P], zeros[:], start=False, stop=True)
            ins.then_inc(sem("sm_mm"), 1)
            pe.wait_ge(sem("ctxN_in"), 16)
            for q in range(NQ):
                pe.wait_ge(sem("att_exp"), q + 1)
                if q:
                    pe.wait_ge(sem("attT_ready"), q)
                for h in range(2):
                    ins = pe.transpose(bank[4][:, h * P:(h + 1) * P], rho[:, q, h * P:(h + 1) * P], ident)
                ins.then_inc(sem("att_tr"), 1)
                pe.wait_ge(sem("attT_ready"), q + 1)
                if q >= 2:
                    pe.wait_ge(sem("dots_ready"), 2 * (q - 1))
                for b2 in range(2):
                    for h in range(2):
                        ins = pe.matmul(bank[5 + q % 2][64 * b2:64 * b2 + 64, 0:D], attT[:, h, 64 * b2:64 * b2 + 64],
                                        ctxN[:, 2 * q + b2, h, :], start=(h == 0), stop=(h == 1))
                ins.then_inc(sem("txth_mm"), 1)
            ln_transpose(1, 1)
            for half in ("lnT0_ready", "lnT1_ready"):
                pe.wait_ge(sem(half), 2)
            pe.wait_ge(sem("v_in"), 16)
            qkv = V("qkv", KT, 3 * D)
            for k in range(KT):
                project(bank[4 + k][:], qkv, D + k * P).then_inc(sem("k_mm0"), 1)
            for k in range(KT):
                project(bank[6 + k][:], qkv, k * P).then_inc(sem("q_mm0"), 1)
            for b in range(B):
                if b >= 4:
                    pe.wait_ge(sem("vblk_ready"), 4 * (b // 2 - 1))
                for kt in range(KT):
                    for c in range(2):
                        ins = pe.matmul(bank[b % 4 // 2][64 * c:64 * c + 64, (b % 2) * D:(b % 2 + 1) * D],
                                        lnT[:, kt, b * S:(b + 1) * S], qkv[:, kt, 2 * D:3 * D],
                                        start=(kt == 0), stop=(kt == KT - 1))
                ins.then_inc(sem("v_mm0"), 1)
            def scores0(i):
                k, q = i // NQ, i % NQ
                if q == 0:
                    pe.wait_ge(sem("qT_ready0"), 2)
                    pe.wait_ge(sem("blk_ready0"), k + 1)
                if i >= 2:
                    pe.wait_ge(sem("sc_shift"), i - 1)
                for b2 in range(2):
                    b = 2 * q + b2
                    ins = pe.matmul(bank[4 + i % 2][64 * b2:64 * b2 + 64, :], qT[:, k, b * S:(b + 1) * S],
                                    blk[:, :, b * S:(b + 1) * S], start=True, stop=True)
                ins.then_inc(sem("sc_mm0"), 1)

            def values0(i):
                k, q = i // NQ, i % NQ
                pe.wait_ge(sem("sc_norm"), i + 1)
                if i >= 1:
                    pe.wait_ge(sem("prT_ready"), i)
                if i == 0:
                    pe.wait_ge(sem("vblk_ready"), 2 * B)
                for g in range(4):
                    ins = pe.transpose(bank[0][:, g * P:(g + 1) * P], pr[:, i % 2, g * P:(g + 1) * P], ident)
                ins.then_inc(sem("pr_tr"), 1)
                pe.wait_ge(sem("prT_ready"), i + 1)
                for b2 in range(2):
                    b = 2 * q + b2
                    for g in range(4):
                        ins = pe.matmul(bank[6 + k][32 * g:32 * g + 32, b * S:(b + 1) * S],
                                        vblk[:, b, 4 * k + g].rearrange("p c e -> p (c e)"),
                                        prT[:, i % 2, g * P + b2 * S:g * P + (b2 + 1) * S], start=True, stop=True)
                ins.then_inc(sem("pv_tile0"), 1)

            scores0(0)
            for i in range(1, 2 * NQ):
                scores0(i)
                values0(i - 1)
            values0(2 * NQ - 1)

            def out_proj(l, w):
                pe.wait_ge(sem(f"oT_ready{l}"), 2)
                for q in range(NQ):
                    for k in range(KT):
                        ins = pe.matmul(bank[2 * l + 4 - 4 * l + q // 2][:, (q % 2) * D:(q % 2 + 1) * D],
                                        oT[:, k, q * P:(q + 1) * P], w[:, k, :], start=(k == 0), stop=(k == KT - 1))
                    ins.then_inc(sem(f"o_mm{l}"), 1)
            out_proj(0, V("wo", KT, D))

            def route(l, k, n):
                ln_transpose(k, n)
                for half in ("lnT0_ready", "lnT1_ready"):
                    pe.wait_ge(sem(half), k + 1)
                g = V(f"gw{l}", KT, E)
                for q in range(NQ):
                    for kt in range(KT):
                        ins = pe.matmul(bank[7][:, q * E:(q + 1) * E], lnT[:, kt, q * P:(q + 1) * P], g[:, kt, :],
                                        start=(kt == 0), stop=(kt == KT - 1))
                ins.then_inc(sem(f"lg_mm{l}"), 1)
                pe.wait_ge(sem(f"sel{l}"), 1)
                ones, tri = C("ones"), C("tri")
                for q in range(NQ):
                    for i in range(q + 1):
                        pe.matmul(bank[7][:, 64 + q * E:64 + (q + 1) * E], ones if i < q else tri, sel[:, i, :],
                                  start=(i == 0), stop=(i == q))
                for i in range(NQ):
                    ins = pe.matmul(bank[7][:, 128:128 + E], ones, sel[:, i, :], start=(i == 0), stop=(i == NQ - 1))
                ins.then_inc(sem(f"pos_mm{l}"), 1)
            route(0, 2, 2)
            qawk, qawv, qaq = V("qawk", KT, D), V("qawv", KT, D), V("qaq", KT, P)
            pe.wait_ge(sem("smT_ready"), 2)
            for m in range(KT):
                for kt in range(KT):
                    ins = pe.matmul(bank[4 + m][:, 0:D], qawk[:, kt, m * P:(m + 1) * P], smT[:, kt, :],
                                    start=(kt == 0), stop=(kt == KT - 1))
                ins.then_inc(sem("qk_mm"), 1)
            for h in range(2):
                for kt in range(KT):
                    ins = pe.matmul(bank[6][:, h * D:(h + 1) * D], smT[:, kt, h * P:(h + 1) * P], qawv[:, kt, :],
                                    start=(kt == 0), stop=(kt == KT - 1))
                ins.then_inc(sem("qv_mm"), 1)
            pe.wait_ge(sem("qkT_ready"), 2)
            for kt in range(KT):
                ins = pe.matmul(bank[4][:, 0:D], qaq[:, kt, :], qkT[:, kt, :],
                                start=(kt == 0), stop=(kt == KT - 1))
            ins.then_inc(sem("ms_mm"), 1)
            pe.wait_ge(sem("mem_norm"), 1)
            for h in range(2):
                ins = pe.transpose(bank[5][:, h * P:(h + 1) * P],
                                   mpr[:, 4 * h:4 * h + 4, :].rearrange("p b n -> p (b n)"), ident)
            ins.then_inc(sem("mp_tr"), 1)
            pe.wait_ge(sem("ptm_ready"), 1)
            pe.wait_ge(sem("qv_ready"), 2)
            for q in range(NQ):
                pe.matmul(bank[2 + q // 2][:, (q % 2) * D:(q % 2 + 1) * D], ptm[:, q, :], qv[:, q // 2, :],
                          start=True, stop=True).then_inc(sem("mem_mm"), 1)
            pe.wait_ge(sem("mem_sq"), NQ)
            pe.matmul(bank[7][:, 192:192 + NQ], C("bmean"), ssq[:], start=True, stop=True).then_inc(sem("mss_mm"), 1)

            def ffn_loop(l, tile_body):
                pe.wait_ge(sem(f"meta{l}"), 1)
                with pe.Fori(0, 2) as half:
                    for s in range(SLOTS):
                        e = half * SLOTS + s
                        nt = pe.value_load(meta[0:1, 0, bass.ds(e, 1)], min_val=1, max_val=4)
                        first = pe.value_load(meta[0:1, 1, bass.ds(e, 1)], min_val=0, max_val=NT_MAX)
                        with pe.Fori(0, nt) as t:
                            n = first + t
                            pe.wait_ge(sem(f"slot{s}_in"), half * 16 + 16 * (1 + 2 * l))
                            pe.wait_ge(sem(f"row_in{l}"), n * 16 + 16)
                            pe.wait_ge(sem(f"xT_done{l}"), HEAD + n)
                            for kt in range(KT):
                                ins = pe.transpose(bank[0][:, kt * P:(kt + 1) * P], xrow[:, kt * P:(kt + 1) * P], ident)
                            ins.then_inc(sem(f"row_used{l}"), 1)
                            tile_body(s, n)

            def down(l, s, n, act_sb, w, K, done):
                pe.wait_ge(sem(f"y_evac{l}"), HEAD + n)
                for k in range(K):
                    pe.wait_ge(sem(done), HEAD + n * K + (k + 1))
                    ins = pe.matmul(bank[7][:, 0:D], act_sb[:, k, :], w[:, k, :], start=(k == 0), stop=(k == K - 1))
                ins.then_inc(sem(f"y_mm{l}"), 1)

            def tile0(s, n):
                w1, w2, wg = E0(s, "w1", KT, F0), E0(s, "w2", KT, F0), E0(s, "wg", 4, F0)
                pe.wait_ge(sem("xT_done0"), HEAD + n + 1)
                for m in range(4):
                    if m < 2:
                        pe.wait_ge(sem("z_done"), HEAD + n * 4)
                    else:
                        pe.wait_ge(sem("z_done"), HEAD + n * 4 + (m - 1))
                    for i, w in enumerate((w1, w2)):
                        for kt in range(KT):
                            ins = pe.matmul(bank[1 + 2 * i + m % 2][:, 0:P], w[:, kt, m * P:(m + 1) * P], xT[:, kt, :],
                                            start=(kt == 0), stop=(kt == KT - 1))
                    ins.then_inc(sem("x12_mm"), 1)
                pe.wait_ge(sem("s_done"), HEAD + n * 4)
                for k in range(4):
                    pe.wait_ge(sem("z_done"), HEAD + n * 4 + (k + 1))
                    for m in range(4):
                        ins = pe.matmul(bank[5 + m // 2][:, (m % 2) * P:(m % 2 + 1) * P],
                                        wg[:, k, m * P:(m + 1) * P], zT[:, k, :], start=(k == 0 and m % 2 == 0),
                                        stop=(k == 3), skip_group_check=True)
                        if k == 3 and m % 2 == 1:
                            ins.then_inc(sem("g_mm"), 1)
                down(0, s, n, sT, E0(s, "w3", 4, D), 4, "s_done")

            def tile1(s, n):
                w1 = E1(s, "w1", KT, F1)
                pe.wait_ge(sem("h_done"), HEAD + n * 8)
                pe.wait_ge(sem("xT_done1"), HEAD + n + 1)
                for m in range(8):
                    for kt in range(KT):
                        ins = pe.matmul(bank[1 + m // 2][:, (m % 2) * P:(m % 2 + 1) * P], w1[:, kt, m * P:(m + 1) * P],
                                        xT[:, kt, :], start=(kt == 0), stop=(kt == KT - 1))
                    if m % 2 == 1:
                        ins.then_inc(sem("h_mm"), 1)
                down(1, s, n, hT, E1(s, "w2", 8, D), 8, "h_done")

            ffn_loop(0, tile0)
            pe.wait_ge(sem("h2_sq"), NQ)
            pe.matmul(bank[7][:, 192:192 + NQ], C("bmean"), ssq[:], start=True, stop=True).then_inc(sem("hss_mm"), 1)
            ln_transpose(3, 4)
            for half in ("lnT0_ready", "lnT1_ready"):
                pe.wait_ge(sem(half), 4)
            pe.wait_ge(sem("r_in"), 16)
            for k in range(KT):
                project(bank[4 + k][:], R("rk", KT, D), k * P).then_inc(sem("k_mm1"), 1)
            for k in range(KT):
                project(bank[2 + k][:], R("rq", KT, D), k * P).then_inc(sem("q_mm1"), 1)
            for q in range(NQ):
                for kt in range(KT):
                    ins = pe.matmul(bank[6 + q // 2][:, (q % 2) * D:(q % 2 + 1) * D], lnT[:, kt, q * P:(q + 1) * P],
                                    R("rv", KT, D)[:, kt, :], start=(kt == 0), stop=(kt == KT - 1))
                ins.then_inc(sem("v_mm1"), 1)

            def scores1(i):
                k, q = i // NQ, i % NQ
                if q == 0:
                    pe.wait_ge(sem("kT_ready1"), 2)
                    pe.wait_ge(sem("blk_ready1"), k + 1)
                if i >= 2:
                    pe.wait_ge(sem("sc_decay"), i - 1)
                for b2 in range(2):
                    b = 2 * q + b2
                    ins = pe.matmul(bank[4 + i % 2][64 * b2:64 * b2 + 64, :], kT[:, k, b * S:(b + 1) * S],
                                    blk[:, :, b * S:(b + 1) * S], start=True, stop=True)
                ins.then_inc(sem("sc_mm1"), 1)

            def values1(i):
                k, q = i // NQ, i % NQ
                pe.wait_ge(sem("sc_decay"), i + 1)
                if i == 0:
                    pe.wait_ge(sem("vz_ready"), 2 * NQ)
                if q == 0 and k == 1:
                    pe.wait_ge(sem("o_evac1"), 2)
                for g in range(4):
                    for b2 in range(2):
                        for c in range(2):
                            h = 2 * g + c
                            ins = pe.matmul(bank[6 + b2][32 * g:32 * g + 32, q * S:(q + 1) * S],
                                            vz[64 * b2:64 * b2 + 64, q, HH * k + h, :],
                                            pr[64 * b2:64 * b2 + 64, i % 2, h * S:(h + 1) * S],
                                            start=(c == 0), stop=(c == 1))
                ins.then_inc(sem("pv_tile1"), 1)
            scores1(0)
            for i in range(1, 2 * NQ):
                scores1(i)
                values1(i - 1)
            values1(2 * NQ - 1)
            gm = C("gmean")
            pe.wait_ge(sem("gsum_ready"), 1)
            pe.matmul(bank[7][:, 256:272], gm, gstat[:].rearrange("p k b -> p (k b)"), start=True, stop=True)\
              .then_inc(sem("gm_mm"), 1)
            pe.wait_ge(sem("gsum_ready"), 2)
            pe.matmul(bank[7][:, 288:304], gm, gstat[:].rearrange("p k b -> p (k b)"), start=True, stop=True)\
              .then_inc(sem("gm_mm"), 1)
            out_proj(1, R("ro", KT, D))
            route(1, 4, 5)
            ffn_loop(1, tile1)

        @block.vector
        def _(dve):
            chained = [0]

            def link(ins):
                chained[0] += 1
                ins.then_inc(sem("dve_chain"), 1)
                dve.wait_ge(sem("dve_chain"), chained[0])

            def layer_norm(k, n):
                for q in range(NQ):
                    ins = dve.bn_stats(bn[:, q, :], x[:, q, :])
                link(ins)
                for q in range(NQ):
                    ins = dve.bn_aggr(mv[:, q, :], bn[:, q, :])
                link(ins)
                dve.tensor_scalar(veps[:], mv[:, :, 1], LN_EPS, None, ALU.add).then_inc(sem("var_ready"), 1)
                dve.wait_ge(sem("rstd_ready"), k + 1)
                for q in range(NQ):
                    dve.tensor_scalar(ln[:, q, :], x[:, q, :], mv[:, q, 0:1], rstd[:, q:q + 1], ALU.subtract,
                                      ALU.mult).then_inc(sem("ln_ready"), 1)

            def lnT_half(k):
                dve.wait_ge(sem("tr_ready"), k + 1)
                dve.tensor_copy(lnT[:, 1, :], bank[1][:]).then_inc(sem("lnT1_ready"), 1)

            for name in ("rho_evac", "h_filled", "z_done", "xT_done0", "xT_done1", "y_evac0", "y_evac1"):
                dve.sem_inc(sem(name), HEAD)
            link(dve.memset(wz[:], 0.0))
            dve.wait_ge(sem("x_in"), 16)
            layer_norm(0, 0)
            dve.wait_ge(sem("w_in"), 16)
            dve.tensor_copy(wz[:, :, 31], W("wvec")).then_inc(sem("wz_ready"), 1)
            lnT_half(0)
            dve.wait_ge(sem("mask_in"), 16)
            dve.tensor_scalar(negm[:], mask_sb[:], -NEG, NEG, ALU.mult, ALU.add).then_inc(sem("negm_ready"), 1)
            for q in range(NQ):
                dve.wait_ge(sem("txt_mm"), 2 * q + 2)
                dve.tensor_copy(txt[:, q, 1].rearrange("p b t -> p (b t)"), bank[5 + 2 * (q % 2)][:])\
                   .then_inc(sem("txt1_ready"), 1)
            dve.memset(hmx[:], 0.0).then_inc(sem("slot_free"), SLOTS)
            dve.wait_ge(sem("txt0_ready"), NQ)
            dve.wait_ge(sem("txt1_ready"), NQ)
            dve.wait_ge(sem("feat_ready"), 2)
            dve.wait_ge(sem("negm_ready"), 1)
            with dve.Fori(0, NQ) as p:
                dve.wait_ge(sem("h_filled"), HEAD + p * 32)
                dve.tensor_copy(txs[:].rearrange("p k b t -> p (k b t)"),
                                txt[:, bass.ds(p, 1)].rearrange("p o k b t -> p (o k b t)")).then_inc(sem("staged"), 1)
                dve.tensor_copy(fts[:], featT[:, :, bass.ds(p * P, P)]).then_inc(sem("staged"), 1)
                dve.wait_ge(sem("staged"), p * 2 + 2)
                for j in range(32):
                    dve.wait_ge(sem("slot_free"), p * 32 + (j + 1))
                    for g in range(4):
                        for k in range(KT):
                            ins = dve.tensor_scalar(hbuf[:, j % SLOTS, g, k, :], txs[:, k, g // 2, :],
                                                    fts[:, k, 32 * g + j:32 * g + j + 1], None, ALU.add)
                    ins.then_inc(sem("h_filled"), 1)
                dve.wait_ge(sem("slot_free"), p * 32 + (32 + SLOTS))
                dve.tensor_tensor(rho[:, bass.ds(p, 1), :].rearrange("p o t -> p (o t)"), bank[0][:, 0:T],
                                  negm[:, bass.ds(p, 1), :].rearrange("p o t -> p (o t)"), ALU.add)\
                   .then_inc(sem("rho_evac"), 1)
            dve.wait_ge(sem("rho_evac"), HEAD + NQ)
            dve.tensor_reduce(nmax[:], rho, AX_X, ALU.max, negate=True).then_inc(sem("nmax_ready"), 1)
            dve.wait_ge(sem("att_exp"), NQ)
            dve.reciprocal(rinv[:], rsum[:]).then_inc(sem("rinv_ready"), 1)
            dve.wait_ge(sem("v_in"), 16)
            for q in range(NQ):
                dve.wait_ge(sem("txth_mm"), q + 1)
                for c, w in enumerate(("wcw", "wcb")):
                    dve.tensor_tensor_reduce(out=junk[:] if c else tmp[:, q, :], in0=bank[5 + q % 2][:, 0:D], in1=V(w),
                                             scale=1.0, scalar=0.0, op0=ALU.mult, op1=ALU.add,
                                             accum_out=dots[:, q, c:c + 1]).then_inc(sem("dots_ready"), 1)
                dve.wait_ge(sem("dots_ready"), 2 * (q + 1))
            for q in range(NQ):
                dve.wait_ge(sem("wbs_ready"), 2 * (q + 1))
                link(dve.scalar_tensor_tensor(out=x[:, q, :], in0=ln[:, q, :], scalar=wbs[:, q, 0:1], in1=x[:, q, :],
                                              op0=ALU.mult, op1=ALU.add))
                dve.tensor_scalar(x[:, q, :], x[:, q, :], wbs[:, q, 1:2], None, ALU.add).then_inc(sem("x1_ready"), 1)
            dve.wait_ge(sem("x1_ready"), NQ)
            layer_norm(1, 1)
            lnT_half(1)

            def masked(l, srcT):
                def one(k):
                    if k:
                        dve.wait_ge(sem(f"sc_mm{l}"), NQ)
                    for h in range(HH):
                        ins = dve.tensor_scalar(blk[:, h, :], srcT[:, k, :], C("hmask")[:, h:h + 1], None, ALU.mult)
                    ins.then_inc(sem(f"blk_ready{l}"), 1)
                return one

            dve.wait_ge(sem("kT_ready0"), 2)
            mask0 = masked(0, kT)
            mask0(0)
            for k in range(KT):
                dve.wait_ge(sem("q_mm0"), k + 1)
                dve.tensor_scalar(qT[:, k, :], bank[6 + k][:], V("bqk")[:, k:k + 1], float(HD) ** -0.5, ALU.add,
                                  ALU.mult).then_inc(sem("qT_ready0"), 1)
            dve.wait_ge(sem("vblk_zero"), 1)
            bv = V("bv").rearrange("p (g c e) -> p g c e", g=HH, c=2)
            for b in range(B):
                dve.wait_ge(sem("v_mm0"), 2 * (b // 2) + 2)
                v_ps = bank[b % 4 // 2][:, (b % 2) * D:(b % 2 + 1) * D].rearrange("p (g c e) -> p g c e", g=HH, c=2)
                for c in range(2):
                    r = slice(64 * c, 64 * c + 64)
                    dve.tensor_tensor(vblk[r, b, :, c, :], v_ps[r, :, c, :], bv[r, :, c, :], ALU.add)\
                       .then_inc(sem("vblk_ready"), 1)

            def shift0(i):
                dve.wait_ge(sem("sc_mm0"), i + 1)
                sc = bank[4 + i % 2][:].rearrange("p (h m) -> p h m", h=HH)
                link(dve.tensor_reduce(hmx[:, i % 2, :], sc, AX_X, ALU.max))
                if i >= 2:
                    dve.wait_ge(sem("pr_tr"), i - 1)
                dve.tensor_tensor(pr[:, i % 2, :].rearrange("p (h m) -> p h m", h=HH), sc,
                                  bc(hmx[:, i % 2, :], 2, S), ALU.subtract).then_inc(sem("sc_shift"), 1)

            def norm0(i):
                dve.wait_ge(sem("sc_exp"), i + 1)
                v = pr[:, i % 2, :].rearrange("p (h m) -> p h m", h=HH)
                link(dve.tensor_reduce(hsum[:, i % 2, :], v, AX_X, ALU.add))
                link(dve.reciprocal(hinv[:, i % 2, :], hsum[:, i % 2, :]))
                dve.tensor_tensor(v, v, bc(hinv[:, i % 2, :], 2, S), ALU.mult).then_inc(sem("sc_norm"), 1)

            shift0(0)
            for i in range(1, 2 * NQ):
                if i == NQ:
                    mask0(1)
                shift0(i)
                norm0(i - 1)
            norm0(2 * NQ - 1)

            def add_out(l, bias, n):
                if bias is not None:
                    for q in range(NQ):
                        ins = dve.tensor_tensor(x[:, q, :], x[:, q, :], bias, ALU.add)
                    link(ins)
                for q in range(NQ):
                    dve.wait_ge(sem(f"o_mm{l}"), 2 * (q // 2) + 2)
                    ins = dve.tensor_tensor(x[:, q, :], bank[4 - 2 * l + q // 2][:, (q % 2) * D:(q % 2 + 1) * D],
                                            x[:, q, :], ALU.add)
                link(ins)
            add_out(0, V("bo"), 0)

            def route(l, k, n, kt_):
                layer_norm(k, n)
                lnT_half(kt_)
                dve.wait_ge(sem(f"lg_mm{l}"), 1)
                lg_ps = bank[7][:, 0:NQ * E].rearrange("p (q e) -> p q e", q=NQ)
                if l == 0:
                    link(dve.tensor_tensor(lg[:], lg_ps, bc(V("gb0"), 1, NQ), ALU.add))
                else:
                    link(dve.tensor_copy(lg[:], lg_ps))
                for q in range(NQ):
                    ins = dve.max(top[:, q, :], lg[:, q, :])
                link(ins)
                for q in range(NQ):
                    ins = dve.max_index(topi[:, q, :], top[:, q, :], lg[:, q, :])
                link(ins)
                dve.tensor_tensor(gd[:], top[:, :, 1], top[:, :, 0], ALU.subtract).then_inc(sem(f"gd_ready{l}"), 1)
                link(dve.tensor_copy(topf[:], topi[:, :, 0:2]))
                iota = bc(bc(C("iota"), 1, 2), 1, NQ)
                link(dve.tensor_tensor(oh[:], iota, bc(topf[:], 3, E), ALU.is_equal))
                dve.tensor_tensor(sel[:], oh[:, :, 0, :], oh[:, :, 1, :], ALU.add).then_inc(sem(f"sel{l}"), 1)
                dve.wait_ge(sem(f"ge_ready{l}"), 1)
                link(dve.tensor_scalar(gden[:], ge[:], 1.0, None, ALU.add))
                link(dve.reciprocal(gw[:, :, 0], gden[:]))
                link(dve.tensor_tensor(gw[:, :, 1], ge[:], gw[:, :, 0], ALU.mult))
                dve.wait_ge(sem(f"pos_mm{l}"), 1)
                cnt = bank[7][:, 128:128 + E]
                link(dve.tensor_scalar(ntf[:, 0, :], cnt, float(P), 1.0, ALU.is_gt, ALU.add))
                for t in (2, 3):
                    link(dve.scalar_tensor_tensor(out=ntf[:, 0, :], in0=cnt, scalar=float(t * P), in1=ntf[:, 0, :],
                                                  op0=ALU.is_gt, op1=ALU.add))
                link(dve.tensor_tensor_scan(ntf[:, 2, :], C("ones")[:, 0:E], ntf[:, 0, :], 0.0, ALU.mult, ALU.add))
                link(dve.tensor_tensor(ntf[:, 1, :], ntf[:, 2, :], ntf[:, 0, :], ALU.subtract))
                pos = bank[7][:, 64:64 + NQ * E].rearrange("p (q e) -> p q e", q=NQ)
                link(dve.scalar_tensor_tensor(out=rowf[:], in0=bc(ntf[:, 1, :], 1, NQ), scalar=float(P), in1=pos,
                                              op0=ALU.mult, op1=ALU.add))
                link(dve.tensor_tensor(ohr[:], oh[:], bc(rowf[:], 2, 2), ALU.mult))
                link(dve.tensor_reduce(ridf[:], ohr[:], AX_X, ALU.add))
                dve.tensor_copy(rid[:], ridf[:].rearrange("p q k -> p (q k)")).then_inc(sem(f"rid{l}"), 1)
                dve.tensor_copy(meta[:], ntf[:]).then_inc(sem(f"meta{l}"), 1)
            route(0, 2, 2, 2)

            dve.wait_ge(sem("ms_mm"), 1)
            ms = bank[4][:, 0:D].rearrange("p (b n) -> p b n", b=B)
            link(dve.tensor_reduce(mmx[:], ms, AX_X, ALU.max))
            dve.tensor_tensor(mpr[:], ms, bc(mmx[:], 2, NWIN), ALU.subtract).then_inc(sem("mem_shift"), 1)
            dve.wait_ge(sem("mem_exp"), 1)
            link(dve.tensor_reduce(msum[:], mpr[:], AX_X, ALU.add))
            link(dve.reciprocal(mmx[:], msum[:]))
            dve.tensor_tensor(mpr[:], mpr[:], bc(mmx[:], 2, NWIN), ALU.mult).then_inc(sem("mem_norm"), 1)
            dve.wait_ge(sem("mp_tr"), 1)
            pmask = C("pmask", 2, P)
            for q in range(NQ):
                h = q // 2
                ins = dve.tensor_tensor(ptm[:, q, :], bank[5][:, h * P:(h + 1) * P], pmask[:, q % 2, :], ALU.mult)
            ins.then_inc(sem("ptm_ready"), 1)
            dve.wait_ge(sem("mss_mm"), 1)
            dve.tensor_scalar(veps[:], bank[7][:, 192:192 + NQ], RMS_EPS, None, ALU.add).then_inc(sem("var_ready"), 1)
            dve.wait_ge(sem("rstd_ready"), 4)
            for q in range(NQ):
                ins = dve.scalar_tensor_tensor(out=memn[:, q, :], in0=bank[2 + q // 2][:, (q % 2) * D:(q % 2 + 1) * D],
                                               scalar=rinv[:, q:q + 1], in1=V("mnw"), op0=ALU.mult, op1=ALU.mult)
            ins.then_inc(sem("memn_ready"), 1)

            def ffn_loop(l, tile_body, b_of):
                dve.wait_ge(sem(f"meta{l}"), 1)
                with dve.Fori(0, 2) as half:
                    for s in range(SLOTS):
                        e = half * SLOTS + s
                        nt = dve.value_load(meta[0:1, 0, bass.ds(e, 1)], min_val=1, max_val=4)
                        first = dve.value_load(meta[0:1, 1, bass.ds(e, 1)], min_val=0, max_val=NT_MAX)
                        with dve.Fori(0, nt) as t:
                            n = first + t
                            dve.wait_ge(sem(f"row_used{l}"), HEAD + n + 1)
                            dve.tensor_copy(xT[:].rearrange("p k t -> p (k t)"), bank[0][:, 0:KT * P])\
                               .then_inc(sem(f"xT_done{l}"), 1)
                            tile_body(s, n)
                            dve.wait_ge(sem(f"y_mm{l}"), HEAD + n + 1)
                            dve.wait_ge(sem(f"y_stored{l}"), HEAD + n * 16)
                            dve.tensor_tensor(yrow[:], bank[7][:, 0:D], b_of(s), ALU.add).then_inc(sem(f"y_evac{l}"), 1)

            def tile0(s, n):
                dve.wait_ge(sem("g_mm"), HEAD + n * 2)
                for m in range(4):
                    dve.wait_ge(sem("x1_done"), n * 4 + (m + 1))
                    dve.scalar_tensor_tensor(out=zT[:, m, :], in0=bank[3 + m % 2][:, 0:P],
                                             scalar=E0(s, "b2")[:, m:m + 1], in1=hT[:, m, :], op0=ALU.add,
                                             op1=ALU.mult).then_inc(sem("z_done"), 1)

            ffn_loop(0, tile0, lambda s: E0(s, "b3"))

            def combine(l, done):
                for q in range(NQ):
                    for c in range(2):
                        ins = dve.scalar_tensor_tensor(out=x[:, q, :], in0=yk[:, q, c, :], scalar=gw[:, q, c:c + 1],
                                                       in1=x[:, q, :], op0=ALU.mult, op1=ALU.add)
                        if done and q == NQ - 1 and c:
                            ins.then_inc(sem("x_done"), 1)
                        else:
                            link(ins)
            dve.wait_ge(sem("gathered0"), 16 * 2 * NQ)
            combine(0, False)
            layer_norm(4, 3)
            dve.wait_ge(sem("ln_ready"), 16)
            dve.wait_ge(sem("memn_ready"), 1)
            for q in range(NQ):
                dve.tensor_tensor(ln[:, q, :], ln[:, q, :], memn[:, q, :], ALU.add).then_inc(sem("h2_ready"), 1)
            dve.wait_ge(sem("hss_mm"), 1)
            dve.tensor_scalar(veps[:], bank[7][:, 192:192 + NQ], RMS_EPS, None, ALU.add).then_inc(sem("var_ready"), 1)
            dve.wait_ge(sem("rstd_ready"), 6)
            for q in range(NQ):
                ins = dve.scalar_tensor_tensor(out=tmp[:, q, :], in0=ln[:, q, :], scalar=rinv[:, q:q + 1],
                                               in1=V("hnw"), op0=ALU.mult, op1=ALU.mult)
            link(ins)
            for q in range(NQ):
                dve.tensor_tensor(x[:, q, :], x[:, q, :], tmp[:, q, :], ALU.add).then_inc(sem("x_ready"), 1)
            dve.wait_ge(sem("x_ready"), 4)
            layer_norm(6, 4)
            lnT_half(3)
            for k in range(KT):
                dve.wait_ge(sem("q_mm1"), k + 1)
                ins = dve.tensor_copy(qT[:, k, :], bank[2 + k][:])
            link(ins)
            mask1 = masked(1, qT)
            mask1(0)

            def decay(i):
                k = i // NQ
                dve.wait_ge(sem("sc_mm1"), i + 1)
                if i >= 2:
                    dve.wait_ge(sem("pv_tile1"), i - 1)
                dve.tensor_tensor(pr[:, i % 2, :], bank[4 + i % 2][:], C("decay", KT, HH * S)[:, k, :], ALU.mult)\
                   .then_inc(sem("sc_decay"), 1)

            def evac_o1(k):
                dve.wait_ge(sem("pv_tile1"), NQ * (k + 1))
                for b2 in range(2):
                    dst = oT[:, k, :].rearrange("p (q b s) -> p q b s", q=NQ, b=2)[:, :, b2, :]
                    dve.tensor_copy(dst, bank[6 + b2][:, 0:NQ * S].rearrange("p (q s) -> p q s", q=NQ))\
                       .then_inc(sem("o_evac1"), 1)
            for i in range(2 * NQ):
                if i == NQ:
                    mask1(1)
                decay(i)
                if i == NQ:
                    evac_o1(0)
            evac_o1(1)
            dve.wait_ge(sem("o_evac1"), 4)
            o4 = oT[:].rearrange("p k (b s) -> p (k b) s", b=B)
            dve.tensor_reduce(gstat[:].rearrange("p k b -> p (k b)"), o4, AX_X, ALU.add).then_inc(sem("gsum_ready"), 1)
            dve.wait_ge(sem("gm_mm"), 1)
            link(dve.tensor_tensor(o4, o4, bc(bank[7][:, 256:272], 2, S), ALU.subtract))
            sq = tmp.rearrange("p q d -> p (q d)").rearrange("p (n s) -> p n s", s=S)
            link(dve.tensor_tensor(sq, o4, o4, ALU.mult))
            dve.tensor_reduce(gstat[:].rearrange("p k b -> p (k b)"), sq, AX_X, ALU.add).then_inc(sem("gsum_ready"), 1)
            dve.wait_ge(sem("gm_mm"), 2)
            dve.tensor_scalar(gvar[:].rearrange("p k b -> p (k b)"), bank[7][:, 288:304], GN_EPS, None, ALU.add)\
               .then_inc(sem("var_ready"), 1)
            dve.wait_ge(sem("rstd_ready"), 8)
            link(dve.tensor_tensor(gsc[:], grs[:], bc(V("gnw"), 2, B), ALU.mult))
            link(dve.tensor_tensor(o4, o4, bc(gsc[:].rearrange("p k b -> p (k b)"), 2, S), ALU.mult))
            for k in range(KT):
                dve.tensor_scalar(oT[:, k, :], oT[:, k, :], V("gnb")[:, k:k + 1], None, ALU.add)\
                   .then_inc(sem("oT_ready1"), 1)
            add_out(1, None, 1)
            route(1, 8, 5, 4)
            ffn_loop(1, lambda s, n: None, lambda s: E1(s, "b2"))
            dve.wait_ge(sem("gathered1"), 16 * 2 * NQ)
            combine(1, True)


def _view(t, at, dims):
    a, n = at
    v = t[:, a:a + n]
    if not dims:
        return v
    if len(dims) == 2:
        return v.rearrange("p (a b) -> p a b", a=dims[0])
    return v.rearrange("p (a b c) -> p a b c", a=dims[0], b=dims[1])


def _evac_prT(act, sem, prT, bank, i):
    act.wait_ge(sem("pr_tr"), i + 1)
    if i >= 2:
        act.wait_ge(sem("pv_tile0"), i - 1)
    act.activation(prT[:, i % 2, :], bank[0][:], ACT.Copy).then_inc(sem("prT_ready"), 1)


def kernel(**inputs):
    import concourse.bacc as _bacc
    from concourse.bass_utils import run_bass_kernel_spmd as _run

    arrays = layout({k: np.asarray(v) for k, v in inputs.items()})
    nc = _bacc.Bacc("TRN2", target_bir_lowering=False, num_devices=1)
    args = [nc.dram_tensor(n, a.shape, mybir.dt.from_np(a.dtype), kind="ExternalInput").ap()
            for n, a in arrays.items()]
    out = nc.dram_tensor("out_dram", (TOK, D), F32, kind="ExternalOutput").ap()
    perceiver(nc, *args, out)
    r = _run(nc, [arrays], core_ids=[0])
    return r.results[0]["out_dram"].reshape(B, S, D)


def layout(i):
    def rows(w):
        k = w.shape[0] // P
        return w.reshape(k, P, -1).transpose(1, 0, 2).reshape(P, -1)

    def col(v):
        return v.reshape(-1, P).T

    def wide(v):
        return np.broadcast_to(v.reshape(1, -1), (P, v.size))

    def pack(parts, cols):
        a = np.concatenate([parts[n] for n in cols], axis=-1)
        return np.ascontiguousarray(a)

    ar = np.arange(P)
    l, m = np.arange(S)[None, :], np.arange(S)[:, None]
    gam = np.array([1.0 - 2.0 ** (-5 - (8 * h) // H) for h in range(H)], np.float32)
    power = np.where(l >= m, gam[:, None, None] ** np.maximum(l - m, 0).astype(np.float32), 0).astype(np.float32)
    power = power * np.float32(HD ** -0.5)
    decay = np.tile(power.transpose(1, 0, 2).reshape(S, -1), (2, 1))
    f = np.float32
    consts = dict(
        ident=np.eye(P, dtype=f), tri=(ar[:, None] < ar[None, :]).astype(f), ones=np.ones((P, P), f),
        gmean=(ar[:, None] // HD == ar[None, :] // HD).astype(f) / f(HD * S),
        bmean=(ar[:, None] // S == ar[None, :] // S).astype(f) / f(S * D),
        pmask=np.concatenate([(ar[:, None] // NWIN == 2 * c + ar[None, :] // S).astype(f) for c in range(2)], 1),
        hmask=(ar[:, None] // HD == np.arange(HH)[None, :]).astype(f), decay=decay.astype(f),
        iota=np.tile(np.arange(E, dtype=f), (P, 1)))
    w = dict(Ws=rows(i["L0_xattn_Ws"]), W=rows(i["L0_xattn_W"]), wvec=col(i["L0_xattn_w"]), bvec=col(i["L0_xattn_b"]))
    heads = lambda a: rows(a.transpose(1, 0, 2).reshape(D, D))
    v = dict(
        qkv=rows(i["L0_attn_W_qkv"].T), wo=rows(i["L0_attn_W_out"].T), bqk=col(i["L0_attn_b_qkv"][0:2 * D]),
        wcw=wide(i["L0_xattn_Wcw"]), wcb=wide(i["L0_xattn_Wcb"]), bcw=wide(i["L0_xattn_bcw"]),
        bcb=wide(i["L0_xattn_bcb"]), bv=wide(i["L0_attn_b_qkv"][2 * D:]), bo=wide(i["L0_attn_b_out"]),
        gw0=rows(i["L0_ffn_gate_w"]), gb0=wide(i["L0_ffn_gate_b"]), gw1=rows(i["L1_ffn_w_gate"]),
        qawk=rows(i["L1_xattn_qa_wk"].T), qawv=rows(i["L1_xattn_qa_wv"].T), qaq=rows(np.tile(i["L1_xattn_qa_q"].T, (1, 2))),
        mnw=np.tile(i["L1_xattn_mn_w"], (2, 1)), hnw=np.tile(i["L1_xattn_hn_w"], (2, 1)),
        gnw=col(i["L1_attn_gn_weight"]), gnb=col(i["L1_attn_gn_bias"]))

    r = dict(rq=heads(i["L1_attn_Wq"]), rk=heads(i["L1_attn_Wk"]), rv=heads(i["L1_attn_Wv"]),
             ro=rows(i["L1_attn_Wout"]))

    def erows(a):
        return np.stack([rows(a[e]) for e in range(E)])

    def ecol(a):
        return np.stack([col(a[e]) for e in range(E)])

    def ewide(a):
        return np.stack([wide(a[e]) for e in range(E)])

    e0 = dict(w1=erows(i["L0_ffn_w1"]), w2=erows(i["L0_ffn_w2"]), wg=erows(i["L0_ffn_wg"]), w3=erows(i["L0_ffn_w3"]),
              b1=ecol(i["L0_ffn_b1"]), b2=ecol(i["L0_ffn_b2"]), bg=ecol(i["L0_ffn_bg"]), b3=ewide(i["L0_ffn_b3"]))
    e1 = dict(w1=erows(i["L1_ffn_w1"]), w2=erows(i["L1_ffn_w2"]), b1=ecol(i["L1_ffn_b1"]), b2=ewide(i["L1_ffn_b2"]))
    c = i["ctx_1024"]
    ws = i["L1_xattn_ws_w"].T.reshape(NQ, 8, P, D).transpose(0, 2, 1, 3)
    mask = np.repeat(i["mask_BxS2_ik0"], S, axis=0).reshape(NQ, P, T).transpose(1, 0, 2)
    return dict(
        x_in=np.ascontiguousarray(i["x"].reshape(TOK, D)),
        ctx_rows=np.ascontiguousarray(c.reshape(B, 2, P, D).transpose(2, 0, 1, 3)),
        ctx_cols=np.ascontiguousarray(c.transpose(2, 0, 1).reshape(KT, P, B, T).transpose(1, 0, 2, 3)),
        mask_in=np.ascontiguousarray(mask), w_in=pack(w, W_COLS), c_in=pack(consts, C_COLS), v_in=pack(v, V_COLS), r_in=pack(r, R_COLS),
        ws_in=np.ascontiguousarray(ws), e0_in=pack(e0, E0_COLS), e1_in=pack(e1, E1_COLS))
```

```python
from contextlib import ExitStack

import numpy as np
import concourse.bass as bass
from concourse import mybir

F32 = mybir.dt.float32
I32 = mybir.dt.int32
U32 = mybir.dt.uint32
ALU = mybir.AluOpType
ACT = mybir.ActivationFunctionType
AX_X = mybir.AxisListType.X
P = 128

B, S, D, T = 8, 64, 256, 256
TOK = B * S
NQ = TOK // P
KT = D // P
H, HD = 16, D // 16
HH = H // KT
STRIDE, WIN = 8, 16
NWIN = T // STRIDE
TPAD = T + STRIDE
E = 8
F0 = 512
F1 = 1024
NT_MAX = 15
NEG = -1e30
NT_ROWS = NT_MAX + 5
LN_EPS, GN_EPS, RMS_EPS = 1e-5, 1e-5, 1.1920929e-07
HEAD = 1
SLOTS = 4

W_COLS = dict(W=KT * D, Ws=KT * D, wvec=KT, bvec=KT, ident=P)
C_COLS = dict(tri=P, ones=P, gmean=P, bmean=P, pmask=2 * P, hmask=HH, decay=KT * HH * S,
              iota=P)
V_COLS = dict(qkv=KT * 3 * D, wo=KT * D, bqkv=6, wcw=D, wcb=D, bcw=1, bcb=1, bo=D,
              gw0=KT * 32, gb0=E, gw1=KT * 32, qawk=KT * D, qawv=KT * D, qaq=KT * P, mnw=D, hnw=D,
              gnw=KT, gnb=KT)
R_COLS = dict(rq=KT * D, rk=KT * D, rv=KT * D, ro=KT * D)
E0_COLS = dict(w1=KT * F0, w2=KT * F0, wg=4 * F0, w3=4 * D, b1=4, b2=4, bg=4, b3=D)
E1_COLS = dict(w1=KT * F1, w2=8 * D, b1=8, b2=D)


def offsets(cols):
    at, out = 0, {}
    for name, n in cols.items():
        out[name] = (at, n)
        at += n
    return out, at


W_AT, W_N = offsets(W_COLS)
C_AT, C_N = offsets(C_COLS)
V_AT, V_N = offsets(V_COLS)
R_AT, R_N = offsets(R_COLS)
E0_AT, E0_N = offsets(E0_COLS)
E1_AT, E1_N = offsets(E1_COLS)


def perceiver(nc, x_in, ctx_rows, ctx_cols, mask_in, w_in, c_in, v_in, r_in, ws_in, e0_in, e1_in, out):
    with ExitStack() as ctx:
        def sb(name, shape, dt=F32):
            return ctx.enter_context(nc.sbuf_tensor(name, shape, dt))

        sems = {}

        def sem(name):
            if name not in sems:
                sems[name] = ctx.enter_context(nc.semaphore(name))
            return sems[name]

        bank = [ctx.enter_context(nc.psum_tensor(f"bank{i}", [P, 512], F32)) for i in range(8)]

        xg = [nc.dram_tensor(f"expert_rows{l}", [NT_ROWS * P, D], F32).ap() for l in range(2)]
        yg = [nc.dram_tensor(f"expert_out{l}", [NT_ROWS * P, D], F32).ap() for l in range(2)]

        w_sb = sb("w_sb", [P, W_N])
        c_sb = sb("c_sb", [P, C_N])
        v_sb = sb("v_sb", [P, V_N])

        def W(name, *dims):
            return _view(w_sb, W_AT[name], dims)

        def C(name, *dims):
            return _view(c_sb, C_AT[name], dims)

        def V(name, *dims):
            return _view(v_sb, V_AT[name], dims)

        def R(name, *dims):
            return _view(v_sb, R_AT[name], dims)

        x = sb("x", [P, NQ, D])
        ln = sb("ln", [P, NQ, D])
        lnT = sb("lnT", [P, KT, TOK])
        bn = sb("bn", [P, NQ, 6])
        mv = sb("mv", [P, NQ, 2])
        veps = sb("veps", [P, NQ])
        mhalf = sb("mhalf", [P, 16])
        token = sb("token", [P, 1])
        rstd = sb("rstd", [P, NQ])
        zeros = sb("zeros", [P, D])
        memn = sb("memn", [P, NQ, D])

        arena_a = sb("arena_a", [P, 2 * E0_N + NQ * D])
        hbuf = arena_a[:, 0:4 * 2048].rearrange("p (s g k t) -> p s g k t", s=SLOTS, g=4, k=KT)
        tmp = arena_a[:, 2 * E0_N:2 * E0_N + NQ * D].rearrange("p (q d) -> p q d", q=NQ)
        arena_s = sb("arena_s", [P, 2 * E0_N])
        slot = [arena_s[:, 0:E0_N], arena_s[:, E0_N:2 * E0_N],
                arena_a[:, 0:E0_N], arena_a[:, E0_N:2 * E0_N]]

        arena_b = sb("arena_b", [P, 11264])
        at = [0]

        def carve(n):
            a = at[0]
            at[0] += n
            assert at[0] <= 11264, at[0]
            return arena_b[:, a:a + n]

        ctxT = carve(KT * B * TPAD).rearrange("p (k b t) -> p k b t", k=KT, b=B)
        ctxN = carve((B + 2) * 2 * D).rearrange("p (b h d) -> p b h d", b=B + 2, h=2)
        txs_at = at[0]
        txs = carve(KT * 2 * T).rearrange("p (k b t) -> p k b t", k=KT, b=2)
        rho = carve(T)
        fts = carve(KT * P).rearrange("p (k f) -> p k f", k=KT)
        at[0] = 0
        blk = carve(HH * TOK).rearrange("p (h t) -> p h t", h=HH)
        blks = [blk, slot[3][:, 0:HH * TOK].rearrange("p (h t) -> p h t", h=HH)]
        vblk = carve(B * D).rearrange("p (b g c e) -> p b g c e", b=B, g=H // 2, c=2)
        qT = carve(KT * TOK).rearrange("p (k t) -> p k t", k=KT)
        kT = carve(KT * TOK).rearrange("p (k t) -> p k t", k=KT)
        oT = carve(KT * TOK).rearrange("p (k t) -> p k t", k=KT)
        at[0] = HH * TOK
        vz = carve(NQ * H * 32).rearrange("p (q h e) -> p q h e", q=NQ, h=H)
        assert NQ * H * 32 <= B * D
        at[0] = txs_at
        smT = carve(KT * B * NWIN).rearrange("p (k n) -> p k n", k=KT)
        qkT = carve(KT * B * NWIN).rearrange("p (k n) -> p k n", k=KT)
        qv = carve(2 * D).rearrange("p (h d) -> p h d", h=2)
        mpr = carve(B * NWIN).rearrange("p (b n) -> p b n", b=B)

        arena_c = sb("arena_c", [P, 5120])
        pr = arena_c[:, 0:3 * 512].rearrange("p (s n) -> p s n", s=3)
        prT = arena_c[:, 3 * 512:5 * 512].rearrange("p (s n) -> p s n", s=2)
        ws_sb = arena_c[:, 0:8 * D].rearrange("p (k d) -> p k d", k=8)
        negm = arena_c[:, 2048:2048 + (NQ + 1) * T].rearrange("p (q t) -> p q t", q=NQ + 1)
        mask_sb = negm[:, 1:, :].bitcast(I32)
        attT = arena_c[:, 3328:3328 + 4 * P].rearrange("p (h b f) -> p h b f", h=2, b=2)
        featT = arena_c[:, 4096:5120].rearrange("p (k t) -> p k t", k=KT)
        wz = sb("wz", [P, KT, 63])
        nmax = sb("nmax", [P, 1])
        rsum = sb("rsum", [P, NQ + 1])
        rinv = sb("rinv", [P, NQ])
        dots = sb("dots", [P, NQ + 1, 2])
        dot = sb("dot", [P, 2])
        wbpre = sb("wbpre", [P, NQ, 2])
        wbs = sb("wbs", [P, 2, NQ])
        junk = sb("junk", [P, 2 * D])
        hmx = sb("hmx", [P, 2, HH])
        hsum = sb("hsum", [P, 2, HH])
        hinv = sb("hinv", [P, 2, HH])
        gstat = sb("gstat", [P, KT, B])
        gvar = sb("gvar", [P, KT, B])
        grs = sb("grs", [P, KT, B])
        gsc = sb("gsc", [P, KT, B])
        ssq = sb("ssq", [P, NQ])
        mmx = sb("mmx", [P, B])
        msum = sb("msum", [P, B])
        ca = [0]

        def carve_c(*dims):
            n = int(np.prod(dims))
            a = ca[0]
            ca[0] += n
            return _view(arena_c, (a, n), dims if len(dims) > 1 else ())
        ptm = carve_c(NQ, P)
        lgT = carve_c(P)
        pick = carve_c(NQ, P)
        lastw = carve_c(NQ, P)
        lastT = carve_c(NQ, P)
        lg = sb("lg", [P, NQ, E])
        top = sb("top", [P, NQ, 8])
        topi = sb("topi", [P, NQ, 8], U32)
        topf = sb("topf", [P, NQ, 2])
        oh = sb("oh", [P, NQ, 2, E])
        sel = sb("sel", [P, NQ + 1, E])
        ntf = sb("ntf", [P, 3, E])
        rowf = sb("rowf", [P, NQ, E])
        ohr = sb("ohr", [P, NQ, 2, E])
        ridf = sb("ridf", [P, NQ, 2])
        rid = sb("rid", [P, NQ * 2], U32)
        meta = sb("meta", [P, 3, E], I32)
        gd = sb("gd", [P, NQ])
        ge = sb("ge", [P, NQ])
        lrow = sb("lrow", [P, NQ])
        lwt = sb("lwt", [P, NQ, 2])
        lsum = sb("lsum", [P, NQ])
        loff = sb("loff", [P, 1])
        gden = sb("gden", [P, NQ])
        gw = sb("gw", [P, NQ, 2])
        xrow = carve_c(D)
        xT = carve_c(KT, P)
        hT = carve_c(8, P)
        zT = carve_c(4, P)
        sT = carve_c(4, P)
        yrow = carve_c(D)
        assert ca[0] <= 5120
        yk = arena_b[:, 0:NQ * 2 * D].rearrange("p (q k d) -> p q k d", q=NQ, k=2)

        blk_ctx = ctx.enter_context(nc.Block())
        block = blk_ctx

        def bc(ap, axis, n):
            a = ap.unsqueeze(axis)
            shape = list(a.shape)
            shape[axis] = n
            return a.broadcast_to(shape)

        SC = (4, 5, 1)
        MB = (2, 6)
        VB = (0, 2, 3, 1)

        def experts(l, slot_of, at_of):
            def view(s, name, *dims):
                a, n = at_of[name]
                return _view(slot_of[s], (a, n), dims)
            return view

        E0 = experts(0, slot, E0_AT)
        E1 = experts(1, slot, E1_AT)

        @block.sync
        def _(sp):
            sp.dma_start(x[:], x_in.rearrange("(q p) d -> p q d", p=P)).then_inc(sem("x_in"), 16)
            sp.dma_start(w_sb[:], w_in).then_inc(sem("w_in"), 16)
            for q in range(NQ):
                for k in range(KT):
                    sp.dma_start(ctxT[:, k, 2 * q:2 * q + 2, 0:T], ctx_cols[:, k, 2 * q:2 * q + 2])\
                      .then_inc(sem(f"ctxT_in{q}"), 16)
            sp.dma_start(mask_sb[:], mask_in).then_inc(sem("mask_in"), 16)
            sp.dma_start(ws_sb[:], ws_in[0]).then_inc(sem("ws_in"), 16)
            sp.dma_start(c_sb[:], c_in).then_inc(sem("c_in"), 16)
            sp.dma_start(ctxN[:, 2:], ctx_rows).then_inc(sem("ctxN_in"), 16)
            sp.dma_start(v_sb[:], v_in).then_inc(sem("v_in"), 16)
            with sp.Fori(0, NQ - 1) as p:
                sp.wait_ge(sem("ws_used"), p + 1)
                sp.dma_start(ws_sb[:], ws_in[bass.ds(p + 1, 1)].rearrange("o p k d -> (o p) k d")).then_inc(sem("ws_in"), 16)
            sp.wait_ge(sem("pool_const"), 5)
            for l in range(2):
                for rows in (xg[l], yg[l]):
                    sp.dma_start(rows.rearrange("(n p) d -> p n d", p=P),
                                 bc(zeros[:], 1, NT_ROWS)).then_inc(sem("rows_zero"), 16)
            sp.wait_ge(sem("o_mm0"), NQ)
            sp.dma_start(v_sb[:, 0:R_N], r_in).then_inc(sem("r_in"), 16)
            for l in range(2):
                sp.wait_ge(sem(f"meta{l}"), 1)
                sp.wait_ge(sem(f"scattered{l}"), 16 * 2 * NQ)
                with sp.Fori(0, 2) as half:
                    for s in range(SLOTS):
                        e = half * SLOTS + s
                        nt = sp.value_load(meta[0:1, 0, bass.ds(e, 1)], min_val=1, max_val=4)
                        first = sp.value_load(meta[0:1, 1, bass.ds(e, 1)], min_val=0, max_val=NT_MAX - 1)
                        with sp.Fori(0, nt) as t:
                            n = first + t
                            sp.wait_ge(sem(f"row_used{l}"), n + 1)
                            sp.dma_start(xrow[:], xg[l][bass.ds(n * P + 2 * P, P), :]).then_inc(sem(f"row_in{l}"), 16)
            for q in range(NQ):
                sp.wait_ge(sem("x_done"), q + 1)
                sp.dma_start(out[q * P:(q + 1) * P, :], x[:, q, :]).then_inc(sem("out_done"), 16)
            sp.wait_ge(sem("out_done"), 16 * NQ)

        @block.gpsimd
        def _(pool):
            def rsqrt(k, dst, src, n):
                pool.wait_ge(sem("var_ready"), k + 1)
                pool.tensor_tensor(dst, src, mhalf[:, 0:n], ALU.pow).then_inc(sem("rstd_ready"), 1)

            passes = [0]

            def passed():
                passes[0] += 1
                pool.tensor_tensor(token[:], mhalf[:, 0:1], mhalf[:, 0:1], ALU.add).then_inc(sem("passed"), 1)
                pool.wait_ge(sem("passed"), passes[0])

            pool.sem_inc(sem("h_filled3"), HEAD)
            pool.memset(mhalf[:], -0.5).then_inc(sem("pool_const"), 1)
            pool.memset(zeros[:], 0.0).then_inc(sem("pool_const"), 1)
            pool.memset(ctxT[:, :, :, T:TPAD], 0.0).then_inc(sem("pool_const"), 1)
            pool.memset(ctxN[:, 0:2], 0.0).then_inc(sem("pool_const"), 1)
            pool.memset(attT[:], 0.0).then_inc(sem("pool_const"), 1)
            pool.wait_ge(sem("pool_const"), 5)
            rsqrt(0, rstd[:], veps[:], NQ)
            with pool.Fori(0, NQ) as p:
                pool.wait_ge(sem("staged"), p * 3 + 3)
                for j in range(32):
                    pool.wait_ge(sem("slot_free"), p * 32 + (j + 1))
                    pool.tensor_tensor(hbuf[:, j % SLOTS, 3], txs[:, :, 1, :],
                                       fts[:, :, 96 + j:97 + j].broadcast_to([P, KT, T]), ALU.add)\
                        .then_inc(sem("h_filled3"), 1)
            pool.wait_ge(sem("slot_free"), SLOTS + NQ * 32)
            pool.wait_ge(sem("staged"), 3 * NQ)
            for s in range(3):
                pool.dma_start(slot[s][:, 0:E0_N], e0_in[s]).then_inc(sem(f"slot{s}_in"), 16)
            rsqrt(1, rstd[:], veps[:], NQ)
            pool.wait_ge(sem("x1_ready"), NQ)
            pool.memset(vblk[:], 0.0).then_inc(sem("vblk_zero"), 1)
            for i in range(2 * NQ):
                pool.wait_ge(sem("sc_inv"), i + 1)
                v = pr[:, i % 3, :].rearrange("p (h m) -> p h m", h=HH)
                pool.tensor_tensor(v, v, bc(hinv[:, i % 2, :], 2, S), ALU.mult).then_inc(sem("sc_norm"), 1)

            pool.wait_ge(sem("sc_mm0"), 2 * NQ)
            pool.dma_start(slot[3][:, 0:E0_N], e0_in[3]).then_inc(sem("slot3_in"), 16)

            def route(l, k, n_in):
                rsqrt(k, rstd[:], veps[:], NQ)
                pool.wait_ge(sem("rows_zero"), 64)
                pool.wait_ge(sem("ln_ready"), 4 * (n_in + 1))
                pool.wait_ge(sem("rid"), l + 1)
                for q in range(NQ):
                    for c in range(2):
                        pool.indirect_dma_start(
                            out=xg[l], out_offset=bass.IndirectOffsetOnAxis(ap=rid[:, 2 * q + c:2 * q + c + 1], axis=0),
                            in_=ln[:, q, :], in_offset=None).then_inc(sem(f"scattered{l}"), 16)

            def more_weights(l, experts_, e_in, n_cols, next_in, next_cols):
                for e in experts_:
                    s = e % SLOTS
                    end = pool.value_load(meta[0:1, 2, e:e + 1], min_val=1, max_val=NT_MAX)
                    if e + SLOTS < E:
                        pool.wait_ge(sem(f"y_evac{l}"), HEAD + end)
                        passed()
                        pool.dma_start(slot[s][:, 0:n_cols], e_in[e + SLOTS]).then_inc(sem(f"slot{s}_in"), 16)
                    elif next_in is not None:
                        pool.wait_ge(sem(f"y_evac{l}"), HEAD + end)
                        passed()
                        pool.dma_start(slot[s][:, 0:next_cols], next_in[s]).then_inc(sem(f"slot{s}_in"), 16)

            def gather(l):
                end = pool.value_load(meta[0:1, 2, E - 1:E], min_val=E, max_val=NT_MAX)
                pool.wait_ge(sem(f"y_stored{l}"), end * 16)
                passed()
                for q in range(NQ):
                    for c in range(2):
                        pool.indirect_dma_start(
                            out=yk[:, q, c, :], out_offset=None, in_=yg[l],
                            in_offset=bass.IndirectOffsetOnAxis(ap=rid[:, 2 * q + c:2 * q + c + 1], axis=0)
                        ).then_inc(sem(f"gathered{q}"), 16)

            route(0, 2, 2)
            pool.wait_ge(sem(f"meta0"), 1)
            rsqrt(3, rinv[:], veps[:], NQ)
            more_weights(0, range(E - 1), e0_in, E0_N, e1_in, E1_N)
            gather(0)
            more_weights(0, range(E - 1, E), e0_in, E0_N, e1_in, E1_N)
            rsqrt(4, rstd[:], veps[:], NQ)
            rsqrt(5, rinv[:], veps[:], NQ)
            rsqrt(6, rstd[:], veps[:], NQ)
            pool.wait_ge(sem("x_ready"), 4)
            pool.memset(vz[:], 0.0).then_inc(sem("vz_zero"), 1)
            rsqrt(7, grs[:].rearrange("p k b -> p (k b)"), gvar[:].rearrange("p k b -> p (k b)"), KT * B)
            route(1, 8, 5)
            pool.wait_ge(sem(f"meta1"), 1)
            more_weights(1, range(SLOTS), e1_in, E1_N, None, 0)
            gather(1)

        @block.scalar
        def _(act):
            for name in ("s_done", "h_done"):
                act.sem_inc(sem(name), HEAD)
            def lnT_half(k):
                act.wait_ge(sem("tr_ready"), k + 1)
                act.activation(lnT[:, 0, :], bank[0][:], ACT.Copy).then_inc(sem("lnT0_ready"), 1)

            def ffn_loop(l, tile_body):
                act.wait_ge(sem(f"meta{l}"), 1)
                with act.Fori(0, 2) as half:
                    for s in range(SLOTS):
                        e = half * SLOTS + s
                        nt = act.value_load(meta[0:1, 0, bass.ds(e, 1)], min_val=1, max_val=4)
                        first = act.value_load(meta[0:1, 1, bass.ds(e, 1)], min_val=0, max_val=NT_MAX - 1)
                        with act.Fori(0, nt) as t:
                            tile_body(s, first + t)

            lnT_half(0)
            act.wait_ge(sem("w_in"), 16)
            for m in range(KT):
                act.wait_ge(sem("feat_mm"), m + 1)
                act.activation(featT[:, m, :], bank[2 + m][:], ACT.Identity,
                               bias=W("bvec")[:, m:m + 1]).then_inc(sem("feat_ready"), 1)
            def exp_scores(n):
                act.wait_ge(sem("nmax_ready"), n + 1)
                act.activation(rho[:], rho[:], ACT.Exp, bias=nmax[:],
                               accum_out=rsum[:, n:n + 1] if isinstance(n, int) else rsum[:, bass.ds(n, 1)])\
                   .then_inc(sem("att_exp"), 1)

            with act.Fori(0, NQ) as p:
                for j in range(32):
                    if j == 7:
                        exp_scores(p)
                    act.wait_ge(sem("h_filled"), HEAD + p * 32 + (j + 1))
                    act.wait_ge(sem("h_filled3"), HEAD + p * 32 + (j + 1))
                    hj = hbuf[:, j % SLOTS].rearrange("p g k t -> p (g k t)")
                    act.activation(hj, hj, ACT.Tanh).then_inc(sem("h_tanh"), 1)
            exp_scores(NQ)
            for m in range(KT):
                act.wait_ge(sem("sm_mm"), 1)
                act.activation(smT[:, m, :], bank[2 + m][:, 0:D], ACT.Copy).then_inc(sem("smT_ready"), 1)
            act.wait_ge(sem("v_in"), 16)
            act.wait_ge(sem("wbpre_ready"), 1)
            for c, b_ in enumerate(("bcw", "bcb")):
                act.activation(wbs[:, c, :], wbpre[:, :, c], ACT.Tanh, bias=V(b_)).then_inc(sem("wbs_ready"), 1)
            for m in range(KT):
                act.wait_ge(sem("qk_mm"), m + 1)
                act.activation(qkT[:, m, :], bank[4 + m][:, 0:D], ACT.Copy).then_inc(sem("qkT_ready"), 1)
            for h in range(2):
                act.wait_ge(sem("qv_mm"), 2)
                act.activation(qv[:, h, :], bank[3][:, h * D:(h + 1) * D], ACT.Copy).then_inc(sem("qv_ready"), 1)
            lnT_half(1)
            for k in range(KT):
                act.wait_ge(sem("k_mm0"), k + 1)
                act.activation(kT[:, k, :], bank[4 + k][:], ACT.Identity,
                               bias=V("bqkv")[:, 2 + k:3 + k]).then_inc(sem("kT_ready0"), 1)
            act.wait_ge(sem("mem_shift"), 1)
            m2 = mpr[:].rearrange("p b n -> p (b n)")
            act.activation(m2, m2, ACT.Exp, scale=1.0 / 16.0).then_inc(sem("mem_exp"), 1)
            def values_evac(q):
                act.wait_ge(sem("v_mm0"), q + 1)
                if q == 0:
                    act.wait_ge(sem("vblk_zero"), 1)
                v_ps = bank[VB[q]][:].rearrange("p (b g c e) -> p b g c e", b=2, g=HH, c=2)
                for c in range(2):
                    r = slice(64 * c, 64 * c + 64)
                    act.activation(vblk[r, 2 * q:2 * q + 2, :, c, :], v_ps[r, :, :, c, :], ACT.Copy)\
                       .then_inc(sem("vblk_ready"), 1)

            values_evac(0)
            values_evac(1)
            for i in range(2 * NQ):
                if i == 1:
                    values_evac(2)
                    values_evac(3)
                act.wait_ge(sem("sc_shift"), i + 1)
                act.activation(pr[:, i % 3, :], pr[:, i % 3, :], ACT.Exp).then_inc(sem("sc_exp"), 1)
                if i >= 1:
                    _evac_prT(act, sem, prT, bank, i - 1)
            _evac_prT(act, sem, prT, bank, 2 * NQ - 1)
            for k in range(KT):
                act.wait_ge(sem("pv_tile0"), NQ * (k + 1))
                act.activation(oT[:, k, :], bank[6 + k][:], ACT.Identity, bias=V("bqkv")[:, 4 + k:5 + k])\
                   .then_inc(sem("oT_ready0"), 1)
            lnT_half(2)
            act.wait_ge(sem("gd_ready"), 1)
            act.activation(ge[:], gd[:], ACT.Exp).then_inc(sem("ge_ready"), 1)
            act.wait_ge(sem("mem_mm"), 1)
            for q in range(NQ):
                act.activation(tmp[:, q, :], bank[MB[q // 2]][:, (q % 2) * D:(q % 2 + 1) * D], ACT.Square,
                               accum_out=ssq[:, q:q + 1]).then_inc(sem("mem_sq"), 1)
            for h in range(2):
                act.activation(memn[:, 2 * h:2 * h + 2, :].rearrange("p q d -> p (q d)"), bank[MB[h]][:], ACT.Copy)\
                   .then_inc(sem("mem_raw"), 1)

            def last_evac(l):
                act.wait_ge(sem("last_tr"), l + 1)
                act.activation(lastT[:].rearrange("p q t -> p (q t)"), bank[6][:], ACT.Copy)\
                   .then_inc(sem("lastT_ready"), 1)

            def tile0(s, n):
                store(0, n)
                act.wait_ge(sem("y_mm0"), HEAD + n)
                for m in range(4):
                    act.wait_ge(sem("g_mm"), HEAD + n * 2 + (m // 2 + 1))
                    act.activation(sT[:, m, :], bank[5 + m // 2][:, (m % 2) * P:(m % 2 + 1) * P], ACT.Silu,
                                   bias=E0(s, "bg")[:, m:m + 1]).then_inc(sem("s_done"), 1)

            def store(l, n):
                act.wait_ge(sem(f"y_evac{l}"), HEAD + n)
                act.dma_start(yg[l][bass.ds(n * P, P), :], yrow[:]).then_inc(sem(f"y_stored{l}"), 16)

            def tile1(s, n):
                store(1, n)
                act.wait_ge(sem("y_mm1"), HEAD + n)
                for m in range(8):
                    act.wait_ge(sem("h_mm"), n * 4 + (m // 2 + 1))
                    act.activation(hT[:, m, :], bank[1 + m // 2][:, (m % 2) * P:(m % 2 + 1) * P], ACT.Gelu,
                                   bias=E1(s, "b1")[:, m:m + 1]).then_inc(sem("h_done"), 1)

            last_evac(0)
            act.wait_ge(sem("rows_zero"), 64)
            for s in range(SLOTS):
                act.wait_ge(sem(f"slot{s}_in"), 16)
            ffn_loop(0, tile0)
            for q in range(NQ):
                act.wait_ge(sem("h2_ready"), q + 1)
                act.activation(tmp[:, q, :], ln[:, q, :], ACT.Square,
                               accum_out=ssq[:, q:q + 1]).then_inc(sem("h2_sq"), 1)
            lnT_half(3)
            for k in range(KT):
                act.wait_ge(sem("k_mm1"), k + 1)
                act.activation(kT[:, k, :], bank[4 + k][:], ACT.Copy).then_inc(sem("kT_ready1"), 1)
            for q in range(NQ):
                for c in range(2):
                    act.wait_ge(sem("v_mm1"), 2 * (q // 2) + 2)
                    if q == 0:
                        act.wait_ge(sem("vz_zero"), 1)
                    v_ps = bank[6 + q // 2][:, (q % 2) * D:(q % 2 + 1) * D].rearrange("p (g c e) -> p g c e", c=2, e=HD)
                    vz_v = vz[:, q].rearrange("p (g c) (d e) -> p g c d e", c=2, e=HD)
                    act.activation(vz_v[:, :, c, c, :], v_ps[:, :, c, :], ACT.Copy).then_inc(sem("vz_ready"), 1)
            lnT_half(4)
            act.wait_ge(sem("gd_ready"), 2)
            act.activation(ge[:], gd[:], ACT.Exp).then_inc(sem("ge_ready"), 1)
            last_evac(1)
            for s in range(SLOTS):
                act.wait_ge(sem(f"slot{s}_in"), 16 * 3)
            ffn_loop(1, tile1)

        @block.tensor
        def _(pe):
            ident = W("ident")
            for name in ("y_mm0", "y_mm1", "g_mm"):
                pe.sem_inc(sem(name), HEAD)

            def ln_transpose(k, n):
                for q in range(NQ):
                    pe.wait_ge(sem("ln_ready"), 4 * n + q + 1)
                    for kt in range(KT):
                        ins = pe.transpose(bank[kt][:, q * P:(q + 1) * P], ln[:, q, kt * P:(kt + 1) * P], ident)
                ins.then_inc(sem("tr_ready"), 1)

            def project(dst, w, o, m=P):
                for kt in range(KT):
                    ins = pe.matmul(dst, w[:, kt, o:o + m], lnT[:, kt, :], start=(kt == 0), stop=(kt == KT - 1))
                return ins

            Wf, Ws = W("W", KT, D), W("Ws", KT, D)

            def project_context(m, kt, b):
                return pe.matmul(bank[4 + m][:], Ws[:, kt, m * P:(m + 1) * P], ctxT[:, kt, bass.ds(b, 2), 0:T],
                                 start=(kt == 0), stop=(kt == KT - 1))

            pe.wait_ge(sem("w_in"), 16)
            ln_transpose(0, 0)
            pe.wait_ge(sem("ctxT_in0"), 32)
            for m in range(KT):
                for kt in range(KT):
                    ins = project_context(m, kt, 0)
                ins.then_inc(sem("txt_mm"), 1)
            for half in ("lnT0_ready", "lnT1_ready"):
                pe.wait_ge(sem(half), 1)
            for m in range(KT):
                project(bank[2 + m][:], Wf, m * P).then_inc(sem("feat_mm"), 1)
            pe.wait_ge(sem("feat_ready"), 2)
            pe.wait_ge(sem("pool_const"), 5)
            for m in range(KT):
                pe.matmul(bank[2 + m][:, 0:D], zeros[:, 0:P], zeros[:], start=True, stop=False)
            pe.matmul(bank[0][:, 0:T], zeros[:, 0:P], zeros[:], start=True, stop=True).then_inc(sem("rho_open"), 1)
            pe.wait_ge(sem("wz_ready"), 1)
            def turn_att(n):
                pe.wait_ge(sem("att_exp"), n + 1)
                for h in range(2):
                    ins = pe.transpose(bank[6][:, h * P:(h + 1) * P], rho[:, h * P:(h + 1) * P], ident)
                ins.then_inc(sem("att_tr"), 1)

            def attend(n, i):
                h, b2 = i // 2, i % 2
                if i == 0:
                    pe.wait_ge(sem("ctxN_in"), 16)
                    pe.wait_ge(sem("attT_ready"), n + 1)
                    pe.wait_ge(sem("dots_ready"), HEAD + 3 * n)
                ctx_b = ctxN[:, 2 * n + b2, h, :] if isinstance(n, int) else ctxN[:, bass.ds(n * 2 + b2, 1), h, :]
                ins = pe.matmul(bank[7][:, 0:D], attT[:, h, b2, :], ctx_b, start=(i == 0), stop=(i == 3))
                if i == 3:
                    ins.then_inc(sem("txth_mm"), 1)

            def pair(p, last):
                for j in range(32):
                    pe.wait_ge(sem("h_tanh"), p * 32 + (j + 1))
                    if j == 0:
                        pe.wait_ge(sem("rho_evac"), p + 1)
                    for k in range(KT):
                        for g in range(4):
                            ins = pe.matmul(bank[0][32 * g:32 * g + 32, 0:T], wz[:, k, 31 - j:63 - j],
                                            hbuf[:, j % SLOTS, g, k, :], start=(j == 0 and k == 0),
                                            stop=(j == 31 and k == KT - 1))
                    ins.then_inc(sem("slot_free"), 1)
                    if 12 <= j < 16 and not last:
                        if j == 12:
                            for q in range(1, NQ):
                                pe.wait_ge(sem(f"ctxT_in{q}"), 32)
                            pe.wait_ge(sem("staged"), p * 3 + 3)
                        ins = project_context((j - 12) // KT, j % KT, p * 2 + 2)
                        if j % KT == KT - 1:
                            ins.then_inc(sem("txt_mm"), 1)
                    if j == 9:
                        turn_att(p)
                    if 20 <= j < 24:
                        attend(p, j - 20)
                    if j == 16:
                        pe.wait_ge(sem("ws_in"), (p + 1) * 16)
                    if j >= 16:
                        i, m = j // 2 - 8, j % 2
                        ins = pe.matmul(bank[2 + m][:, 0:D], ws_sb[:, i, m * P:(m + 1) * P],
                                        ctxT[:, i % 2, :, bass.ds(p * 4 + i // 2, NWIN, step=STRIDE)],
                                        start=False, stop=False)
                    if j == 31:
                        ins.then_inc(sem("ws_used"), 1)

            with pe.Fori(0, NQ - 1) as p:
                pair(p, False)
            pair(NQ - 1, True)
            for m in range(KT):
                ins = pe.matmul(bank[2 + m][:, 0:D], zeros[:, 0:P], zeros[:], start=False, stop=True)
            ins.then_inc(sem("sm_mm"), 1)
            turn_att(NQ)
            for i in range(4):
                attend(NQ, i)
            qawk, qawv, qaq = V("qawk", KT, D), V("qawv", KT, D), V("qaq", KT, P)
            pe.wait_ge(sem("v_in"), 16)
            pe.wait_ge(sem("smT_ready"), 2)
            for m in range(KT):
                for kt in range(KT):
                    ins = pe.matmul(bank[4 + m][:, 0:D], qawk[:, kt, m * P:(m + 1) * P], smT[:, kt, :],
                                    start=(kt == 0), stop=(kt == KT - 1))
                ins.then_inc(sem("qk_mm"), 1)
            for h in range(2):
                for kt in range(KT):
                    ins = pe.matmul(bank[3][:, h * D:(h + 1) * D], smT[:, kt, h * P:(h + 1) * P], qawv[:, kt, :],
                                    start=(kt == 0), stop=(kt == KT - 1))
                ins.then_inc(sem("qv_mm"), 1)
            pe.wait_ge(sem("qkT_ready"), 2)
            for kt in range(KT):
                ins = pe.matmul(bank[2][:, 0:D], qaq[:, kt, :], qkT[:, kt, :],
                                start=(kt == 0), stop=(kt == KT - 1))
            ins.then_inc(sem("ms_mm"), 1)
            ln_transpose(1, 1)
            for half in ("lnT0_ready", "lnT1_ready"):
                pe.wait_ge(sem(half), 2)
            pe.wait_ge(sem("v_in"), 16)
            qkv = V("qkv", KT, 3 * D)
            for k in range(KT):
                project(bank[4 + k][:], qkv, D + k * P).then_inc(sem("k_mm0"), 1)
                project(bank[6 + k][:], qkv, k * P).then_inc(sem("q_mm0"), 1)

            def values_proj(q):
                if q == 1:
                    pe.wait_ge(sem("mem_shift"), 1)
                if q == 2:
                    pe.wait_ge(sem("qv_ready"), 2)
                for b2 in range(2):
                    b = 2 * q + b2
                    for kt in range(KT):
                        for c in range(2):
                            ins = pe.matmul(bank[VB[q]][64 * c:64 * c + 64, b2 * D:(b2 + 1) * D],
                                            lnT[:, kt, b * S:(b + 1) * S], qkv[:, kt, 2 * D:3 * D],
                                            start=(kt == 0), stop=(kt == KT - 1))
                ins.then_inc(sem("v_mm0"), 1)

            def scores0(i):
                k, q = i // NQ, i % NQ
                if q == 0:
                    pe.wait_ge(sem("qT_ready0"), k + 1)
                    pe.wait_ge(sem("blk_ready0"), k + 1)
                if i == 1:
                    pe.wait_ge(sem("kT_ready0"), 2)
                if i == 2:
                    pe.wait_ge(sem("vblk_ready"), 2 * NQ)
                if i >= 3:
                    pe.wait_ge(sem("sc_shift"), i - 2)
                for b2 in range(2):
                    b = 2 * q + b2
                    ins = pe.matmul(bank[SC[i % 3]][64 * b2:64 * b2 + 64, :], qT[:, k, b * S:(b + 1) * S],
                                    blks[k][:, :, b * S:(b + 1) * S], start=True, stop=True)
                ins.then_inc(sem("sc_mm0"), 1)

            def turn0(i):
                pe.wait_ge(sem("sc_norm"), i + 1)
                if i == 0:
                    pe.wait_ge(sem("vblk_ready"), 2)
                else:
                    pe.wait_ge(sem("prT_ready"), i)
                for g in range(4):
                    ins = pe.transpose(bank[0][:, g * P:(g + 1) * P], pr[:, i % 3, g * P:(g + 1) * P], ident)
                ins.then_inc(sem("pr_tr"), 1)

            def values0(i):
                k, q = i // NQ, i % NQ
                pe.wait_ge(sem("prT_ready"), i + 1)
                if i == 0:
                    pe.wait_ge(sem("qT_ready0"), 2)
                    pe.wait_ge(sem("vblk_ready"), 2 * NQ)
                for b2 in range(2):
                    b = 2 * q + b2
                    for g in range(4):
                        ins = pe.matmul(bank[6 + k][32 * g:32 * g + 32, b * S:(b + 1) * S],
                                        vblk[:, b, 4 * k + g].rearrange("p c e -> p (c e)"),
                                        prT[:, i % 2, g * P + b2 * S:g * P + (b2 + 1) * S], start=True, stop=True)
                ins.then_inc(sem("pv_tile0"), 1)

            values_proj(0)
            scores0(0)
            values_proj(1)
            scores0(1)
            values_proj(2)
            values_proj(3)
            for i in range(2 * NQ):
                if i + 2 < 2 * NQ:
                    scores0(i + 2)
                turn0(i)
                if i >= 1:
                    values0(i - 1)
            values0(2 * NQ - 1)

            def out_proj(l, w):
                pe.wait_ge(sem(f"oT_ready{l}"), 2)
                for q in range(NQ):
                    for k in range(KT):
                        ins = pe.matmul(bank[2 * l + 4 - 4 * l + q // 2][:, (q % 2) * D:(q % 2 + 1) * D],
                                        oT[:, k, q * P:(q + 1) * P], w[:, k, :], start=(k == 0), stop=(k == KT - 1))
                    ins.then_inc(sem(f"o_mm{l}"), 1)
            pe.wait_ge(sem("mem_norm"), 1)
            for h in range(2):
                ins = pe.transpose(bank[3][:, h * P:(h + 1) * P],
                                   mpr[:, 4 * h:4 * h + 4, :].rearrange("p b n -> p (b n)"), ident)
            ins.then_inc(sem("mp_tr"), 1)
            out_proj(0, V("wo", KT, D))

            def route(l, k, n):
                ln_transpose(k, n)
                for half in ("lnT0_ready", "lnT1_ready"):
                    pe.wait_ge(sem(half), k + 1)
                g = V(f"gw{l}", KT, 32)
                for kt in range(KT):
                    for q in range(NQ):
                        ins = pe.matmul(bank[7][32 * q:32 * q + 32, 384:384 + P], g[:, kt, :],
                                        lnT[:, kt, q * P:(q + 1) * P], start=(kt == 0), stop=(kt == KT - 1),
                                        skip_group_check=True)
                ins.then_inc(sem("lg_mm"), 1)
                pe.wait_ge(sem("lgT_ready"), l + 1)
                pe.transpose(bank[5][:, 0:P], lgT[:], ident).then_inc(sem("lg_tr"), 1)
                if l == 0:
                    pe.wait_ge(sem("ptm_ready"), 1)
                    pe.wait_ge(sem("qv_ready"), 2)
                    for q in range(NQ):
                        ins = pe.matmul(bank[MB[q // 2]][:, (q % 2) * D:(q % 2 + 1) * D], ptm[:, q, :],
                                        qv[:, q // 2, :], start=True, stop=True)
                    ins.then_inc(sem("mem_mm"), 1)
                pe.wait_ge(sem("sel"), l + 1)
                pe.matmul(bank[7][:, 0:(NQ + 1) * E], C("tri"), sel[:].rearrange("p q e -> p (q e)"),
                          start=True, stop=False)
                for d in range(1, NQ + 1):
                    ins = pe.matmul(bank[7][:, d * E:(NQ + 1) * E], C("ones"),
                                    sel[:, 0:NQ + 1 - d, :].rearrange("p q e -> p (q e)"),
                                    start=False, stop=(d == NQ))
                ins.then_inc(sem("pos_mm"), 1)
                pe.wait_ge(sem("pick"), l + 1)
                for kt in range(KT):
                    for q in range(NQ):
                        ins = pe.matmul(bank[0][:, kt * P:(kt + 1) * P], ln[:, q, kt * P:(kt + 1) * P], pick[:, q, :],
                                        start=(q == 0 and kt == 0), stop=(q == NQ - 1), skip_group_check=True)
                ins.then_inc(sem(f"row_used{l}"), 1)

            def last_turn(l):
                pe.wait_ge(sem("lastw"), l + 1)
                for q in range(NQ):
                    ins = pe.transpose(bank[6][:, q * P:(q + 1) * P], lastw[:, q, :], ident)
                ins.then_inc(sem("last_tr"), 1)
                pe.wait_ge(sem("lastT_ready"), l + 1)

            def last_add(l):
                end = pe.value_load(meta[0:1, 2, E - 1:E], min_val=E, max_val=NT_MAX)
                pe.wait_ge(sem(f"y_evac{l}"), end + HEAD)
                for q in range(NQ):
                    pe.matmul(bank[1 + q // 2][:, (q % 2) * D:(q % 2 + 1) * D], lastT[:, q, :], yrow[:],
                              start=True, stop=True).then_inc(sem("last_mm"), 1)

            def memory_ms():
                pe.wait_ge(sem("mem_sq"), NQ)
                pe.matmul(bank[7][:, 256:256 + NQ], C("bmean"), ssq[:], start=True, stop=True)\
                  .then_inc(sem("mss_mm"), 1)

            route(0, 2, 2)
            pe.wait_ge(sem("mem_raw"), 2)
            last_turn(0)
            memory_ms()
            def rows_turn(l, n):
                pe.wait_ge(sem(f"row_in{l}"), n * 16)
                for kt in range(KT):
                    ins = pe.transpose(bank[0][:, kt * P:(kt + 1) * P], xrow[:, kt * P:(kt + 1) * P], ident)
                ins.then_inc(sem(f"row_used{l}"), 1)

            def ffn_loop(l, tile_body):
                pe.wait_ge(sem(f"meta{l}"), 1)
                with pe.Fori(0, 2) as half:
                    for s in range(SLOTS):
                        e = half * SLOTS + s
                        nt = pe.value_load(meta[0:1, 0, bass.ds(e, 1)], min_val=1, max_val=4)
                        first = pe.value_load(meta[0:1, 1, bass.ds(e, 1)], min_val=0, max_val=NT_MAX - 1)
                        with pe.Fori(0, nt) as t:
                            n = first + t
                            pe.wait_ge(sem(f"slot{s}_in"), half * 16 + 16 * (1 + 2 * l))
                            pe.wait_ge(sem(f"xT_done{l}"), HEAD + n + 1)
                            tile_body(s, n)

            def down(l, s, n, act_sb, w, K, done):
                rows_turn(l, n + 1)
                pe.wait_ge(sem(f"y_evac{l}"), HEAD + n)
                for k in range(K):
                    pe.wait_ge(sem(done), HEAD + n * K + (k + 1))
                    ins = pe.matmul(bank[7][:, 0:D], act_sb[:, k, :], w[:, k, :], start=(k == 0), stop=(k == K - 1))
                ins.then_inc(sem(f"y_mm{l}"), 1)

            def tile0(s, n):
                w1, w2, wg = E0(s, "w1", KT, F0), E0(s, "w2", KT, F0), E0(s, "wg", 4, F0)
                for m in range(4):
                    if m < 2:
                        pe.wait_ge(sem("z_done"), HEAD + n * 4)
                    else:
                        pe.wait_ge(sem("z_done"), HEAD + n * 4 + (m - 1))
                    for i, w in enumerate((w1, w2)):
                        for kt in range(KT):
                            ins = pe.matmul(bank[1 + 2 * i + m % 2][:, 0:P], w[:, kt, m * P:(m + 1) * P], xT[:, kt, :],
                                            start=(kt == 0), stop=(kt == KT - 1))
                    ins.then_inc(sem("x12_mm"), 1)
                pe.wait_ge(sem("s_done"), HEAD + n * 4)
                for k in range(4):
                    pe.wait_ge(sem("z_done"), HEAD + n * 4 + (k + 1))
                    for m in range(4):
                        ins = pe.matmul(bank[5 + m // 2][:, (m % 2) * P:(m % 2 + 1) * P],
                                        wg[:, k, m * P:(m + 1) * P], zT[:, k, :], start=(k == 0 and m % 2 == 0),
                                        stop=(k == 3), skip_group_check=True)
                        if k == 3 and m % 2 == 1:
                            ins.then_inc(sem("g_mm"), 1)
                down(0, s, n, sT, E0(s, "w3", 4, D), 4, "s_done")

            def tile1(s, n):
                w1 = E1(s, "w1", KT, F1)
                pe.wait_ge(sem("h_done"), HEAD + n * 8)
                for m in range(8):
                    for kt in range(KT):
                        ins = pe.matmul(bank[1 + m // 2][:, (m % 2) * P:(m % 2 + 1) * P], w1[:, kt, m * P:(m + 1) * P],
                                        xT[:, kt, :], start=(kt == 0), stop=(kt == KT - 1))
                    if m % 2 == 1:
                        ins.then_inc(sem("h_mm"), 1)
                down(1, s, n, hT, E1(s, "w2", 8, D), 8, "h_done")

            ffn_loop(0, tile0)
            last_add(0)
            pe.wait_ge(sem("h2_sq"), NQ)
            pe.matmul(bank[7][:, 192:192 + NQ], C("bmean"), ssq[:], start=True, stop=True).then_inc(sem("hss_mm"), 1)
            ln_transpose(3, 4)
            for half in ("lnT0_ready", "lnT1_ready"):
                pe.wait_ge(sem(half), 4)
            pe.wait_ge(sem("r_in"), 16)
            for k in range(KT):
                project(bank[4 + k][:], R("rk", KT, D), k * P).then_inc(sem("k_mm1"), 1)
            for k in range(KT):
                project(bank[2 + k][:], R("rq", KT, D), k * P).then_inc(sem("q_mm1"), 1)
            for q in range(NQ):
                for kt in range(KT):
                    ins = pe.matmul(bank[6 + q // 2][:, (q % 2) * D:(q % 2 + 1) * D], lnT[:, kt, q * P:(q + 1) * P],
                                    R("rv", KT, D)[:, kt, :], start=(kt == 0), stop=(kt == KT - 1))
                ins.then_inc(sem("v_mm1"), 1)

            def scores1(i):
                k, q = i // NQ, i % NQ
                if q == 0:
                    pe.wait_ge(sem("kT_ready1"), 2)
                    pe.wait_ge(sem("blk_ready1"), k + 1)
                if i >= 3:
                    pe.wait_ge(sem("sc_decay"), i - 2)
                for b2 in range(2):
                    b = 2 * q + b2
                    ins = pe.matmul(bank[SC[i % 3]][64 * b2:64 * b2 + 64, :], kT[:, k, b * S:(b + 1) * S],
                                    blk[:, :, b * S:(b + 1) * S], start=True, stop=True)
                ins.then_inc(sem("sc_mm1"), 1)

            def values1(i):
                k, q = i // NQ, i % NQ
                pe.wait_ge(sem("sc_decay"), i + 1)
                if i == 0:
                    pe.wait_ge(sem("vz_ready"), 2 * NQ)
                if q == 0 and k == 1:
                    pe.wait_ge(sem("o_evac1"), 2)
                for g in range(4):
                    for b2 in range(2):
                        for c in range(2):
                            h = 2 * g + c
                            ins = pe.matmul(bank[6 + b2][32 * g:32 * g + 32, q * S:(q + 1) * S],
                                            vz[64 * b2:64 * b2 + 64, q, HH * k + h, :],
                                            pr[64 * b2:64 * b2 + 64, i % 3, h * S:(h + 1) * S],
                                            start=(c == 0), stop=(c == 1))
                ins.then_inc(sem("pv_tile1"), 1)
            scores1(0)
            scores1(1)
            for i in range(2 * NQ):
                if i + 2 < 2 * NQ:
                    scores1(i + 2)
                values1(i)
            gm = C("gmean")
            pe.wait_ge(sem("gsum_ready"), 1)
            pe.matmul(bank[7][:, 256:272], gm, gstat[:].rearrange("p k b -> p (k b)"), start=True, stop=True)\
              .then_inc(sem("gm_mm"), 1)
            pe.wait_ge(sem("gsum_ready"), 2)
            pe.matmul(bank[7][:, 288:304], gm, gstat[:].rearrange("p k b -> p (k b)"), start=True, stop=True)\
              .then_inc(sem("gm_mm"), 1)
            out_proj(1, R("ro", KT, D))
            route(1, 4, 5)
            last_turn(1)
            ffn_loop(1, tile1)
            last_add(1)

        @block.vector
        def _(dve):
            chained = [0]

            def link(ins):
                chained[0] += 1
                ins.then_inc(sem("dve_chain"), 1)
                dve.wait_ge(sem("dve_chain"), chained[0])

            def layer_norm(k, n, ready=None, meanwhile=None):
                for q in range(NQ):
                    if ready is not None:
                        ready(q)
                    ins = dve.bn_stats(bn[:, q, :], x[:, q, :])
                link(ins)
                for q in range(NQ):
                    ins = dve.bn_aggr(mv[:, q, :], bn[:, q, :])
                link(ins)
                dve.tensor_scalar(veps[:], mv[:, :, 1], LN_EPS, None, ALU.add).then_inc(sem("var_ready"), 1)
                if meanwhile is not None:
                    meanwhile()
                dve.wait_ge(sem("rstd_ready"), k + 1)
                for q in range(NQ):
                    dve.tensor_scalar(ln[:, q, :], x[:, q, :], mv[:, q, 0:1], rstd[:, q:q + 1], ALU.subtract,
                                      ALU.mult).then_inc(sem("ln_ready"), 1)

            def lnT_half(k):
                dve.wait_ge(sem("tr_ready"), k + 1)
                dve.tensor_copy(lnT[:, 1, :], bank[1][:]).then_inc(sem("lnT1_ready"), 1)

            for name in ("h_filled", "dots_ready", "z_done", "xT_done0", "xT_done1", "y_evac0", "y_evac1"):
                dve.sem_inc(sem(name), HEAD)
            dve.memset(sel[:, NQ, :], 0.0)
            link(dve.memset(wz[:], 0.0))
            dve.wait_ge(sem("x_in"), 16)
            layer_norm(0, 0)
            dve.wait_ge(sem("w_in"), 16)
            dve.tensor_copy(wz[:, :, 31], W("wvec")).then_inc(sem("wz_ready"), 1)
            lnT_half(0)
            dve.memset(negm[:, 0, :], 0.0).then_inc(sem("negm_ready"), 1)
            dve.memset(hmx[:], 0.0).then_inc(sem("slot_free"), SLOTS)
            dve.wait_ge(sem("feat_ready"), 2)
            dve.wait_ge(sem("rho_open"), 1)

            def masked_scores(row, n):
                dve.wait_ge(sem("negm_ready"), n + 1)
                dve.tensor_tensor(rho[:], bank[0][:, 0:T], negm[:, row, :].rearrange("p o t -> p (o t)"), ALU.add)\
                   .then_inc(sem("rho_evac"), 1)

            def max_scores(n):
                dve.wait_ge(sem("rho_evac"), n + 1)
                dve.tensor_reduce(nmax[:], rho[:], AX_X, ALU.max, negate=True).then_inc(sem("nmax_ready"), 1)

            def att_evac(n):
                dve.wait_ge(sem("att_tr"), n + 1)
                for b2 in range(2):
                    cols = slice(S * b2, S * b2 + S)
                    ins = dve.tensor_copy(attT[:, :, b2, cols], bank[6][:, 0:2 * P].rearrange("p (h f) -> p h f", h=2)[:, :, cols])
                ins.then_inc(sem("attT_ready"), 1)

            def context_dots(n):
                dve.wait_ge(sem("txth_mm"), n + 1)
                dve.wait_ge(sem("dots_ready"), HEAD + 3 * n)
                for c, w in enumerate(("wcw", "wcb")):
                    dve.tensor_tensor_reduce(out=junk[:, c * D:(c + 1) * D], in0=bank[7][:, 0:D], in1=V(w),
                                             scale=1.0, scalar=0.0, op0=ALU.mult, op1=ALU.add,
                                             accum_out=dot[:, c:c + 1]).then_inc(sem("dots_ready"), 1)

            def keep_dots(n):
                dve.wait_ge(sem("dots_ready"), HEAD + 3 * n + 2)
                row = slice(n, n + 1) if isinstance(n, int) else bass.ds(n, 1)
                dve.tensor_copy(dots[:, row, :].rearrange("p o c -> p (o c)"), dot[:]).then_inc(sem("dots_ready"), 1)

            with dve.Fori(0, NQ) as p:
                dve.wait_ge(sem("h_filled"), HEAD + p * 32)
                dve.wait_ge(sem("h_filled3"), HEAD + p * 32)
                dve.tensor_copy(fts[:], featT[:, :, bass.ds(p * P, P)]).then_inc(sem("staged"), 1)
                dve.wait_ge(sem("txt_mm"), p * 2 + 2)
                for k in range(KT):
                    dve.tensor_copy(txs[:, k].rearrange("p b t -> p (b t)"), bank[4 + k][:]).then_inc(sem("staged"), 1)
                dve.wait_ge(sem("staged"), p * 3 + 3)
                for j in range(32):
                    dve.wait_ge(sem("slot_free"), p * 32 + (j + 1))
                    if j == SLOTS - 1:
                        masked_scores(bass.ds(p, 1), p)
                    if j == 12:
                        dve.wait_ge(sem("mask_in"), 16)
                        row = bass.ds(p + 1, 1)
                        dve.tensor_scalar(negm[:, row, :].rearrange("p o t -> p (o t)"),
                                          negm[:, row, :].rearrange("p o t -> p (o t)").bitcast(I32), -NEG, NEG,
                                          ALU.mult, ALU.add).then_inc(sem("negm_ready"), 1)
                    if j == 5:
                        max_scores(p)
                    if j == 14:
                        att_evac(p)
                    if j == 28:
                        dve.wait_ge(sem("v_in"), 16)
                        context_dots(p)
                    if j == 30:
                        keep_dots(p)
                    for g in range(3):
                        for k in range(KT):
                            ins = dve.tensor_scalar(hbuf[:, j % SLOTS, g, k, :], txs[:, k, g // 2, :],
                                                    fts[:, k, 32 * g + j:32 * g + j + 1], None, ALU.add)
                    ins.then_inc(sem("h_filled"), 1)
            dve.wait_ge(sem("slot_free"), NQ * 32 + SLOTS)
            masked_scores(slice(NQ, NQ + 1), NQ)
            max_scores(NQ)
            dve.wait_ge(sem("att_exp"), NQ + 1)
            dve.reciprocal(rinv[:], rsum[:, 1:]).then_inc(sem("rinv_ready"), 1)
            att_evac(NQ)
            context_dots(NQ)
            keep_dots(NQ)
            dve.wait_ge(sem("rinv_ready"), 1)
            dve.wait_ge(sem("dots_ready"), HEAD + 3 * (NQ + 1))
            dve.tensor_tensor(wbpre[:], dots[:, 1:, :], bc(rinv[:], 2, 2), ALU.mult).then_inc(sem("wbpre_ready"), 1)
            dve.wait_ge(sem("wbs_ready"), 2)
            for q in range(NQ):
                ins = dve.scalar_tensor_tensor(out=x[:, q, :], in0=ln[:, q, :], scalar=wbs[:, 0, q:q + 1],
                                               in1=x[:, q, :], op0=ALU.mult, op1=ALU.add)
            link(ins)
            for q in range(NQ):
                dve.tensor_scalar(x[:, q, :], x[:, q, :], wbs[:, 1, q:q + 1], None, ALU.add)\
                   .then_inc(sem("x1_ready"), 1)
            dve.wait_ge(sem("x1_ready"), NQ)
            layer_norm(1, 1)
            lnT_half(1)
            dve.wait_ge(sem("ms_mm"), 1)
            ms = bank[2][:, 0:D].rearrange("p (b n) -> p b n", b=B)
            link(dve.tensor_reduce(mmx[:], ms, AX_X, ALU.max))
            dve.tensor_tensor(mpr[:], ms, bc(mmx[:], 2, NWIN), ALU.subtract).then_inc(sem("mem_shift"), 1)

            def masked(l, srcT):
                def one(k):
                    dst = blks[k] if l == 0 else blk
                    if k and l == 1:
                        dve.wait_ge(sem("sc_mm1"), NQ)
                    for h in range(HH):
                        ins = dve.tensor_scalar(dst[:, h, :], srcT[:, k, :], C("hmask")[:, h:h + 1], None, ALU.mult)
                    ins.then_inc(sem(f"blk_ready{l}"), 1)
                return one

            dve.wait_ge(sem("kT_ready0"), 1)
            mask0 = masked(0, kT)
            mask0(0)
            for k in range(KT):
                dve.wait_ge(sem("q_mm0"), k + 1)
                dve.tensor_scalar(qT[:, k, :], bank[6 + k][:], V("bqkv")[:, k:k + 1], float(HD) ** -0.5, ALU.add,
                                  ALU.mult).then_inc(sem("qT_ready0"), 1)
            dve.wait_ge(sem("mem_exp"), 1)
            link(dve.tensor_reduce(msum[:], mpr[:], AX_X, ALU.add))
            link(dve.reciprocal(mmx[:], msum[:]))
            dve.tensor_tensor(mpr[:], mpr[:], bc(mmx[:], 2, NWIN), ALU.mult).then_inc(sem("mem_norm"), 1)
            def shift0(i):
                dve.wait_ge(sem("sc_mm0"), i + 1)
                sc = bank[SC[i % 3]][:].rearrange("p (h m) -> p h m", h=HH)
                link(dve.tensor_reduce(hmx[:, i % 2, :], sc, AX_X, ALU.max))
                if i >= 3:
                    dve.wait_ge(sem("pr_tr"), i - 2)
                dve.tensor_tensor(pr[:, i % 3, :].rearrange("p (h m) -> p h m", h=HH), sc,
                                  bc(hmx[:, i % 2, :], 2, S), ALU.subtract).then_inc(sem("sc_shift"), 1)

            def norm0(i):
                dve.wait_ge(sem("sc_exp"), i + 1)
                v = pr[:, i % 3, :].rearrange("p (h m) -> p h m", h=HH)
                link(dve.tensor_reduce(hsum[:, i % 2, :], v, AX_X, ALU.add))
                if i >= 2:
                    dve.wait_ge(sem("sc_norm"), i - 1)
                dve.reciprocal(hinv[:, i % 2, :], hsum[:, i % 2, :]).then_inc(sem("sc_inv"), 1)

            shift0(0)
            for i in range(1, 2 * NQ):
                shift0(i)
                norm0(i - 1)
                if i == 1:
                    dve.wait_ge(sem("kT_ready0"), 2)
                    mask0(1)
            norm0(2 * NQ - 1)

            def add_out(l, bias, n):
                if bias is not None:
                    for q in range(NQ):
                        ins = dve.tensor_tensor(x[:, q, :], x[:, q, :], bias, ALU.add)
                    link(ins)
                for q in range(NQ):
                    dve.wait_ge(sem(f"o_mm{l}"), 2 * (q // 2) + 2)
                    ins = dve.tensor_tensor(x[:, q, :], bank[4 - 2 * l + q // 2][:, (q % 2) * D:(q % 2 + 1) * D],
                                            x[:, q, :], ALU.add)
                link(ins)
            add_out(0, V("bo"), 0)

            def route(l, k, n, kt_, meanwhile=None):
                layer_norm(k, n, None, meanwhile)
                lnT_half(kt_)
                dve.wait_ge(sem("lg_mm"), l + 1)
                dve.tensor_copy(lgT[:], bank[7][:, 384:384 + P]).then_inc(sem("lgT_ready"), 1)
                dve.wait_ge(sem("lg_tr"), l + 1)
                lg_ps = bank[5][:, 0:P].rearrange("p (q e) -> p q e", q=NQ)[:, :, 0:E]
                if l == 0:
                    link(dve.tensor_tensor(lg[:], lg_ps, bc(V("gb0"), 1, NQ), ALU.add))
                else:
                    link(dve.tensor_copy(lg[:], lg_ps))
                for q in range(NQ):
                    ins = dve.max(top[:, q, :], lg[:, q, :])
                link(ins)
                for q in range(NQ):
                    ins = dve.max_index(topi[:, q, :], top[:, q, :], lg[:, q, :])
                link(ins)
                dve.tensor_tensor(gd[:], top[:, :, 1], top[:, :, 0], ALU.subtract).then_inc(sem("gd_ready"), 1)
                link(dve.tensor_copy(topf[:], topi[:, :, 0:2]))
                iota = bc(bc(C("iota")[:, 0:E], 1, 2), 1, NQ)
                link(dve.tensor_tensor(oh[:], iota, bc(topf[:], 3, E), ALU.is_equal))
                dve.tensor_tensor(sel[:, 0:NQ], oh[:, :, 0, :], oh[:, :, 1, :], ALU.add).then_inc(sem("sel"), 1)
                dve.wait_ge(sem("ge_ready"), l + 1)
                link(dve.tensor_scalar(gden[:], ge[:], 1.0, None, ALU.add))
                link(dve.reciprocal(gw[:, :, 0], gden[:]))
                link(dve.tensor_tensor(gw[:, :, 1], ge[:], gw[:, :, 0], ALU.mult))
                dve.wait_ge(sem("pos_mm"), l + 1)
                cnt = bank[7][:, NQ * E:(NQ + 1) * E]
                link(dve.tensor_scalar(ntf[:, 0, :], cnt, float(P), 1.0, ALU.is_gt, ALU.add))
                for t in (2, 3):
                    link(dve.scalar_tensor_tensor(out=ntf[:, 0, :], in0=cnt, scalar=float(t * P), in1=ntf[:, 0, :],
                                                  op0=ALU.is_gt, op1=ALU.add))
                link(dve.tensor_tensor_scan(ntf[:, 2, :], C("ones")[:, 0:E], ntf[:, 0, :], 0.0, ALU.mult, ALU.add))
                link(dve.tensor_tensor(ntf[:, 1, :], ntf[:, 2, :], ntf[:, 0, :], ALU.subtract))
                pos = bank[7][:, 0:NQ * E].rearrange("p (q e) -> p q e", q=NQ)
                link(dve.scalar_tensor_tensor(out=rowf[:], in0=bc(ntf[:, 1, :], 1, NQ), scalar=float(P), in1=pos,
                                              op0=ALU.mult, op1=ALU.add))
                link(dve.tensor_tensor(ohr[:], oh[:], bc(rowf[:], 2, 2), ALU.mult))
                link(dve.tensor_reduce(ridf[:], ohr[:], AX_X, ALU.add))
                dve.tensor_scalar(rid[:], ridf[:].rearrange("p q k -> p (q k)"), float(P), None, ALU.add)\
                   .then_inc(sem("rid"), 1)
                dve.tensor_copy(meta[:], ntf[:]).then_inc(sem(f"meta{l}"), 1)
                for q in range(NQ):
                    ins = dve.tensor_scalar(pick[:, q, :], C("iota"), ridf[:, q, 0:1], None, ALU.is_equal)
                link(ins)
                for q in range(NQ):
                    ins = dve.scalar_tensor_tensor(out=pick[:, q, :], in0=C("iota"), scalar=ridf[:, q, 1:2],
                                                   in1=pick[:, q, :], op0=ALU.is_equal, op1=ALU.add)
                ins.then_inc(sem("pick"), 1)
                dve.tensor_scalar(loff[:], ntf[:, 2, E - 1:E], -float(P), float(P), ALU.mult, ALU.add)
                link(dve.tensor_tensor(lwt[:], oh[:, :, :, E - 1], gw[:], ALU.mult))
                dve.tensor_scalar(lrow[:], rowf[:, :, E - 1], loff[:], None, ALU.add)
                link(dve.tensor_tensor(lsum[:], lwt[:, :, 0], lwt[:, :, 1], ALU.add))
                for q in range(NQ):
                    ins = dve.tensor_scalar(lastw[:, q, :], C("iota"), lrow[:, q:q + 1], lsum[:, q:q + 1],
                                            ALU.is_equal, ALU.mult)
                ins.then_inc(sem("lastw"), 1)
            def memory_masked():
                dve.wait_ge(sem("mp_tr"), 1)
                pmask = C("pmask", 2, P)
                for q in range(NQ):
                    h = q // 2
                    ins = dve.tensor_tensor(ptm[:, q, :], bank[3][:, h * P:(h + 1) * P], pmask[:, q % 2, :], ALU.mult)
                ins.then_inc(sem("ptm_ready"), 1)

            route(0, 2, 2, 2, memory_masked)

            dve.wait_ge(sem("mss_mm"), 1)
            dve.tensor_scalar(veps[:], bank[7][:, 256:256 + NQ], RMS_EPS, None, ALU.add).then_inc(sem("var_ready"), 1)

            def rows_copy(l, n):
                dve.wait_ge(sem(f"row_used{l}"), n + 1)
                dve.tensor_copy(xT[:].rearrange("p k t -> p (k t)"), bank[0][:, 0:KT * P])\
                   .then_inc(sem(f"xT_done{l}"), 1)

            def ffn_loop(l, tile_body, b_of):
                dve.wait_ge(sem(f"meta{l}"), 1)
                rows_copy(l, 0)
                with dve.Fori(0, 2) as half:
                    for s in range(SLOTS):
                        e = half * SLOTS + s
                        nt = dve.value_load(meta[0:1, 0, bass.ds(e, 1)], min_val=1, max_val=4)
                        first = dve.value_load(meta[0:1, 1, bass.ds(e, 1)], min_val=0, max_val=NT_MAX - 1)
                        with dve.Fori(0, nt) as t:
                            n = first + t
                            tile_body(s, n)
                            rows_copy(l, n + 1)
                            dve.wait_ge(sem(f"y_mm{l}"), HEAD + n + 1)
                            dve.wait_ge(sem(f"y_stored{l}"), n * 16 + 16)
                            dve.tensor_tensor(yrow[:], bank[7][:, 0:D], b_of(s), ALU.add).then_inc(sem(f"y_evac{l}"), 1)

            def tile0(s, n):
                dve.wait_ge(sem("g_mm"), HEAD + n * 2)
                for m in range(4):
                    dve.wait_ge(sem("x12_mm"), n * 4 + (m + 1))
                    dve.tensor_scalar(hT[:, m, :], bank[1 + m % 2][:, 0:P], E0(s, "b1")[:, m:m + 1], None, ALU.add)\
                       .then_inc(sem("x1_done"), 1)
                    dve.wait_ge(sem("x1_done"), n * 4 + (m + 1))
                    dve.scalar_tensor_tensor(out=zT[:, m, :], in0=bank[3 + m % 2][:, 0:P],
                                             scalar=E0(s, "b2")[:, m:m + 1], in1=hT[:, m, :], op0=ALU.add,
                                             op1=ALU.mult).then_inc(sem("z_done"), 1)

            ffn_loop(0, tile0, lambda s: E0(s, "b3"))

            def combine(l, q):
                dve.wait_ge(sem(f"gathered{q}"), 32 * (l + 1))
                for c in range(2):
                    link(dve.scalar_tensor_tensor(out=x[:, q, :], in0=yk[:, q, c, :], scalar=gw[:, q, c:c + 1],
                                                  in1=x[:, q, :], op0=ALU.mult, op1=ALU.add))
                dve.wait_ge(sem("last_mm"), NQ * l + 2 * (q // 2) + 2)
                ins = dve.tensor_tensor(x[:, q, :], x[:, q, :], bank[1 + q // 2][:, (q % 2) * D:(q % 2 + 1) * D],
                                        ALU.add)
                if l == 1:
                    ins.then_inc(sem("x_done"), 1)
                else:
                    link(ins)
            dve.wait_ge(sem("rstd_ready"), 4)
            dve.wait_ge(sem("mem_raw"), 2)
            for q in range(NQ):
                ins = dve.scalar_tensor_tensor(out=memn[:, q, :], in0=memn[:, q, :], scalar=rinv[:, q:q + 1],
                                               in1=V("mnw"), op0=ALU.mult, op1=ALU.mult)
            ins.then_inc(sem("memn_ready"), 1)
            layer_norm(4, 3, lambda q: combine(0, q))
            dve.wait_ge(sem("ln_ready"), 16)
            dve.wait_ge(sem("memn_ready"), 1)
            for q in range(NQ):
                dve.tensor_tensor(ln[:, q, :], ln[:, q, :], memn[:, q, :], ALU.add).then_inc(sem("h2_ready"), 1)
            dve.wait_ge(sem("hss_mm"), 1)
            dve.tensor_scalar(veps[:], bank[7][:, 192:192 + NQ], RMS_EPS, None, ALU.add).then_inc(sem("var_ready"), 1)
            dve.wait_ge(sem("rstd_ready"), 6)
            for q in range(NQ):
                ins = dve.scalar_tensor_tensor(out=tmp[:, q, :], in0=ln[:, q, :], scalar=rinv[:, q:q + 1],
                                               in1=V("hnw"), op0=ALU.mult, op1=ALU.mult)
            link(ins)
            for q in range(NQ):
                dve.tensor_tensor(x[:, q, :], x[:, q, :], tmp[:, q, :], ALU.add).then_inc(sem("x_ready"), 1)
            dve.wait_ge(sem("x_ready"), 4)
            layer_norm(6, 4)
            lnT_half(3)
            for k in range(KT):
                dve.wait_ge(sem("q_mm1"), k + 1)
                ins = dve.tensor_copy(qT[:, k, :], bank[2 + k][:])
            link(ins)
            mask1 = masked(1, qT)
            mask1(0)

            def decay(i):
                k = i // NQ
                dve.wait_ge(sem("sc_mm1"), i + 1)
                if i >= 3:
                    dve.wait_ge(sem("pv_tile1"), i - 2)
                dve.tensor_tensor(pr[:, i % 3, :], bank[SC[i % 3]][:], C("decay", KT, HH * S)[:, k, :], ALU.mult)\
                   .then_inc(sem("sc_decay"), 1)

            def evac_o1(k):
                dve.wait_ge(sem("pv_tile1"), NQ * (k + 1))
                for b2 in range(2):
                    dst = oT[:, k, :].rearrange("p (q b s) -> p q b s", q=NQ, b=2)[:, :, b2, :]
                    dve.tensor_copy(dst, bank[6 + b2][:, 0:NQ * S].rearrange("p (q s) -> p q s", q=NQ))\
                       .then_inc(sem("o_evac1"), 1)
            for i in range(2 * NQ):
                if i == NQ:
                    mask1(1)
                decay(i)
                if i == NQ:
                    evac_o1(0)
            evac_o1(1)
            dve.wait_ge(sem("o_evac1"), 4)
            o4 = oT[:].rearrange("p k (b s) -> p (k b) s", b=B)
            dve.tensor_reduce(gstat[:].rearrange("p k b -> p (k b)"), o4, AX_X, ALU.add).then_inc(sem("gsum_ready"), 1)
            dve.wait_ge(sem("gm_mm"), 1)
            link(dve.tensor_tensor(o4, o4, bc(bank[7][:, 256:272], 2, S), ALU.subtract))
            sq = tmp.rearrange("p q d -> p (q d)").rearrange("p (n s) -> p n s", s=S)
            link(dve.tensor_tensor(sq, o4, o4, ALU.mult))
            dve.tensor_reduce(gstat[:].rearrange("p k b -> p (k b)"), sq, AX_X, ALU.add).then_inc(sem("gsum_ready"), 1)
            dve.wait_ge(sem("gm_mm"), 2)
            dve.tensor_scalar(gvar[:].rearrange("p k b -> p (k b)"), bank[7][:, 288:304], GN_EPS, None, ALU.add)\
               .then_inc(sem("var_ready"), 1)
            dve.wait_ge(sem("rstd_ready"), 8)
            link(dve.tensor_tensor(gsc[:], grs[:], bc(V("gnw"), 2, B), ALU.mult))
            link(dve.tensor_tensor(o4, o4, bc(gsc[:].rearrange("p k b -> p (k b)"), 2, S), ALU.mult))
            for k in range(KT):
                dve.tensor_scalar(oT[:, k, :], oT[:, k, :], V("gnb")[:, k:k + 1], None, ALU.add)\
                   .then_inc(sem("oT_ready1"), 1)
            add_out(1, None, 1)
            route(1, 8, 5, 4)
            ffn_loop(1, lambda s, n: None, lambda s: E1(s, "b2"))
            for q in range(NQ):
                combine(1, q)


def _view(t, at, dims):
    a, n = at
    v = t[:, a:a + n]
    if not dims:
        return v
    if len(dims) == 2:
        return v.rearrange("p (a b) -> p a b", a=dims[0])
    return v.rearrange("p (a b c) -> p a b c", a=dims[0], b=dims[1])


def _evac_prT(act, sem, prT, bank, i):
    act.wait_ge(sem("pr_tr"), i + 1)
    if i >= 2:
        act.wait_ge(sem("pv_tile0"), i - 1)
    act.activation(prT[:, i % 2, :], bank[0][:], ACT.Copy).then_inc(sem("prT_ready"), 1)


def kernel(**inputs):
    import concourse.bacc as _bacc
    from concourse.bass_utils import run_bass_kernel_spmd as _run

    arrays = layout({k: np.asarray(v) for k, v in inputs.items()})
    nc = _bacc.Bacc("TRN2", target_bir_lowering=False, num_devices=1)
    args = [nc.dram_tensor(n, a.shape, mybir.dt.from_np(a.dtype), kind="ExternalInput").ap()
            for n, a in arrays.items()]
    out = nc.dram_tensor("out_dram", (TOK, D), F32, kind="ExternalOutput").ap()
    perceiver(nc, *args, out)
    r = _run(nc, [arrays], core_ids=[0])
    return r.results[0]["out_dram"].reshape(B, S, D)


def layout(i):
    def rows(w):
        k = w.shape[0] // P
        return w.reshape(k, P, -1).transpose(1, 0, 2).reshape(P, -1)

    def col(v):
        return v.reshape(-1, P).T

    def wide(v):
        return np.broadcast_to(v.reshape(1, -1), (P, v.size))

    def pack(parts, cols):
        a = np.concatenate([parts[n] for n in cols], axis=-1)
        return np.ascontiguousarray(a)

    ar = np.arange(P)
    l, m = np.arange(S)[None, :], np.arange(S)[:, None]
    gam = np.array([1.0 - 2.0 ** (-5 - (8 * h) // H) for h in range(H)], np.float32)
    power = np.where(l >= m, gam[:, None, None] ** np.maximum(l - m, 0).astype(np.float32), 0).astype(np.float32)
    power = power * np.float32(HD ** -0.5)
    decay = np.tile(power.transpose(1, 0, 2).reshape(S, -1), (2, 1))
    f = np.float32
    consts = dict(
        tri=(ar[:, None] < ar[None, :]).astype(f), ones=np.ones((P, P), f),
        gmean=(ar[:, None] // HD == ar[None, :] // HD).astype(f) / f(HD * S),
        bmean=(ar[:, None] // S == ar[None, :] // S).astype(f) / f(S * D),
        pmask=np.concatenate([(ar[:, None] // NWIN == 2 * c + ar[None, :] // S).astype(f) for c in range(2)], 1),
        hmask=(ar[:, None] // HD == np.arange(HH)[None, :]).astype(f), decay=decay.astype(f),
        iota=np.tile(np.arange(P, dtype=f), (P, 1)))
    w = dict(Ws=rows(i["L0_xattn_Ws"]), W=rows(i["L0_xattn_W"]), wvec=col(i["L0_xattn_w"]), bvec=col(i["L0_xattn_b"]),
             ident=np.eye(P, dtype=f))
    gate = lambda a: np.pad(a, ((0, 0), (0, 32 - E)))
    heads = lambda a: rows(a.transpose(1, 0, 2).reshape(D, D))
    v = dict(
        qkv=rows(i["L0_attn_W_qkv"].T), wo=rows(i["L0_attn_W_out"].T), bqkv=col(i["L0_attn_b_qkv"]),
        wcw=wide(i["L0_xattn_Wcw"]), wcb=wide(i["L0_xattn_Wcb"]), bcw=wide(i["L0_xattn_bcw"]),
        bcb=wide(i["L0_xattn_bcb"]), bo=wide(i["L0_attn_b_out"]),
        gw0=rows(gate(i["L0_ffn_gate_w"])), gb0=wide(i["L0_ffn_gate_b"]), gw1=rows(gate(i["L1_ffn_w_gate"])),
        qawk=rows(i["L1_xattn_qa_wk"].T), qawv=rows(i["L1_xattn_qa_wv"].T), qaq=rows(np.tile(i["L1_xattn_qa_q"].T, (1, 2))),
        mnw=np.tile(i["L1_xattn_mn_w"], (2, 1)), hnw=np.tile(i["L1_xattn_hn_w"], (2, 1)),
        gnw=col(i["L1_attn_gn_weight"]), gnb=col(i["L1_attn_gn_bias"]))

    r = dict(rq=heads(i["L1_attn_Wq"]), rk=heads(i["L1_attn_Wk"]), rv=heads(i["L1_attn_Wv"]),
             ro=rows(i["L1_attn_Wout"]))

    def erows(a):
        return np.stack([rows(a[e]) for e in range(E)])

    def ecol(a):
        return np.stack([col(a[e]) for e in range(E)])

    def ewide(a):
        return np.stack([wide(a[e]) for e in range(E)])

    e0 = dict(w1=erows(i["L0_ffn_w1"]), w2=erows(i["L0_ffn_w2"]), wg=erows(i["L0_ffn_wg"]), w3=erows(i["L0_ffn_w3"]),
              b1=ecol(i["L0_ffn_b1"]), b2=ecol(i["L0_ffn_b2"]), bg=ecol(i["L0_ffn_bg"]), b3=ewide(i["L0_ffn_b3"]))
    e1 = dict(w1=erows(i["L1_ffn_w1"]), w2=erows(i["L1_ffn_w2"]), b1=ecol(i["L1_ffn_b1"]), b2=ewide(i["L1_ffn_b2"]))
    c = i["ctx_1024"]
    ws = i["L1_xattn_ws_w"].T.reshape(NQ, 8, P, D).transpose(0, 2, 1, 3)
    mask = np.repeat(i["mask_BxS2_ik0"], S, axis=0).reshape(NQ, P, T).transpose(1, 0, 2)
    return dict(
        x_in=np.ascontiguousarray(i["x"].reshape(TOK, D)),
        ctx_rows=np.ascontiguousarray(c.reshape(B, 2, P, D).transpose(2, 0, 1, 3)),
        ctx_cols=np.ascontiguousarray(c.transpose(2, 0, 1).reshape(KT, P, B, T).transpose(1, 0, 2, 3)),
        mask_in=np.ascontiguousarray(mask), w_in=pack(w, W_COLS), c_in=pack(consts, C_COLS), v_in=pack(v, V_COLS), r_in=pack(r, R_COLS),
        ws_in=np.ascontiguousarray(ws), e0_in=pack(e0, E0_COLS), e1_in=pack(e1, E1_COLS))
```

```python
from contextlib import ExitStack

import numpy as np
import concourse.bass as bass
from concourse import mybir

F32 = mybir.dt.float32
I32 = mybir.dt.int32
U32 = mybir.dt.uint32
ALU = mybir.AluOpType
ACT = mybir.ActivationFunctionType
AX_X = mybir.AxisListType.X
P = 128

B, S, D, T = 8, 64, 256, 256
TOK = B * S
NQ = TOK // P
KT = D // P
H, HD = 16, D // 16
HH = H // KT
STRIDE, WIN = 8, 16
NWIN = T // STRIDE
TPAD = T + STRIDE
E = 8
F0 = 512
F1 = 1024
NT_MAX = 15
NEG = -1e30
NT_ROWS = NT_MAX + 5
LN_EPS, GN_EPS, RMS_EPS = 1e-5, 1e-5, 1.1920929e-07
HEAD = 1
SLOTS = 4
ROWS_AHEAD = 8

W_COLS = dict(W=KT * D, Ws=KT * D, wvec=KT, bvec=KT, ident=P)
C_COLS = dict(tri=P, ones=P, gmean=P, bmean=P, pmask=2 * P, hmask=HH, decay=KT * HH * S,
              iota=P)
V_COLS = dict(qkv=KT * 3 * D, wo=KT * D, bqkv=6, wcw=D, wcb=D, bcw=1, bcb=1, bo=D,
              gw0=KT * 32, gb0=E, gw1=KT * 32, qawk=KT * D, qawv=KT * D, qaq=KT * P, mnw=D, hnw=D,
              gnw=KT, gnb=KT)
R_COLS = dict(rq=KT * D, rk=KT * D, rv=KT * D, ro=KT * D)
E0_COLS = dict(w1=KT * F0, w2=KT * F0, wg=4 * F0, w3=4 * D, b1=4, b2=4, bg=4, b3=D)
E1_COLS = dict(w1=KT * F1, w2=8 * D, b1=8, b2=D)


def offsets(cols):
    at, out = 0, {}
    for name, n in cols.items():
        out[name] = (at, n)
        at += n
    return out, at


W_AT, W_N = offsets(W_COLS)
C_AT, C_N = offsets(C_COLS)
V_AT, V_N = offsets(V_COLS)
R_AT, R_N = offsets(R_COLS)
E0_AT, E0_N = offsets(E0_COLS)
E1_AT, E1_N = offsets(E1_COLS)


def perceiver(nc, x_in, ctx_rows, ctx_cols, mask_in, w_in, c_in, v_in, r_in, ws_in, e0_in, e1_in, out):
    with ExitStack() as ctx:
        def sb(name, shape, dt=F32):
            return ctx.enter_context(nc.sbuf_tensor(name, shape, dt))

        sems = {}

        def sem(name):
            if name not in sems:
                sems[name] = ctx.enter_context(nc.semaphore(name))
            return sems[name]

        bank = [ctx.enter_context(nc.psum_tensor(f"bank{i}", [P, 512], F32)) for i in range(8)]

        xg = [nc.dram_tensor(f"expert_rows{l}", [NT_ROWS * P, D], F32).ap() for l in range(2)]
        yg = [nc.dram_tensor(f"expert_out{l}", [NT_ROWS * P, D], F32).ap() for l in range(2)]

        w_sb = sb("w_sb", [P, W_N])
        c_sb = sb("c_sb", [P, C_N])
        v_sb = sb("v_sb", [P, V_N])

        def W(name, *dims):
            return _view(w_sb, W_AT[name], dims)

        def C(name, *dims):
            return _view(c_sb, C_AT[name], dims)

        def V(name, *dims):
            return _view(v_sb, V_AT[name], dims)

        def R(name, *dims):
            return _view(v_sb, R_AT[name], dims)

        x = sb("x", [P, NQ, D])
        ln = sb("ln", [P, NQ, D])
        lnT = sb("lnT", [P, KT, TOK])
        bn = sb("bn", [P, NQ, 6])
        mv = sb("mv", [P, NQ, 2])
        veps = sb("veps", [P, NQ])
        mhalf = sb("mhalf", [P, 16])
        token = sb("token", [P, 1])
        rstd = sb("rstd", [P, NQ])
        zeros = sb("zeros", [P, D])
        memn = sb("memn", [P, NQ, D])

        arena_a = sb("arena_a", [P, 2 * E0_N + NQ * D])
        tmp = arena_a[:, 2 * E0_N:2 * E0_N + NQ * D].rearrange("p (q d) -> p q d", q=NQ)
        arena_s = sb("arena_s", [P, 2 * E0_N])
        pairs_h = [t[:, i * 4096:(i + 1) * 4096].rearrange("p (u g k t) -> p u g k t", u=2, g=4, k=KT)
                   for t in (arena_a, arena_s) for i in range(2)]

        def hbuf(j):
            return pairs_h[j % ROWS_AHEAD // 2][:, j % 2]

        slot = [arena_s[:, 0:E0_N], arena_s[:, E0_N:2 * E0_N],
                arena_a[:, 0:E0_N], arena_a[:, E0_N:2 * E0_N]]

        arena_b = sb("arena_b", [P, 11264])
        at = [0]

        def carve(n):
            a = at[0]
            at[0] += n
            assert at[0] <= 11264, at[0]
            return arena_b[:, a:a + n]

        ctxT = carve(KT * B * TPAD).rearrange("p (k b t) -> p k b t", k=KT, b=B)
        ctxN = carve((B + 2) * 2 * D).rearrange("p (b h d) -> p b h d", b=B + 2, h=2)
        txs_at = at[0]
        txs = carve(KT * 2 * T).rearrange("p (k b t) -> p k b t", k=KT, b=2)
        rho = carve(T)
        fts = carve(KT * P).rearrange("p (k f) -> p k f", k=KT)
        at[0] = 0
        blk = carve(HH * TOK).rearrange("p (h t) -> p h t", h=HH)
        blks0 = [blk, slot[3][:, 0:HH * TOK].rearrange("p (h t) -> p h t", h=HH)]
        vblk = carve(B * D).rearrange("p (b g c e) -> p b g c e", b=B, g=H // 2, c=2)
        qT = carve(KT * TOK).rearrange("p (k t) -> p k t", k=KT)
        kT = carve(KT * TOK).rearrange("p (k t) -> p k t", k=KT)
        oT = carve(KT * TOK).rearrange("p (k t) -> p k t", k=KT)
        at[0] = HH * TOK
        vz = carve(NQ * H * 32).rearrange("p (q h e) -> p q h e", q=NQ, h=H)
        assert NQ * H * 32 <= B * D
        pr1_at = HH * TOK + B * D + 3 * KT * TOK
        at[0] = txs_at
        smT = carve(KT * B * NWIN).rearrange("p (k n) -> p k n", k=KT)
        qkT = carve(KT * B * NWIN).rearrange("p (k n) -> p k n", k=KT)
        qv = carve(2 * D).rearrange("p (h d) -> p h d", h=2)
        mpr = carve(B * NWIN).rearrange("p (b n) -> p b n", b=B)

        arena_c = sb("arena_c", [P, 5120])
        pr = arena_c[:, 0:4 * 512].rearrange("p (s n) -> p s n", s=4)
        prT = arena_c[:, 4 * 512:6 * 512].rearrange("p (s n) -> p s n", s=2)
        ws_sb = arena_c[:, 0:8 * D].rearrange("p (k d) -> p k d", k=8)
        negm = arena_c[:, 2048:2048 + (NQ + 1) * T].rearrange("p (q t) -> p q t", q=NQ + 1)
        mask_sb = negm[:, 1:, :].bitcast(I32)
        attT = arena_c[:, 3328:3328 + 4 * P].rearrange("p (h b f) -> p h b f", h=2, b=2)
        featT = arena_c[:, 4096:5120].rearrange("p (k t) -> p k t", k=KT)
        blks1 = [blk, arena_c[:, 0:HH * TOK].rearrange("p (h t) -> p h t", h=HH)]
        pr1 = arena_b[:, pr1_at:pr1_at + 3 * 512].rearrange("p (s n) -> p s n", s=3)
        wz = sb("wz", [P, KT, 63])
        nmax = sb("nmax", [P, 1])
        rsum = sb("rsum", [P, NQ + 1])
        rinv = sb("rinv", [P, NQ])
        dots = sb("dots", [P, NQ + 1, 2])
        dot = sb("dot", [P, 2])
        wbpre = sb("wbpre", [P, NQ, 2])
        wbs = sb("wbs", [P, 2, NQ])
        junk = sb("junk", [P, 2 * D])
        hmx = sb("hmx", [P, 2, HH])
        hsum = sb("hsum", [P, 2, HH])
        hinv = sb("hinv", [P, 2, HH])
        gstat = sb("gstat", [P, KT, B])
        gvar = sb("gvar", [P, KT, B])
        grs = sb("grs", [P, KT, B])
        gsc = sb("gsc", [P, KT, B])
        ssq = sb("ssq", [P, NQ])
        mmx = sb("mmx", [P, B])
        msum = sb("msum", [P, B])
        ca = [0]

        def carve_c(*dims):
            n = int(np.prod(dims))
            a = ca[0]
            ca[0] += n
            return _view(arena_c, (a, n), dims if len(dims) > 1 else ())
        ptm = carve_c(NQ, P)
        lgT = carve_c(P)
        pick = carve_c(NQ, P)
        lastw = carve_c(NQ, P)
        lastT = carve_c(NQ, P)
        lg = sb("lg", [P, NQ, E])
        top = sb("top", [P, NQ, 8])
        topi = sb("topi", [P, NQ, 8], U32)
        topf = sb("topf", [P, NQ, 2])
        oh = sb("oh", [P, NQ, 2, E])
        sel = sb("sel", [P, NQ + 1, E])
        ntf = sb("ntf", [P, 3, E])
        rowf = sb("rowf", [P, NQ, E])
        ohr = sb("ohr", [P, NQ, 2, E])
        ridf = sb("ridf", [P, NQ, 2])
        rid = sb("rid", [P, NQ * 2], U32)
        meta = sb("meta", [P, 3, E], I32)
        gd = sb("gd", [P, NQ])
        ge = sb("ge", [P, NQ])
        lrow = sb("lrow", [P, NQ])
        lwt = sb("lwt", [P, NQ, 2])
        lsum = sb("lsum", [P, NQ])
        loff = sb("loff", [P, 1])
        gden = sb("gden", [P, NQ])
        gw = sb("gw", [P, NQ, 2])
        xrow = carve_c(D)
        xT = carve_c(KT, P)
        hT = carve_c(8, P)
        zT = carve_c(4, P)
        sT = carve_c(4, P)
        yrow = carve_c(D)
        assert ca[0] <= 5120
        yk = arena_b[:, 0:NQ * 2 * D].rearrange("p (q k d) -> p q k d", q=NQ, k=2)

        blk_ctx = ctx.enter_context(nc.Block())
        block = blk_ctx

        def bc(ap, axis, n):
            a = ap.unsqueeze(axis)
            shape = list(a.shape)
            shape[axis] = n
            return a.broadcast_to(shape)

        SC = (4, 5, 1)
        SC0 = (4, 5, 1, 3)
        OB = (2, 6)
        MB = (2, 6)
        RB = ((6, 7), (0, 3))
        MH = 5
        VB = (0, 2, 3, 0)

        def experts(l, slot_of, at_of):
            def view(s, name, *dims):
                a, n = at_of[name]
                return _view(slot_of[s], (a, n), dims)
            return view

        E0 = experts(0, slot, E0_AT)
        E1 = experts(1, slot, E1_AT)

        def tile_counts(eng, e):
            return (eng.value_load(meta[0:1, 0, bass.ds(e, 1)], min_val=1, max_val=4),
                    eng.value_load(meta[0:1, 1, bass.ds(e, 1)], min_val=0, max_val=NT_MAX - 1))

        def all_tiles(eng, tile):
            with eng.Fori(0, 2) as half:
                counts = [tile_counts(eng, half * SLOTS)]
                for s in range(SLOTS):
                    def ahead():
                        if s + 1 < SLOTS:
                            counts.append(tile_counts(eng, half * SLOTS + (s + 1)))
                    nt, first = counts[s]
                    with eng.Fori(0, nt) as t:
                        tile(s, half, first + t, ahead)

        @block.sync
        def _(sp):
            sp.dma_start(x[:], x_in.rearrange("(q p) d -> p q d", p=P)).then_inc(sem("x_in"), 16)
            sp.dma_start(w_sb[:], w_in).then_inc(sem("w_in"), 16)
            for q in range(NQ):
                for k in range(KT):
                    sp.dma_start(ctxT[:, k, 2 * q:2 * q + 2, 0:T], ctx_cols[:, k, 2 * q:2 * q + 2])\
                      .then_inc(sem(f"ctxT_in{q}"), 16)
            sp.dma_start(mask_sb[:], mask_in).then_inc(sem("mask_in"), 16)
            sp.dma_start(ws_sb[:], ws_in[0]).then_inc(sem("ws_in"), 16)
            sp.dma_start(c_sb[:], c_in).then_inc(sem("c_in"), 16)
            sp.dma_start(ctxN[:, 2:], ctx_rows).then_inc(sem("ctxN_in"), 16)
            sp.dma_start(v_sb[:], v_in).then_inc(sem("v_in"), 16)
            with sp.Fori(0, NQ - 1) as p:
                sp.wait_ge(sem("ws_used"), p + 1)
                sp.dma_start(ws_sb[:], ws_in[bass.ds(p + 1, 1)].rearrange("o p k d -> (o p) k d")).then_inc(sem("ws_in"), 16)
            sp.wait_ge(sem("pool_const"), 5)
            for l in range(2):
                for rows in (xg[l], yg[l]):
                    sp.dma_start(rows.rearrange("(n p) d -> p n d", p=P),
                                 bc(zeros[:], 1, NT_ROWS)).then_inc(sem("rows_zero"), 16)
            sp.wait_ge(sem("o_mm0"), NQ)
            sp.dma_start(v_sb[:, 0:R_N], r_in).then_inc(sem("r_in"), 16)
            for l in range(2):
                sp.wait_ge(sem(f"meta{l}"), 1)
                sp.wait_ge(sem(f"scattered{l}"), 16 * 2 * NQ)

                def load_row(s, half, n, ahead):
                    sp.wait_ge(sem(f"row_used{l}"), n + 1)
                    sp.dma_start(xrow[:], xg[l][bass.ds(n * P + 2 * P, P), :]).then_inc(sem(f"row_in{l}"), 16)
                    ahead()
                all_tiles(sp, load_row)
            for q in range(NQ):
                sp.wait_ge(sem("x_done"), q + 1)
                sp.dma_start(out[q * P:(q + 1) * P, :], x[:, q, :]).then_inc(sem("out_done"), 16)
            sp.wait_ge(sem("out_done"), 16 * NQ)

        @block.gpsimd
        def _(pool):
            def rsqrt(k, dst, src, n):
                pool.wait_ge(sem("var_ready"), k + 1)
                pool.tensor_tensor(dst, src, mhalf[:, 0:n], ALU.pow).then_inc(sem("rstd_ready"), 1)

            passes = [0]

            def passed():
                passes[0] += 1
                pool.tensor_tensor(token[:], mhalf[:, 0:1], mhalf[:, 0:1], ALU.add).then_inc(sem("passed"), 1)
                pool.wait_ge(sem("passed"), passes[0])

            pool.sem_inc(sem("h_filled3"), HEAD)
            pool.memset(mhalf[:], -0.5).then_inc(sem("pool_const"), 1)
            pool.memset(zeros[:], 0.0).then_inc(sem("pool_const"), 1)
            pool.memset(ctxT[:, :, :, T:TPAD], 0.0).then_inc(sem("pool_const"), 1)
            pool.memset(ctxN[:, 0:2], 0.0).then_inc(sem("pool_const"), 1)
            pool.memset(attT[:], 0.0).then_inc(sem("pool_const"), 1)
            pool.wait_ge(sem("pool_const"), 5)
            rsqrt(0, rstd[:], veps[:], NQ)
            with pool.Fori(0, NQ) as p:
                pool.wait_ge(sem("staged"), p * 3 + 3)
                for j in range(32):
                    pool.wait_ge(sem("slot_free"), p * 32 + (j + 1))
                    if j % 2:
                        pool.tensor_tensor(hbuf(j)[:, 2, 1, :], txs[:, 1, 1, :],
                                           fts[:, 1, 64 + j:65 + j].broadcast_to([P, T]), ALU.add)
                    pool.tensor_tensor(hbuf(j)[:, 3], txs[:, :, 1, :],
                                       fts[:, :, 96 + j:97 + j].broadcast_to([P, KT, T]), ALU.add)\
                        .then_inc(sem("h_filled3"), 1)
            pool.wait_ge(sem("slot_free"), ROWS_AHEAD + NQ * 32)
            pool.wait_ge(sem("staged"), 3 * NQ)
            for s in range(3):
                pool.dma_start(slot[s][:, 0:E0_N], e0_in[s]).then_inc(sem(f"slot{s}_in"), 16)
            rsqrt(1, rstd[:], veps[:], NQ)
            pool.wait_ge(sem("x1_ready"), NQ)
            pool.memset(vblk[:], 0.0).then_inc(sem("vblk_zero"), 1)
            for i in range(2 * NQ):
                pool.wait_ge(sem("sc_inv"), i + 1)
                v = pr[:, i % 4, :].rearrange("p (h m) -> p h m", h=HH)
                pool.tensor_tensor(v, v, bc(hinv[:, i % 2, :], 2, S), ALU.mult).then_inc(sem("sc_norm"), 1)

            pool.wait_ge(sem("sc_mm0"), 2 * NQ)
            pool.dma_start(slot[3][:, 0:E0_N], e0_in[3]).then_inc(sem("slot3_in"), 16)

            def route(l, k, n_in):
                rsqrt(k, rstd[:], veps[:], NQ)
                pool.wait_ge(sem("rows_zero"), 64)
                pool.wait_ge(sem("ln_ready"), 4 * (n_in + 1))
                pool.wait_ge(sem("rid"), l + 1)
                for q in range(NQ):
                    for c in range(2):
                        pool.indirect_dma_start(
                            out=xg[l], out_offset=bass.IndirectOffsetOnAxis(ap=rid[:, 2 * q + c:2 * q + c + 1], axis=0),
                            in_=ln[:, q, :], in_offset=None).then_inc(sem(f"scattered{l}"), 16)

            def more_weights(l, experts_, e_in, n_cols, next_in, next_cols):
                for e in experts_:
                    s = e % SLOTS
                    end = pool.value_load(meta[0:1, 2, e:e + 1], min_val=1, max_val=NT_MAX)
                    if e + SLOTS < E:
                        pool.wait_ge(sem(f"y_evac{l}"), HEAD + end)
                        passed()
                        pool.dma_start(slot[s][:, 0:n_cols], e_in[e + SLOTS]).then_inc(sem(f"slot{s}_in"), 16)
                    elif next_in is not None:
                        pool.wait_ge(sem(f"y_evac{l}"), HEAD + end)
                        passed()
                        pool.dma_start(slot[s][:, 0:next_cols], next_in[s]).then_inc(sem(f"slot{s}_in"), 16)

            def gather(l):
                end = pool.value_load(meta[0:1, 2, E - 1:E], min_val=E, max_val=NT_MAX)
                pool.wait_ge(sem(f"y_stored{l}"), end * 16)
                passed()
                for q in range(NQ):
                    for c in range(2):
                        pool.indirect_dma_start(
                            out=yk[:, q, c, :], out_offset=None, in_=yg[l],
                            in_offset=bass.IndirectOffsetOnAxis(ap=rid[:, 2 * q + c:2 * q + c + 1], axis=0)
                        ).then_inc(sem(f"gathered{q}"), 16)

            route(0, 2, 2)
            pool.wait_ge(sem(f"meta0"), 1)
            rsqrt(3, rinv[:], veps[:], NQ)
            pool.wait_ge(sem("rstd_ready"), 4)
            pool.wait_ge(sem("mem_raw"), 2)
            pool.tensor_tensor(memn[:], memn[:], bc(rinv[:], 2, D), ALU.mult).then_inc(sem("memn_ready"), 1)
            pool.wait_ge(sem("memn_ready"), 1)
            pool.tensor_tensor(memn[:], memn[:], bc(V("mnw"), 1, NQ), ALU.mult).then_inc(sem("memn_ready"), 1)
            more_weights(0, range(E - 1), e0_in, E0_N, e1_in, E1_N)
            gather(0)
            more_weights(0, range(E - 1, E), e0_in, E0_N, e1_in, E1_N)
            rsqrt(4, rstd[:], veps[:], NQ)
            rsqrt(5, rinv[:], veps[:], NQ)
            rsqrt(6, rstd[:], veps[:], NQ)
            pool.wait_ge(sem("x_ready"), 4)
            pool.memset(vz[:], 0.0).then_inc(sem("vz_zero"), 1)
            for k in range(KT):
                rsqrt(7 + k, grs[:, k, :], gvar[:, k, :], B)
            route(1, 9, 5)
            pool.wait_ge(sem(f"meta1"), 1)
            more_weights(1, range(SLOTS), e1_in, E1_N, None, 0)
            gather(1)

        @block.scalar
        def _(act):
            for name in ("s_done", "h_done"):
                act.sem_inc(sem(name), HEAD)
            def lnT_half(k):
                act.wait_ge(sem("tr_ready"), k + 1)
                act.activation(lnT[:, 0, :], bank[0][:], ACT.Copy).then_inc(sem("lnT0_ready"), 1)

            def ffn_loop(l, tile_body):
                act.wait_ge(sem(f"meta{l}"), 1)

                def tile(s, half, n, ahead):
                    tile_body(s, n, ahead)
                all_tiles(act, tile)

            lnT_half(0)
            act.wait_ge(sem("w_in"), 16)
            for i, (b, cols) in enumerate(((2, slice(0, P)), (6, slice(P, TOK)))):
                for m in range(KT):
                    act.wait_ge(sem("feat_mm"), 2 * i + m + 1)
                    act.activation(featT[:, m, cols], bank[b + m][:, cols], ACT.Identity,
                                   bias=W("bvec")[:, m:m + 1]).then_inc(sem("feat_ready"), 1)
            def exp_scores(n):
                act.wait_ge(sem("nmax_ready"), n + 1)
                act.activation(rho[:], rho[:], ACT.Exp, bias=nmax[:],
                               accum_out=rsum[:, n:n + 1] if isinstance(n, int) else rsum[:, bass.ds(n, 1)])\
                   .then_inc(sem("att_exp"), 1)

            with act.Fori(0, NQ) as p:
                for j in range(0, 32, 2):
                    if j == 6:
                        exp_scores(p)
                    act.wait_ge(sem("h_filled"), HEAD + p * 32 + (j + 2))
                    act.wait_ge(sem("h_filled3"), HEAD + p * 32 + (j + 2))
                    hj = pairs_h[j % ROWS_AHEAD // 2].rearrange("p u g k t -> p (u g k t)")
                    act.activation(hj, hj, ACT.Tanh).then_inc(sem("h_tanh"), 2)
            exp_scores(NQ)
            for m in range(KT):
                act.wait_ge(sem("sm_mm"), 1)
                act.activation(smT[:, m, :], bank[2 + m][:, 0:D], ACT.Copy).then_inc(sem("smT_ready"), 1)
            act.wait_ge(sem("v_in"), 16)
            act.wait_ge(sem("wbpre_ready"), 1)
            for c, b_ in enumerate(("bcw", "bcb")):
                act.activation(wbs[:, c, :], wbpre[:, :, c], ACT.Tanh, bias=V(b_)).then_inc(sem("wbs_ready"), 1)
            for m in range(KT):
                act.wait_ge(sem("qk_mm"), m + 1)
                act.activation(qkT[:, m, :], bank[4 + m][:, 0:D], ACT.Copy).then_inc(sem("qkT_ready"), 1)
            for h in range(2):
                act.wait_ge(sem("qv_mm"), 2)
                act.activation(qv[:, h, :], bank[3][:, h * D:(h + 1) * D], ACT.Copy).then_inc(sem("qv_ready"), 1)
            lnT_half(1)
            act.wait_ge(sem("c_in"), 16)
            act.wait_ge(sem("k_mm0"), 1)
            act.activation(kT[:, 0, :], bank[4][:], ACT.Identity, bias=V("bqkv")[:, 2:3])\
               .then_inc(sem("kT_ready0"), 1)
            act.wait_ge(sem("kT_ready0"), 1)
            for h in range(MH, HH):
                act.activation(blk[:, h, :], kT[:, 0, :], ACT.Copy, scale=C("hmask")[:, h:h + 1])\
                   .then_inc(sem("blkA_ready"), 1)
            act.wait_ge(sem("mem_shift"), 1)
            m2 = mpr[:].rearrange("p b n -> p (b n)")
            act.activation(m2, m2, ACT.Exp, scale=1.0 / 16.0).then_inc(sem("mem_exp"), 1)
            def values_evac(q):
                act.wait_ge(sem("v_mm0"), q + 1)
                if q == 0:
                    act.wait_ge(sem("vblk_zero"), 1)
                v_ps = bank[VB[q]][:].rearrange("p (b g c e) -> p b g c e", b=2, g=HH, c=2)
                for c in range(2):
                    r = slice(64 * c, 64 * c + 64)
                    act.activation(vblk[r, 2 * q:2 * q + 2, :, c, :], v_ps[r, :, :, c, :], ACT.Copy)\
                       .then_inc(sem("vblk_ready"), 1)

            def heads_evac(k):
                act.wait_ge(sem("pv_tile0"), NQ * (k + 1))
                act.activation(oT[:, k, :], bank[6 + k][:], ACT.Identity, bias=V("bqkv")[:, 4 + k:5 + k])\
                   .then_inc(sem("oT_ready0"), 1)

            values_evac(0)
            act.wait_ge(sem("k_mm0"), 2)
            act.activation(kT[:, 1, :], bank[1][:], ACT.Identity, bias=V("bqkv")[:, 3:4])\
               .then_inc(sem("kT_ready0"), 1)
            for i in range(2 * NQ):
                if i == 1:
                    values_evac(2)
                    values_evac(3)
                act.wait_ge(sem("sc_shift"), i + 1)
                act.activation(pr[:, i % 4, :], pr[:, i % 4, :], ACT.Exp).then_inc(sem("sc_exp"), 1)
                if i == 0:
                    values_evac(1)
                if i >= 2:
                    _evac_prT(act, sem, prT, bank, i - 2)
                if i == 2 * NQ - 1:
                    heads_evac(0)
            _evac_prT(act, sem, prT, bank, 2 * NQ - 2)
            _evac_prT(act, sem, prT, bank, 2 * NQ - 1)
            heads_evac(1)
            lnT_half(2)
            act.wait_ge(sem("mem_mm"), 1)
            for q in range(NQ):
                act.activation(tmp[:, q, :], bank[MB[q // 2]][:, (q % 2) * D:(q % 2 + 1) * D], ACT.Square,
                               accum_out=ssq[:, q:q + 1]).then_inc(sem("mem_sq"), 1)
            for h in range(2):
                act.activation(memn[:, 2 * h:2 * h + 2, :].rearrange("p q d -> p (q d)"), bank[MB[h]][:], ACT.Copy)\
                   .then_inc(sem("mem_raw"), 1)
            act.wait_ge(sem("gd_ready"), 1)
            act.activation(ge[:], gd[:], ACT.Exp).then_inc(sem("ge_ready"), 1)

            def last_evac(l):
                act.wait_ge(sem("last_tr"), l + 1)
                act.activation(lastT[:].rearrange("p q t -> p (q t)"), bank[6][:], ACT.Copy)\
                   .then_inc(sem("lastT_ready"), 1)

            def tile0(s, n, ahead):
                store(0, n)
                ahead()
                act.wait_ge(sem("y_mm0"), HEAD + n)
                for m in range(4):
                    act.wait_ge(sem("g_mm"), HEAD + n * 2 + (m // 2 + 1))
                    act.activation(sT[:, m, :], bank[5 + m // 2][:, (m % 2) * P:(m % 2 + 1) * P], ACT.Silu,
                                   bias=E0(s, "bg")[:, m:m + 1]).then_inc(sem("s_done"), 1)

            def store(l, n):
                act.wait_ge(sem(f"y_evac{l}"), HEAD + n)
                act.dma_start(yg[l][bass.ds(n * P, P), :], yrow[:]).then_inc(sem(f"y_stored{l}"), 16)

            def tile1(s, n, ahead):
                store(1, n)
                ahead()
                act.wait_ge(sem("y_mm1"), HEAD + n)
                for m in range(8):
                    act.wait_ge(sem("h_mm"), n * 4 + (m // 2 + 1))
                    act.activation(hT[:, m, :], bank[1 + m // 2][:, (m % 2) * P:(m % 2 + 1) * P], ACT.Gelu,
                                   bias=E1(s, "b1")[:, m:m + 1]).then_inc(sem("h_done"), 1)

            last_evac(0)
            act.wait_ge(sem("rows_zero"), 64)
            for s in range(SLOTS):
                act.wait_ge(sem(f"slot{s}_in"), 16)
            ffn_loop(0, tile0)
            for q in range(NQ):
                act.wait_ge(sem("h2_ready"), q + 1)
                act.activation(tmp[:, q, :], ln[:, q, :], ACT.Square,
                               accum_out=ssq[:, q:q + 1]).then_inc(sem("h2_sq"), 1)
            lnT_half(3)
            act.wait_ge(sem("qT_ready1"), 1)
            for h in range(MH, HH):
                act.activation(blk[:, h, :], qT[:, 0, :], ACT.Copy, scale=C("hmask")[:, h:h + 1])\
                   .then_inc(sem("blkA_ready"), 1)
            act.wait_ge(sem("k_mm1"), 1)
            act.activation(kT[:, 0, :], bank[4][:], ACT.Copy).then_inc(sem("kT_ready1"), 1)
            for q in range(NQ):
                if q == 2:
                    act.wait_ge(sem("k_mm1"), 2)
                    act.activation(kT[:, 1, :], bank[0][:], ACT.Copy).then_inc(sem("kT_ready1"), 1)
                for c in range(2):
                    act.wait_ge(sem("v_mm1"), 2 * (q // 2) + 2)
                    if q == 0:
                        act.wait_ge(sem("vz_zero"), 1)
                    v_ps = bank[6 + q // 2][:, (q % 2) * D:(q % 2 + 1) * D].rearrange("p (g c e) -> p g c e", c=2, e=HD)
                    vz_v = vz[:, q].rearrange("p (g c) (d e) -> p g c d e", c=2, e=HD)
                    act.activation(vz_v[:, :, c, c, :], v_ps[:, :, c, :], ACT.Copy).then_inc(sem("vz_ready"), 1)
            lnT_half(4)
            act.wait_ge(sem("gd_ready"), 2)
            act.activation(ge[:], gd[:], ACT.Exp).then_inc(sem("ge_ready"), 1)
            last_evac(1)
            for s in range(SLOTS):
                act.wait_ge(sem(f"slot{s}_in"), 16 * 3)
            ffn_loop(1, tile1)

        @block.tensor
        def _(pe):
            ident = W("ident")
            for name in ("y_mm0", "y_mm1", "g_mm"):
                pe.sem_inc(sem(name), HEAD)

            def ln_transpose(k, n):
                for q in range(NQ):
                    pe.wait_ge(sem("ln_ready"), 4 * n + q + 1)
                    for kt in range(KT):
                        ins = pe.transpose(bank[kt][:, q * P:(q + 1) * P], ln[:, q, kt * P:(kt + 1) * P], ident)
                ins.then_inc(sem("tr_ready"), 1)

            def project(dst, w, o, m=P):
                for kt in range(KT):
                    ins = pe.matmul(dst, w[:, kt, o:o + m], lnT[:, kt, :], start=(kt == 0), stop=(kt == KT - 1))
                return ins

            def warm(n, b):
                for _ in range(n):
                    pe.matmul(bank[b][:, 0:P], zeros[:, 0:P], zeros[:, 0:P], start=True, stop=True)

            Wf, Ws = W("W", KT, D), W("Ws", KT, D)

            def project_context(m, kt, b):
                return pe.matmul(bank[4 + m][:], Ws[:, kt, m * P:(m + 1) * P], ctxT[:, kt, bass.ds(b, 2), 0:T],
                                 start=(kt == 0), stop=(kt == KT - 1))

            pe.wait_ge(sem("pool_const"), 5)
            warm(10, 2)
            pe.wait_ge(sem("w_in"), 16)
            ln_transpose(0, 0)
            pe.wait_ge(sem("ctxT_in0"), 32)
            for m in range(KT):
                for kt in range(KT):
                    ins = project_context(m, kt, 0)
                ins.then_inc(sem("txt_mm"), 1)
            for half in ("lnT0_ready", "lnT1_ready"):
                pe.wait_ge(sem(half), 1)
            for b, cols in ((2, slice(0, P)), (6, slice(P, TOK))):
                for m in range(KT):
                    for kt in range(KT):
                        ins = pe.matmul(bank[b + m][:, cols], Wf[:, kt, m * P:(m + 1) * P], lnT[:, kt, cols],
                                        start=(kt == 0), stop=(kt == KT - 1))
                    ins.then_inc(sem("feat_mm"), 1)
            pe.wait_ge(sem("feat_ready"), 4)
            for m in range(KT):
                pe.matmul(bank[2 + m][:, 0:D], zeros[:, 0:P], zeros[:], start=True, stop=False)
            pe.matmul(bank[0][:, 0:T], zeros[:, 0:P], zeros[:], start=True, stop=True).then_inc(sem("rho_open"), 1)
            pe.wait_ge(sem("wz_ready"), 1)
            def turn_att(n):
                pe.wait_ge(sem("att_exp"), n + 1)
                for h in range(2):
                    ins = pe.transpose(bank[6][:, h * P:(h + 1) * P], rho[:, h * P:(h + 1) * P], ident)
                ins.then_inc(sem("att_tr"), 1)

            def attend(n, i):
                h, b2 = i // 2, i % 2
                if i == 0:
                    pe.wait_ge(sem("ctxN_in"), 16)
                    pe.wait_ge(sem("attT_ready"), n + 1)
                    pe.wait_ge(sem("dots_ready"), HEAD + 3 * n)
                ctx_b = ctxN[:, 2 * n + b2, h, :] if isinstance(n, int) else ctxN[:, bass.ds(n * 2 + b2, 1), h, :]
                ins = pe.matmul(bank[7][:, 0:D], attT[:, h, b2, :], ctx_b, start=(i == 0), stop=(i == 3))
                if i == 3:
                    ins.then_inc(sem("txth_mm"), 1)

            def pair(p, last):
                for j in range(32):
                    pe.wait_ge(sem("h_tanh"), p * 32 + (j + 1))
                    if j == 0:
                        pe.wait_ge(sem("rho_evac"), p + 1)
                    for k in range(KT):
                        for g in range(4):
                            ins = pe.matmul(bank[0][32 * g:32 * g + 32, 0:T], wz[:, k, 31 - j:63 - j],
                                            hbuf(j)[:, g, k, :], start=(j == 0 and k == 0),
                                            stop=(j == 31 and k == KT - 1))
                    ins.then_inc(sem("slot_free"), 1)
                    if 12 <= j < 16 and not last:
                        if j == 12:
                            for q in range(1, NQ):
                                pe.wait_ge(sem(f"ctxT_in{q}"), 32)
                            pe.wait_ge(sem("staged"), p * 3 + 3)
                        ins = project_context((j - 12) // KT, j % KT, p * 2 + 2)
                        if j % KT == KT - 1:
                            ins.then_inc(sem("txt_mm"), 1)
                    if j == 8:
                        turn_att(p)
                    if 16 <= j < 20:
                        attend(p, j - 16)
                    if j == 16:
                        pe.wait_ge(sem("ws_in"), (p + 1) * 16)
                    if j >= 16:
                        i, m = j // 2 - 8, j % 2
                        ins = pe.matmul(bank[2 + m][:, 0:D], ws_sb[:, i, m * P:(m + 1) * P],
                                        ctxT[:, i % 2, :, bass.ds(p * 4 + i // 2, NWIN, step=STRIDE)],
                                        start=False, stop=False)
                    if j == 31:
                        ins.then_inc(sem("ws_used"), 1)

            with pe.Fori(0, NQ - 1) as p:
                pair(p, False)
            pair(NQ - 1, True)
            for m in range(KT):
                ins = pe.matmul(bank[2 + m][:, 0:D], zeros[:, 0:P], zeros[:], start=False, stop=True)
            ins.then_inc(sem("sm_mm"), 1)
            turn_att(NQ)
            for i in range(4):
                attend(NQ, i)
            pe.wait_ge(sem("c_in"), 16)
            qawk, qawv, qaq = V("qawk", KT, D), V("qawv", KT, D), V("qaq", KT, P)
            pe.wait_ge(sem("v_in"), 16)
            pe.wait_ge(sem("smT_ready"), 2)
            for m in range(KT):
                for kt in range(KT):
                    ins = pe.matmul(bank[4 + m][:, 0:D], qawk[:, kt, m * P:(m + 1) * P], smT[:, kt, :],
                                    start=(kt == 0), stop=(kt == KT - 1))
                ins.then_inc(sem("qk_mm"), 1)
            for h in range(2):
                for kt in range(KT):
                    ins = pe.matmul(bank[3][:, h * D:(h + 1) * D], smT[:, kt, h * P:(h + 1) * P], qawv[:, kt, :],
                                    start=(kt == 0), stop=(kt == KT - 1))
                ins.then_inc(sem("qv_mm"), 1)
            pe.wait_ge(sem("qkT_ready"), 2)
            for kt in range(KT):
                ins = pe.matmul(bank[2][:, 0:D], qaq[:, kt, :], qkT[:, kt, :],
                                start=(kt == 0), stop=(kt == KT - 1))
            ins.then_inc(sem("ms_mm"), 1)
            warm(12, 5)
            ln_transpose(1, 1)
            warm(4, 5)
            for half in ("lnT0_ready", "lnT1_ready"):
                pe.wait_ge(sem(half), 2)
            pe.wait_ge(sem("v_in"), 16)
            qkv = V("qkv", KT, 3 * D)
            project(bank[4][:], qkv, D).then_inc(sem("k_mm0"), 1)
            project(bank[6][:], qkv, 0).then_inc(sem("q_mm0"), 1)

            def values_proj(q):
                if q == 1:
                    pe.wait_ge(sem("mem_shift"), 1)
                if q == 2:
                    pe.wait_ge(sem("qv_ready"), 2)
                if q == 3:
                    pe.wait_ge(sem("vblk_ready"), 2)
                for b2 in range(2):
                    b = 2 * q + b2
                    for kt in range(KT):
                        for c in range(2):
                            ins = pe.matmul(bank[VB[q]][64 * c:64 * c + 64, b2 * D:(b2 + 1) * D],
                                            lnT[:, kt, b * S:(b + 1) * S], qkv[:, kt, 2 * D:3 * D],
                                            start=(kt == 0), stop=(kt == KT - 1))
                ins.then_inc(sem("v_mm0"), 1)

            def scores0(i):
                k, q = i // NQ, i % NQ
                if q == 0:
                    pe.wait_ge(sem("qT_ready0"), k + 1)
                    pe.wait_ge(sem("blk_ready0"), k + 1)
                    pe.wait_ge(sem("blkA_ready"), HH - MH)
                if i == 2:
                    pe.wait_ge(sem("kT_ready0"), 2)
                if i == 3:
                    pe.wait_ge(sem("vblk_ready"), 6)
                if i >= 4:
                    pe.wait_ge(sem("sc_shift"), i - 3)
                for b2 in range(2):
                    b = 2 * q + b2
                    ins = pe.matmul(bank[SC0[i % 4]][64 * b2:64 * b2 + 64, :], qT[:, k, b * S:(b + 1) * S],
                                    blks0[k][:, :, b * S:(b + 1) * S], start=True, stop=True)
                ins.then_inc(sem("sc_mm0"), 1)

            def turn0(i):
                pe.wait_ge(sem("sc_norm"), i + 1)
                if i == 0:
                    pe.wait_ge(sem("vblk_ready"), 2 * NQ)
                else:
                    pe.wait_ge(sem("prT_ready"), i)
                for g in range(4):
                    ins = pe.transpose(bank[0][:, g * P:(g + 1) * P], pr[:, i % 4, g * P:(g + 1) * P], ident)
                ins.then_inc(sem("pr_tr"), 1)

            def values0(i):
                k, q = i // NQ, i % NQ
                pe.wait_ge(sem("prT_ready"), i + 1)
                if i == NQ:
                    pe.wait_ge(sem("qT_ready0"), 2)
                for b2 in range(2):
                    b = 2 * q + b2
                    for g in range(4):
                        ins = pe.matmul(bank[6 + k][32 * g:32 * g + 32, b * S:(b + 1) * S],
                                        vblk[:, b, 4 * k + g].rearrange("p c e -> p (c e)"),
                                        prT[:, i % 2, g * P + b2 * S:g * P + (b2 + 1) * S], start=True, stop=True)
                ins.then_inc(sem("pv_tile0"), 1)

            def out_proj(l, k, w):
                pe.wait_ge(sem(f"oT_ready{l}"), k + 1)
                for q in range(NQ):
                    ins = pe.matmul(bank[OB[l] + q // 2][:, (q % 2) * D:(q % 2 + 1) * D],
                                    oT[:, k, q * P:(q + 1) * P], w[:, k, :], start=(k == 0 and q % 2 == 0),
                                    stop=(k == KT - 1), skip_group_check=True)
                    if k == KT - 1:
                        ins.then_inc(sem(f"o_mm{l}"), 1)

            values_proj(0)
            scores0(0)
            project(bank[1][:], qkv, D + P).then_inc(sem("k_mm0"), 1)
            scores0(1)
            values_proj(1)
            project(bank[7][:], qkv, P).then_inc(sem("q_mm0"), 1)
            scores0(2)
            values_proj(2)
            values_proj(3)
            for i in range(2 * NQ):
                if i + 3 < 2 * NQ:
                    scores0(i + 3)
                turn0(i)
                if i >= 1:
                    values0(i - 1)
            out_proj(0, 0, V("wo", KT, D))
            values0(2 * NQ - 1)

            pe.wait_ge(sem("mem_norm"), 1)
            pe.wait_ge(sem("prT_ready"), 2 * NQ)
            for h in range(2):
                ins = pe.transpose(bank[0][:, h * P:(h + 1) * P],
                                   mpr[:, 4 * h:4 * h + 4, :].rearrange("p b n -> p (b n)"), ident)
            ins.then_inc(sem("mp_tr"), 1)
            out_proj(0, 1, V("wo", KT, D))

            def route(l, k, n):
                warm(8, 5)
                if l == 0:
                    pe.wait_ge(sem("ptm_ready"), 1)
                    pe.wait_ge(sem("qv_ready"), 2)
                    for q in range(NQ):
                        ins = pe.matmul(bank[MB[q // 2]][:, (q % 2) * D:(q % 2 + 1) * D], ptm[:, q, :],
                                        qv[:, q // 2, :], start=True, stop=True)
                    ins.then_inc(sem("mem_mm"), 1)
                ln_transpose(k, n)
                for half in ("lnT0_ready", "lnT1_ready"):
                    pe.wait_ge(sem(half), k + 1)
                g = V(f"gw{l}", KT, 32)
                for kt in range(KT):
                    for q in range(NQ):
                        ins = pe.matmul(bank[7][32 * q:32 * q + 32, 384:384 + P], g[:, kt, :],
                                        lnT[:, kt, q * P:(q + 1) * P], start=(kt == 0), stop=(kt == KT - 1),
                                        skip_group_check=True)
                ins.then_inc(sem("lg_mm"), 1)
                pe.wait_ge(sem("lgT_ready"), l + 1)
                pe.transpose(bank[5][:, 0:P], lgT[:], ident).then_inc(sem("lg_tr"), 1)
                warm(5, 4)
                pe.wait_ge(sem("sel"), l + 1)
                pe.matmul(bank[7][:, 0:(NQ + 1) * E], C("tri"), sel[:].rearrange("p q e -> p (q e)"),
                          start=True, stop=False)
                for d in range(1, NQ + 1):
                    ins = pe.matmul(bank[7][:, d * E:(NQ + 1) * E], C("ones"),
                                    sel[:, 0:NQ + 1 - d, :].rearrange("p q e -> p (q e)"),
                                    start=False, stop=(d == NQ))
                ins.then_inc(sem("pos_mm"), 1)
                warm(12, 4)
                pe.wait_ge(sem("pick"), l + 1)
                for kt in range(KT):
                    for q in range(NQ):
                        ins = pe.matmul(bank[0][:, kt * P:(kt + 1) * P], ln[:, q, kt * P:(kt + 1) * P], pick[:, q, :],
                                        start=(q == 0 and kt == 0), stop=(q == NQ - 1), skip_group_check=True)
                ins.then_inc(sem(f"row_used{l}"), 1)

            def last_turn(l):
                pe.wait_ge(sem("lastw"), l + 1)
                for q in range(NQ):
                    ins = pe.transpose(bank[6][:, q * P:(q + 1) * P], lastw[:, q, :], ident)
                ins.then_inc(sem("last_tr"), 1)
                pe.wait_ge(sem("lastT_ready"), l + 1)

            def last_add(l):
                end = pe.value_load(meta[0:1, 2, E - 1:E], min_val=E, max_val=NT_MAX)
                pe.wait_ge(sem(f"y_evac{l}"), end + HEAD)
                for q in range(NQ):
                    pe.matmul(bank[1 + q // 2][:, (q % 2) * D:(q % 2 + 1) * D], lastT[:, q, :], yrow[:],
                              start=True, stop=True).then_inc(sem("last_mm"), 1)

            def memory_ms():
                pe.wait_ge(sem("mem_sq"), NQ)
                pe.matmul(bank[7][:, 256:256 + NQ], C("bmean"), ssq[:], start=True, stop=True)\
                  .then_inc(sem("mss_mm"), 1)

            route(0, 2, 2)
            pe.wait_ge(sem("mem_raw"), 2)
            last_turn(0)
            memory_ms()
            def rows_turn(l, n):
                pe.wait_ge(sem(f"row_in{l}"), n * 16)
                for kt in range(KT):
                    ins = pe.transpose(bank[0][:, kt * P:(kt + 1) * P], xrow[:, kt * P:(kt + 1) * P], ident)
                ins.then_inc(sem(f"row_used{l}"), 1)

            def ffn_loop(l, tile_body):
                pe.wait_ge(sem(f"meta{l}"), 1)

                def tile(s, half, n, ahead):
                    pe.wait_ge(sem(f"slot{s}_in"), half * 16 + 16 * (1 + 2 * l))
                    pe.wait_ge(sem(f"xT_done{l}"), HEAD + n + 1)
                    tile_body(s, n, ahead)
                all_tiles(pe, tile)

            def down(l, s, n, act_sb, w, K, done, ahead):
                if l == 0:
                    rows_turn(l, n + 1)
                    ahead()
                pe.wait_ge(sem(f"y_evac{l}"), HEAD + n)
                for k in range(K):
                    pe.wait_ge(sem(done), HEAD + n * K + (k + 1))
                    ins = pe.matmul(bank[7][:, 0:D], act_sb[:, k, :], w[:, k, :], start=(k == 0), stop=(k == K - 1))
                    if l == 1 and k == K - 3:
                        rows_turn(l, n + 1)
                ins.then_inc(sem(f"y_mm{l}"), 1)
                if l == 1:
                    ahead()

            def tile0(s, n, ahead):
                w1, w2, wg = E0(s, "w1", KT, F0), E0(s, "w2", KT, F0), E0(s, "wg", 4, F0)
                for m in range(4):
                    if m < 2:
                        pe.wait_ge(sem("z_done"), HEAD + n * 4)
                    else:
                        pe.wait_ge(sem("z_done"), HEAD + n * 4 + (m - 1))
                    for i, w in enumerate((w1, w2)):
                        for kt in range(KT):
                            ins = pe.matmul(bank[1 + 2 * i + m % 2][:, 0:P], w[:, kt, m * P:(m + 1) * P], xT[:, kt, :],
                                            start=(kt == 0), stop=(kt == KT - 1))
                    ins.then_inc(sem("x12_mm"), 1)
                pe.wait_ge(sem("s_done"), HEAD + n * 4)
                for k in range(4):
                    pe.wait_ge(sem("z_done"), HEAD + n * 4 + (k + 1))
                    for m in range(4):
                        ins = pe.matmul(bank[5 + m // 2][:, (m % 2) * P:(m % 2 + 1) * P],
                                        wg[:, k, m * P:(m + 1) * P], zT[:, k, :], start=(k == 0 and m % 2 == 0),
                                        stop=(k == 3), skip_group_check=True)
                        if k == 3 and m % 2 == 1:
                            ins.then_inc(sem("g_mm"), 1)
                down(0, s, n, sT, E0(s, "w3", 4, D), 4, "s_done", ahead)

            def tile1(s, n, ahead):
                w1 = E1(s, "w1", KT, F1)
                pe.wait_ge(sem("h_done"), HEAD + n * 8)
                for m in range(8):
                    for kt in range(KT):
                        ins = pe.matmul(bank[1 + m // 2][:, (m % 2) * P:(m % 2 + 1) * P], w1[:, kt, m * P:(m + 1) * P],
                                        xT[:, kt, :], start=(kt == 0), stop=(kt == KT - 1))
                    if m % 2 == 1:
                        ins.then_inc(sem("h_mm"), 1)
                down(1, s, n, hT, E1(s, "w2", 8, D), 8, "h_done", ahead)

            ffn_loop(0, tile0)
            last_add(0)
            pe.wait_ge(sem("h2_sq"), NQ)
            pe.matmul(bank[7][:, 192:192 + NQ], C("bmean"), ssq[:], start=True, stop=True).then_inc(sem("hss_mm"), 1)
            warm(24, 5)
            ln_transpose(3, 4)
            warm(4, 5)
            for half in ("lnT0_ready", "lnT1_ready"):
                pe.wait_ge(sem(half), 4)
            pe.wait_ge(sem("r_in"), 16)
            def values_proj1(qs):
                for q in qs:
                    for kt in range(KT):
                        ins = pe.matmul(bank[6 + q // 2][:, (q % 2) * D:(q % 2 + 1) * D],
                                        lnT[:, kt, q * P:(q + 1) * P], R("rv", KT, D)[:, kt, :], start=(kt == 0),
                                        stop=(kt == KT - 1))
                    ins.then_inc(sem("v_mm1"), 1)

            project(bank[2][:], R("rq", KT, D), 0).then_inc(sem("q_mm1"), 1)
            project(bank[4][:], R("rk", KT, D), 0).then_inc(sem("k_mm1"), 1)
            values_proj1((0, 1))

            def scores1(i):
                k, q = i // NQ, i % NQ
                if q == 0:
                    pe.wait_ge(sem("kT_ready1"), k + 1)
                    pe.wait_ge(sem("blk_ready1"), k + 1)
                    pe.wait_ge(sem("blkA_ready"), 2 * (HH - MH))
                if i >= 3:
                    pe.wait_ge(sem("sc_decay"), i - 2)
                for b2 in range(2):
                    b = 2 * q + b2
                    ins = pe.matmul(bank[SC[i % 3]][64 * b2:64 * b2 + 64, :], kT[:, k, b * S:(b + 1) * S],
                                    blks1[k][:, :, b * S:(b + 1) * S], start=True, stop=True)
                ins.then_inc(sem("sc_mm1"), 1)

            def values1(i):
                k, q = i // NQ, i % NQ
                pe.wait_ge(sem("sc_decay"), i + 1)
                if i == 0:
                    pe.wait_ge(sem("vz_ready"), 2 * NQ)
                if i == NQ:
                    pe.wait_ge(sem("qT_ready1"), 2)
                for g in range(4):
                    for b2 in range(2):
                        for c in range(2):
                            h = 2 * g + c
                            ins = pe.matmul(bank[RB[k][b2]][32 * g:32 * g + 32, q * S:(q + 1) * S],
                                            vz[64 * b2:64 * b2 + 64, q, HH * k + h, :],
                                            pr1[64 * b2:64 * b2 + 64, i % 3, h * S:(h + 1) * S],
                                            start=(c == 0), stop=(c == 1))
                ins.then_inc(sem("pv_tile1"), 1)

            def group_mean(n):
                pe.wait_ge(sem("gsum_ready"), n + 1)
                pe.matmul(bank[2][:, n * 16:n * 16 + B], C("gmean"), gstat[:, n // 2, :], start=True, stop=True)\
                  .then_inc(sem("gm_mm"), 1)

            scores1(0)
            scores1(1)
            project(bank[3][:], R("rq", KT, D), P).then_inc(sem("q_mm1"), 1)
            project(bank[0][:], R("rk", KT, D), P).then_inc(sem("k_mm1"), 1)
            values_proj1((2, 3))
            for i in range(2 * NQ):
                if i + 2 < 2 * NQ:
                    scores1(i + 2)
                values1(i)
                if i == NQ:
                    group_mean(0)
                if i == NQ + 2:
                    group_mean(1)
            group_mean(2)
            out_proj(1, 0, R("ro", KT, D))
            group_mean(3)
            out_proj(1, 1, R("ro", KT, D))
            route(1, 4, 5)
            last_turn(1)
            ffn_loop(1, tile1)
            last_add(1)

        @block.vector
        def _(dve):
            chained = [0]

            def link(ins):
                chained[0] += 1
                ins.then_inc(sem("dve_chain"), 1)
                dve.wait_ge(sem("dve_chain"), chained[0])

            def layer_norm(k, n, ready=None, meanwhile=None):
                for q in range(NQ):
                    if ready is not None:
                        ready(q)
                    ins = dve.bn_stats(bn[:, q, :], x[:, q, :])
                link(ins)
                for q in range(NQ):
                    ins = dve.bn_aggr(mv[:, q, :], bn[:, q, :])
                link(ins)
                dve.tensor_scalar(veps[:], mv[:, :, 1], LN_EPS, None, ALU.add).then_inc(sem("var_ready"), 1)
                if meanwhile is not None:
                    meanwhile()
                dve.wait_ge(sem("rstd_ready"), k + 1)
                for q in range(NQ):
                    dve.tensor_scalar(ln[:, q, :], x[:, q, :], mv[:, q, 0:1], rstd[:, q:q + 1], ALU.subtract,
                                      ALU.mult).then_inc(sem("ln_ready"), 1)

            def lnT_half(k):
                dve.wait_ge(sem("tr_ready"), k + 1)
                dve.tensor_copy(lnT[:, 1, :], bank[1][:]).then_inc(sem("lnT1_ready"), 1)

            for name in ("h_filled", "dots_ready", "z_done", "xT_done0", "xT_done1", "y_evac0", "y_evac1"):
                dve.sem_inc(sem(name), HEAD)
            dve.memset(sel[:, NQ, :], 0.0)
            link(dve.memset(wz[:], 0.0))
            dve.wait_ge(sem("x_in"), 16)
            layer_norm(0, 0)
            dve.wait_ge(sem("w_in"), 16)
            dve.tensor_copy(wz[:, :, 31], W("wvec")).then_inc(sem("wz_ready"), 1)
            lnT_half(0)
            dve.memset(negm[:, 0, :], 0.0).then_inc(sem("negm_ready"), 1)
            dve.memset(hmx[:], 0.0).then_inc(sem("slot_free"), ROWS_AHEAD)
            dve.wait_ge(sem("feat_ready"), 2)

            def masked_scores(row, n):
                dve.wait_ge(sem("negm_ready"), n + 1)
                dve.tensor_tensor(rho[:], bank[0][:, 0:T], negm[:, row, :].rearrange("p o t -> p (o t)"), ALU.add)\
                   .then_inc(sem("rho_evac"), 1)

            def max_scores(n):
                dve.wait_ge(sem("rho_evac"), n + 1)
                dve.tensor_reduce(nmax[:], rho[:], AX_X, ALU.max, negate=True).then_inc(sem("nmax_ready"), 1)

            def att_evac(n):
                dve.wait_ge(sem("att_tr"), n + 1)
                for b2 in range(2):
                    cols = slice(S * b2, S * b2 + S)
                    ins = dve.tensor_copy(attT[:, :, b2, cols], bank[6][:, 0:2 * P].rearrange("p (h f) -> p h f", h=2)[:, :, cols])
                ins.then_inc(sem("attT_ready"), 1)

            def context_dots(n):
                dve.wait_ge(sem("txth_mm"), n + 1)
                dve.wait_ge(sem("dots_ready"), HEAD + 3 * n)
                for c, w in enumerate(("wcw", "wcb")):
                    dve.tensor_tensor_reduce(out=junk[:, c * D:(c + 1) * D], in0=bank[7][:, 0:D], in1=V(w),
                                             scale=1.0, scalar=0.0, op0=ALU.mult, op1=ALU.add,
                                             accum_out=dot[:, c:c + 1]).then_inc(sem("dots_ready"), 1)

            def keep_dots(n):
                dve.wait_ge(sem("dots_ready"), HEAD + 3 * n + 2)
                row = slice(n, n + 1) if isinstance(n, int) else bass.ds(n, 1)
                dve.tensor_copy(dots[:, row, :].rearrange("p o c -> p (o c)"), dot[:]).then_inc(sem("dots_ready"), 1)

            with dve.Fori(0, NQ) as p:
                dve.wait_ge(sem("h_filled"), HEAD + p * 32)
                dve.wait_ge(sem("h_filled3"), HEAD + p * 32)
                dve.tensor_copy(fts[:], featT[:, :, bass.ds(p * P, P)]).then_inc(sem("staged"), 1)
                dve.wait_ge(sem("txt_mm"), p * 2 + 2)
                for k in range(KT):
                    dve.tensor_copy(txs[:, k].rearrange("p b t -> p (b t)"), bank[4 + k][:]).then_inc(sem("staged"), 1)
                dve.wait_ge(sem("staged"), p * 3 + 3)
                for j in range(32):
                    dve.wait_ge(sem("slot_free"), p * 32 + (j + 1))
                    if j == 5:
                        dve.wait_ge(sem("slot_free"), p * 32 + ROWS_AHEAD)
                        dve.wait_ge(sem("rho_open"), 1)
                        masked_scores(bass.ds(p, 1), p)
                    if j == 12:
                        dve.wait_ge(sem("feat_ready"), 4)
                        dve.wait_ge(sem("mask_in"), 16)
                        row = bass.ds(p + 1, 1)
                        dve.tensor_scalar(negm[:, row, :].rearrange("p o t -> p (o t)"),
                                          negm[:, row, :].rearrange("p o t -> p (o t)").bitcast(I32), -NEG, NEG,
                                          ALU.mult, ALU.add).then_inc(sem("negm_ready"), 1)
                    if j == 7:
                        max_scores(p)
                    if j == 18:
                        att_evac(p)
                    if j == 28:
                        dve.wait_ge(sem("v_in"), 16)
                        context_dots(p)
                    if j == 30:
                        keep_dots(p)
                    for g in range(3):
                        for k in range(KT if g < 2 or j % 2 == 0 else 1):
                            ins = dve.tensor_scalar(hbuf(j)[:, g, k, :], txs[:, k, g // 2, :],
                                                    fts[:, k, 32 * g + j:32 * g + j + 1], None, ALU.add)
                    ins.then_inc(sem("h_filled"), 1)
            dve.wait_ge(sem("slot_free"), NQ * 32 + ROWS_AHEAD)
            masked_scores(slice(NQ, NQ + 1), NQ)
            max_scores(NQ)
            dve.wait_ge(sem("att_exp"), NQ + 1)
            dve.reciprocal(rinv[:], rsum[:, 1:]).then_inc(sem("rinv_ready"), 1)
            att_evac(NQ)
            context_dots(NQ)
            keep_dots(NQ)
            dve.wait_ge(sem("rinv_ready"), 1)
            dve.wait_ge(sem("dots_ready"), HEAD + 3 * (NQ + 1))
            dve.tensor_tensor(wbpre[:], dots[:, 1:, :], bc(rinv[:], 2, 2), ALU.mult).then_inc(sem("wbpre_ready"), 1)
            dve.wait_ge(sem("wbs_ready"), 2)
            for q in range(NQ):
                ins = dve.scalar_tensor_tensor(out=x[:, q, :], in0=ln[:, q, :], scalar=wbs[:, 0, q:q + 1],
                                               in1=x[:, q, :], op0=ALU.mult, op1=ALU.add)
            link(ins)
            for q in range(NQ):
                dve.tensor_scalar(x[:, q, :], x[:, q, :], wbs[:, 1, q:q + 1], None, ALU.add)\
                   .then_inc(sem("x1_ready"), 1)
            dve.wait_ge(sem("c_in"), 16)
            dve.wait_ge(sem("x1_ready"), NQ)
            layer_norm(1, 1)
            lnT_half(1)
            dve.wait_ge(sem("ms_mm"), 1)
            ms = bank[2][:, 0:D].rearrange("p (b n) -> p b n", b=B)
            link(dve.tensor_reduce(mmx[:], ms, AX_X, ALU.max))
            dve.tensor_tensor(mpr[:], ms, bc(mmx[:], 2, NWIN), ALU.subtract).then_inc(sem("mem_shift"), 1)

            def masked(l, srcT, k, n_heads):
                dst = (blks0, blks1)[l][k]
                for h in range(n_heads):
                    ins = dve.tensor_scalar(dst[:, h, :], srcT[:, k, :], C("hmask")[:, h:h + 1], None, ALU.mult)
                ins.then_inc(sem(f"blk_ready{l}"), 1)

            dve.wait_ge(sem("kT_ready0"), 1)
            masked(0, kT, 0, MH)

            def queries0(k):
                dve.wait_ge(sem("q_mm0"), k + 1)
                dve.tensor_scalar(qT[:, k, :], bank[6 + k][:], V("bqkv")[:, k:k + 1], float(HD) ** -0.5, ALU.add,
                                  ALU.mult).then_inc(sem("qT_ready0"), 1)

            def memory_norm():
                dve.wait_ge(sem("mem_exp"), 1)
                link(dve.tensor_reduce(msum[:], mpr[:], AX_X, ALU.add))
                link(dve.reciprocal(mmx[:], msum[:]))
                dve.tensor_tensor(mpr[:], mpr[:], bc(mmx[:], 2, NWIN), ALU.mult).then_inc(sem("mem_norm"), 1)

            def shift0(i):
                dve.wait_ge(sem("sc_mm0"), i + 1)
                sc = bank[SC0[i % 4]][:].rearrange("p (h m) -> p h m", h=HH)
                link(dve.tensor_reduce(hmx[:, i % 2, :], sc, AX_X, ALU.max))
                if i >= 4:
                    dve.wait_ge(sem("pr_tr"), i - 3)
                dve.tensor_tensor(pr[:, i % 4, :].rearrange("p (h m) -> p h m", h=HH), sc,
                                  bc(hmx[:, i % 2, :], 2, S), ALU.subtract).then_inc(sem("sc_shift"), 1)

            def norm0(i):
                dve.wait_ge(sem("sc_exp"), i + 1)
                v = pr[:, i % 4, :].rearrange("p (h m) -> p h m", h=HH)
                link(dve.tensor_reduce(hsum[:, i % 2, :], v, AX_X, ALU.add))
                if i >= 2:
                    dve.wait_ge(sem("sc_norm"), i - 1)
                dve.reciprocal(hinv[:, i % 2, :], hsum[:, i % 2, :]).then_inc(sem("sc_inv"), 1)

            queries0(0)
            memory_norm()
            shift0(0)
            for i in range(1, 2 * NQ):
                shift0(i)
                norm0(i - 1)
                if i == 1:
                    dve.wait_ge(sem("kT_ready0"), 2)
                    masked(0, kT, 1, HH)
                    queries0(1)
            norm0(2 * NQ - 1)

            def add_out(l, bias, n):
                if bias is not None:
                    for q in range(NQ):
                        ins = dve.tensor_tensor(x[:, q, :], x[:, q, :], bias, ALU.add)
                    link(ins)
                for q in range(NQ):
                    dve.wait_ge(sem(f"o_mm{l}"), 2 * (q // 2) + 2)
                    ins = dve.tensor_tensor(x[:, q, :], bank[OB[l] + q // 2][:, (q % 2) * D:(q % 2 + 1) * D],
                                            x[:, q, :], ALU.add)
                link(ins)
            add_out(0, V("bo"), 0)

            def route(l, k, n, kt_, meanwhile=None):
                layer_norm(k, n, None, meanwhile)
                lnT_half(kt_)
                dve.wait_ge(sem("lg_mm"), l + 1)
                dve.tensor_copy(lgT[:], bank[7][:, 384:384 + P]).then_inc(sem("lgT_ready"), 1)
                dve.wait_ge(sem("lg_tr"), l + 1)
                lg_ps = bank[5][:, 0:P].rearrange("p (q e) -> p q e", q=NQ)[:, :, 0:E]
                if l == 0:
                    link(dve.tensor_tensor(lg[:], lg_ps, bc(V("gb0"), 1, NQ), ALU.add))
                else:
                    link(dve.tensor_copy(lg[:], lg_ps))
                for q in range(NQ):
                    ins = dve.max(top[:, q, :], lg[:, q, :])
                link(ins)
                for q in range(NQ):
                    ins = dve.max_index(topi[:, q, :], top[:, q, :], lg[:, q, :])
                link(ins)
                dve.tensor_tensor(gd[:], top[:, :, 1], top[:, :, 0], ALU.subtract).then_inc(sem("gd_ready"), 1)
                link(dve.tensor_copy(topf[:], topi[:, :, 0:2]))
                iota = bc(bc(C("iota")[:, 0:E], 1, 2), 1, NQ)
                link(dve.tensor_tensor(oh[:], iota, bc(topf[:], 3, E), ALU.is_equal))
                dve.tensor_tensor(sel[:, 0:NQ], oh[:, :, 0, :], oh[:, :, 1, :], ALU.add).then_inc(sem("sel"), 1)
                dve.wait_ge(sem("ge_ready"), l + 1)
                link(dve.tensor_scalar(gden[:], ge[:], 1.0, None, ALU.add))
                link(dve.reciprocal(gw[:, :, 0], gden[:]))
                link(dve.tensor_tensor(gw[:, :, 1], ge[:], gw[:, :, 0], ALU.mult))
                dve.wait_ge(sem("pos_mm"), l + 1)
                cnt = bank[7][:, NQ * E:(NQ + 1) * E]
                link(dve.tensor_scalar(ntf[:, 0, :], cnt, float(P), 1.0, ALU.is_gt, ALU.add))
                for t in (2, 3):
                    link(dve.scalar_tensor_tensor(out=ntf[:, 0, :], in0=cnt, scalar=float(t * P), in1=ntf[:, 0, :],
                                                  op0=ALU.is_gt, op1=ALU.add))
                link(dve.tensor_tensor_scan(ntf[:, 2, :], C("ones")[:, 0:E], ntf[:, 0, :], 0.0, ALU.mult, ALU.add))
                link(dve.tensor_tensor(ntf[:, 1, :], ntf[:, 2, :], ntf[:, 0, :], ALU.subtract))
                pos = bank[7][:, 0:NQ * E].rearrange("p (q e) -> p q e", q=NQ)
                link(dve.scalar_tensor_tensor(out=rowf[:], in0=bc(ntf[:, 1, :], 1, NQ), scalar=float(P), in1=pos,
                                              op0=ALU.mult, op1=ALU.add))
                link(dve.tensor_tensor(ohr[:], oh[:], bc(rowf[:], 2, 2), ALU.mult))
                link(dve.tensor_reduce(ridf[:], ohr[:], AX_X, ALU.add))
                dve.tensor_scalar(rid[:], ridf[:].rearrange("p q k -> p (q k)"), float(P), None, ALU.add)\
                   .then_inc(sem("rid"), 1)
                dve.tensor_copy(meta[:], ntf[:]).then_inc(sem(f"meta{l}"), 1)
                for q in range(NQ):
                    ins = dve.tensor_scalar(pick[:, q, :], C("iota"), ridf[:, q, 0:1], None, ALU.is_equal)
                link(ins)
                for q in range(NQ):
                    ins = dve.scalar_tensor_tensor(out=pick[:, q, :], in0=C("iota"), scalar=ridf[:, q, 1:2],
                                                   in1=pick[:, q, :], op0=ALU.is_equal, op1=ALU.add)
                ins.then_inc(sem("pick"), 1)
                dve.tensor_scalar(loff[:], ntf[:, 2, E - 1:E], -float(P), float(P), ALU.mult, ALU.add)
                link(dve.tensor_tensor(lwt[:], oh[:, :, :, E - 1], gw[:], ALU.mult))
                dve.tensor_scalar(lrow[:], rowf[:, :, E - 1], loff[:], None, ALU.add)
                link(dve.tensor_tensor(lsum[:], lwt[:, :, 0], lwt[:, :, 1], ALU.add))
                for q in range(NQ):
                    ins = dve.tensor_scalar(lastw[:, q, :], C("iota"), lrow[:, q:q + 1], lsum[:, q:q + 1],
                                            ALU.is_equal, ALU.mult)
                ins.then_inc(sem("lastw"), 1)
            def memory_masked():
                dve.wait_ge(sem("mp_tr"), 1)
                pmask = C("pmask", 2, P)
                for q in range(NQ):
                    h = q // 2
                    ins = dve.tensor_tensor(ptm[:, q, :], bank[0][:, h * P:(h + 1) * P], pmask[:, q % 2, :], ALU.mult)
                ins.then_inc(sem("ptm_ready"), 1)

            route(0, 2, 2, 2, memory_masked)

            dve.wait_ge(sem("mss_mm"), 1)
            dve.tensor_scalar(veps[:], bank[7][:, 256:256 + NQ], RMS_EPS, None, ALU.add).then_inc(sem("var_ready"), 1)

            def rows_copy(l, n):
                dve.wait_ge(sem(f"row_used{l}"), n + 1)
                dve.tensor_copy(xT[:].rearrange("p k t -> p (k t)"), bank[0][:, 0:KT * P])\
                   .then_inc(sem(f"xT_done{l}"), 1)

            def ffn_loop(l, tile_body, b_of):
                dve.wait_ge(sem(f"meta{l}"), 1)
                rows_copy(l, 0)

                def tile(s, half, n, ahead):
                    tile_body(s, n)
                    ahead()
                    rows_copy(l, n + 1)
                    dve.wait_ge(sem(f"y_mm{l}"), HEAD + n + 1)
                    dve.wait_ge(sem(f"y_stored{l}"), n * 16 + 16)
                    dve.tensor_tensor(yrow[:], bank[7][:, 0:D], b_of(s), ALU.add).then_inc(sem(f"y_evac{l}"), 1)
                all_tiles(dve, tile)

            def tile0(s, n):
                dve.wait_ge(sem("g_mm"), HEAD + n * 2)
                for m in range(4):
                    dve.wait_ge(sem("x12_mm"), n * 4 + (m + 1))
                    dve.tensor_scalar(hT[:, m, :], bank[1 + m % 2][:, 0:P], E0(s, "b1")[:, m:m + 1], None, ALU.add)\
                       .then_inc(sem("x1_done"), 1)
                    dve.wait_ge(sem("x1_done"), n * 4 + (m + 1))
                    dve.scalar_tensor_tensor(out=zT[:, m, :], in0=bank[3 + m % 2][:, 0:P],
                                             scalar=E0(s, "b2")[:, m:m + 1], in1=hT[:, m, :], op0=ALU.add,
                                             op1=ALU.mult).then_inc(sem("z_done"), 1)

            ffn_loop(0, tile0, lambda s: E0(s, "b3"))

            def combine(l, q):
                dve.wait_ge(sem(f"gathered{q}"), 32 * (l + 1))
                for c in range(2):
                    link(dve.scalar_tensor_tensor(out=x[:, q, :], in0=yk[:, q, c, :], scalar=gw[:, q, c:c + 1],
                                                  in1=x[:, q, :], op0=ALU.mult, op1=ALU.add))
                dve.wait_ge(sem("last_mm"), NQ * l + 2 * (q // 2) + 2)
                ins = dve.tensor_tensor(x[:, q, :], x[:, q, :], bank[1 + q // 2][:, (q % 2) * D:(q % 2 + 1) * D],
                                        ALU.add)
                if l == 1:
                    ins.then_inc(sem("x_done"), 1)
                else:
                    link(ins)
            layer_norm(4, 3, lambda q: combine(0, q))
            dve.wait_ge(sem("ln_ready"), 16)
            dve.wait_ge(sem("memn_ready"), 2)
            for q in range(NQ):
                dve.tensor_tensor(ln[:, q, :], ln[:, q, :], memn[:, q, :], ALU.add).then_inc(sem("h2_ready"), 1)
            dve.wait_ge(sem("hss_mm"), 1)
            dve.tensor_scalar(veps[:], bank[7][:, 192:192 + NQ], RMS_EPS, None, ALU.add).then_inc(sem("var_ready"), 1)
            dve.wait_ge(sem("rstd_ready"), 6)
            for q in range(NQ):
                ins = dve.scalar_tensor_tensor(out=tmp[:, q, :], in0=ln[:, q, :], scalar=rinv[:, q:q + 1],
                                               in1=V("hnw"), op0=ALU.mult, op1=ALU.mult)
            link(ins)
            for q in range(NQ):
                dve.tensor_tensor(x[:, q, :], x[:, q, :], tmp[:, q, :], ALU.add).then_inc(sem("x_ready"), 1)
            dve.wait_ge(sem("x_ready"), 4)
            layer_norm(6, 4)
            lnT_half(3)
            def queries1(k):
                dve.wait_ge(sem("q_mm1"), k + 1)
                dve.tensor_copy(qT[:, k, :], bank[2 + k][:]).then_inc(sem("qT_ready1"), 1)
                dve.wait_ge(sem("qT_ready1"), k + 1)

            queries1(0)
            masked(1, qT, 0, MH)

            def decay(i):
                k = i // NQ
                dve.wait_ge(sem("sc_mm1"), i + 1)
                if i >= 3:
                    dve.wait_ge(sem("pv_tile1"), i - 2)
                dve.tensor_tensor(pr1[:, i % 3, :], bank[SC[i % 3]][:], C("decay", KT, HH * S)[:, k, :], ALU.mult)\
                   .then_inc(sem("sc_decay"), 1)

            def group_sums(k):
                dve.wait_ge(sem("pv_tile1"), NQ * (k + 1))
                for b2 in range(2):
                    dst = oT[:, k, :].rearrange("p (q b s) -> p q b s", q=NQ, b=2)[:, :, b2, :]
                    ins = dve.tensor_copy(dst, bank[RB[k][b2]][:, 0:NQ * S].rearrange("p (q s) -> p q s", q=NQ))
                link(ins)
                dve.tensor_reduce(gstat[:, k, :], o3(k), AX_X, ALU.add).then_inc(sem("gsum_ready"), 1)

            def group_squares(k):
                dve.wait_ge(sem("gm_mm"), 2 * k + 1)
                mean = bank[2][:, 2 * k * 16:2 * k * 16 + B]
                link(dve.tensor_tensor(o3(k), o3(k), bc(mean, 2, S), ALU.subtract))
                sq = tmp.rearrange("p q d -> p (q d)")[:, 0:TOK].rearrange("p (b s) -> p b s", s=S)
                link(dve.tensor_tensor(sq, o3(k), o3(k), ALU.mult))
                dve.tensor_reduce(gstat[:, k, :], sq, AX_X, ALU.add).then_inc(sem("gsum_ready"), 1)

            def group_scale(k):
                dve.wait_ge(sem("gm_mm"), 2 * k + 2)
                dve.tensor_scalar(gvar[:, k, :], bank[2][:, (2 * k + 1) * 16:(2 * k + 1) * 16 + B], GN_EPS, None,
                                  ALU.add).then_inc(sem("var_ready"), 1)
                dve.wait_ge(sem("rstd_ready"), 8 + k)
                link(dve.tensor_scalar(gsc[:, k, :], grs[:, k, :], V("gnw")[:, k:k + 1], None, ALU.mult))
                link(dve.tensor_tensor(o3(k), o3(k), bc(gsc[:, k, :], 2, S), ALU.mult))
                dve.tensor_scalar(oT[:, k, :], oT[:, k, :], V("gnb")[:, k:k + 1], None, ALU.add)\
                   .then_inc(sem("oT_ready1"), 1)

            def o3(k):
                return oT[:, k, :].rearrange("p (b s) -> p b s", b=B)

            for i in range(2 * NQ):
                decay(i)
                if i == 1:
                    queries1(1)
                    masked(1, qT, 1, HH)
                if i == NQ + 1:
                    group_sums(0)
                if i == NQ + 2:
                    group_squares(0)
                if i == NQ + 3:
                    group_scale(0)
            group_sums(1)
            group_squares(1)
            group_scale(1)
            add_out(1, None, 1)
            route(1, 9, 5, 4)
            ffn_loop(1, lambda s, n: None, lambda s: E1(s, "b2"))
            for q in range(NQ):
                combine(1, q)


def _view(t, at, dims):
    a, n = at
    v = t[:, a:a + n]
    if not dims:
        return v
    if len(dims) == 2:
        return v.rearrange("p (a b) -> p a b", a=dims[0])
    return v.rearrange("p (a b c) -> p a b c", a=dims[0], b=dims[1])


def _evac_prT(act, sem, prT, bank, i):
    act.wait_ge(sem("pr_tr"), i + 1)
    if i >= 2:
        act.wait_ge(sem("pv_tile0"), i - 1)
    act.activation(prT[:, i % 2, :], bank[0][:], ACT.Copy).then_inc(sem("prT_ready"), 1)


def kernel(**inputs):
    import concourse.bacc as _bacc
    from concourse.bass_utils import run_bass_kernel_spmd as _run

    arrays = layout({k: np.asarray(v) for k, v in inputs.items()})
    nc = _bacc.Bacc("TRN2", target_bir_lowering=False, num_devices=1)
    args = [nc.dram_tensor(n, a.shape, mybir.dt.from_np(a.dtype), kind="ExternalInput").ap()
            for n, a in arrays.items()]
    out = nc.dram_tensor("out_dram", (TOK, D), F32, kind="ExternalOutput").ap()
    perceiver(nc, *args, out)
    r = _run(nc, [arrays], core_ids=[0])
    return r.results[0]["out_dram"].reshape(B, S, D)


def layout(i):
    def rows(w):
        k = w.shape[0] // P
        return w.reshape(k, P, -1).transpose(1, 0, 2).reshape(P, -1)

    def col(v):
        return v.reshape(-1, P).T

    def wide(v):
        return np.broadcast_to(v.reshape(1, -1), (P, v.size))

    def pack(parts, cols):
        a = np.concatenate([parts[n] for n in cols], axis=-1)
        return np.ascontiguousarray(a)

    ar = np.arange(P)
    l, m = np.arange(S)[None, :], np.arange(S)[:, None]
    gam = np.array([1.0 - 2.0 ** (-5 - (8 * h) // H) for h in range(H)], np.float32)
    power = np.where(l >= m, gam[:, None, None] ** np.maximum(l - m, 0).astype(np.float32), 0).astype(np.float32)
    power = power * np.float32(HD ** -0.5)
    decay = np.tile(power.transpose(1, 0, 2).reshape(S, -1), (2, 1))
    f = np.float32
    consts = dict(
        tri=(ar[:, None] < ar[None, :]).astype(f), ones=np.ones((P, P), f),
        gmean=(ar[:, None] // HD == ar[None, :] // HD).astype(f) / f(HD * S),
        bmean=(ar[:, None] // S == ar[None, :] // S).astype(f) / f(S * D),
        pmask=np.concatenate([(ar[:, None] // NWIN == 2 * c + ar[None, :] // S).astype(f) for c in range(2)], 1),
        hmask=(ar[:, None] // HD == np.arange(HH)[None, :]).astype(f), decay=decay.astype(f),
        iota=np.tile(np.arange(P, dtype=f), (P, 1)))
    w = dict(Ws=rows(i["L0_xattn_Ws"]), W=rows(i["L0_xattn_W"]), wvec=col(i["L0_xattn_w"]), bvec=col(i["L0_xattn_b"]),
             ident=np.eye(P, dtype=f))
    gate = lambda a: np.pad(a, ((0, 0), (0, 32 - E)))
    heads = lambda a: rows(a.transpose(1, 0, 2).reshape(D, D))
    v = dict(
        qkv=rows(i["L0_attn_W_qkv"].T), wo=rows(i["L0_attn_W_out"].T), bqkv=col(i["L0_attn_b_qkv"]),
        wcw=wide(i["L0_xattn_Wcw"]), wcb=wide(i["L0_xattn_Wcb"]), bcw=wide(i["L0_xattn_bcw"]),
        bcb=wide(i["L0_xattn_bcb"]), bo=wide(i["L0_attn_b_out"]),
        gw0=rows(gate(i["L0_ffn_gate_w"])), gb0=wide(i["L0_ffn_gate_b"]), gw1=rows(gate(i["L1_ffn_w_gate"])),
        qawk=rows(i["L1_xattn_qa_wk"].T), qawv=rows(i["L1_xattn_qa_wv"].T), qaq=rows(np.tile(i["L1_xattn_qa_q"].T, (1, 2))),
        mnw=np.tile(i["L1_xattn_mn_w"], (2, 1)), hnw=np.tile(i["L1_xattn_hn_w"], (2, 1)),
        gnw=col(i["L1_attn_gn_weight"]), gnb=col(i["L1_attn_gn_bias"]))

    r = dict(rq=heads(i["L1_attn_Wq"]), rk=heads(i["L1_attn_Wk"]), rv=heads(i["L1_attn_Wv"]),
             ro=rows(i["L1_attn_Wout"]))

    def erows(a):
        return np.stack([rows(a[e]) for e in range(E)])

    def ecol(a):
        return np.stack([col(a[e]) for e in range(E)])

    def ewide(a):
        return np.stack([wide(a[e]) for e in range(E)])

    e0 = dict(w1=erows(i["L0_ffn_w1"]), w2=erows(i["L0_ffn_w2"]), wg=erows(i["L0_ffn_wg"]), w3=erows(i["L0_ffn_w3"]),
              b1=ecol(i["L0_ffn_b1"]), b2=ecol(i["L0_ffn_b2"]), bg=ecol(i["L0_ffn_bg"]), b3=ewide(i["L0_ffn_b3"]))
    e1 = dict(w1=erows(i["L1_ffn_w1"]), w2=erows(i["L1_ffn_w2"]), b1=ecol(i["L1_ffn_b1"]), b2=ewide(i["L1_ffn_b2"]))
    c = i["ctx_1024"]
    ws = i["L1_xattn_ws_w"].T.reshape(NQ, 8, P, D).transpose(0, 2, 1, 3)
    mask = np.repeat(i["mask_BxS2_ik0"], S, axis=0).reshape(NQ, P, T).transpose(1, 0, 2)
    return dict(
        x_in=np.ascontiguousarray(i["x"].reshape(TOK, D)),
        ctx_rows=np.ascontiguousarray(c.reshape(B, 2, P, D).transpose(2, 0, 1, 3)),
        ctx_cols=np.ascontiguousarray(c.transpose(2, 0, 1).reshape(KT, P, B, T).transpose(1, 0, 2, 3)),
        mask_in=np.ascontiguousarray(mask), w_in=pack(w, W_COLS), c_in=pack(consts, C_COLS), v_in=pack(v, V_COLS), r_in=pack(r, R_COLS),
        ws_in=np.ascontiguousarray(ws), e0_in=pack(e0, E0_COLS), e1_in=pack(e1, E1_COLS))
```
